# Optimizing a Trainium2 kernel written in Bass

```python
import numpy as np
import jax
import jax.numpy as jnp

def _softmax(x, axis=-1):
    return jax.nn.softmax(x, axis=axis)

def _gelu(x):
    return jax.nn.gelu(x, approximate=True)

def _silu(x):
    return jax.nn.silu(x)

def _sigmoid(x):
    return jax.nn.sigmoid(x)

def _layernorm(x, axis=-1, eps=1e-05):
    m = jnp.mean(x, axis=axis, keepdims=True)
    v = jnp.var(x, axis=axis, keepdims=True)
    return (x - m) / jnp.sqrt(v + eps)

def _scatter_add(tgt, idx, src, axis=0):
    return tgt.at[idx].add(src)

def _segment_sum(src, seg, n):
    return jax.ops.segment_sum(src, seg, n)
kernel_name = 'mk_decoder_postln_d1_seqx_r4_4ac1e3'

def setup_inputs(seed: int=0):
    np.random.seed(seed)
    _w = jnp.asarray

    def _rec_inputs():
        import jax
        import jax.numpy as jnp
        _rk = jax.random.key(seed)
        x = 7.22e-05 + 1 * jax.random.normal(jax.random.fold_in(_rk, 1), (32, 112, 256), jnp.float32)
        _lenS = 112 - jax.random.randint(jax.random.fold_in(_rk, 7), (32,), 0, max(1, 112 // 4) + 1, jnp.int32)
        _lenS2 = 375 - jax.random.randint(jax.random.fold_in(_rk, 8), (32,), 0, max(1, 375 // 4) + 1, jnp.int32)
        _ctx_1024P = jax.random.normal(jax.random.fold_in(_rk, 11), (32, 16, 256), jnp.float32)
        _ctx_1024c = jax.random.dirichlet(jax.random.fold_in(_rk, 511), 0.3 * jnp.ones((16,), jnp.float32), (32, 375))
        _ctx_1024t = jnp.einsum('bsk,bkd->bsd', _ctx_1024c, _ctx_1024P)
        _ctx_1024t = _ctx_1024t * jax.lax.rsqrt(jnp.mean(jnp.square(_ctx_1024t)) + 1e-12) * 0.953939
        ctx_1024 = 4.13588e-05 + 0.999923 * (_ctx_1024t + 0.3 * jax.random.normal(jax.random.fold_in(_rk, 611), (32, 375, 256), jnp.float32))
        return (x, ctx_1024)
    x, ctx_1024 = _rec_inputs()

    def _L0_attn_setup():
        import jax, jax.numpy as jnp
        import numpy as np
        from jax import lax
        B, T, D, H = (2, 1024, 256, 16)
        DK = DV = D // H
        KS = 4
        ALPHA_MIN, BETA_MAX, EPS = (0.1, 1.0, 1e-06)

        def _causal_dwconv(x, w, b):
            C, K = w.shape
            xp = jnp.pad(x, ((0, 0), (K - 1, 0), (0, 0))).transpose(0, 2, 1)
            out = lax.conv_general_dilated(xp, w[:, None, :], (1,), 'VALID', feature_group_count=C, dimension_numbers=('NCH', 'OIH', 'NCH'))
            out = out + b[None, :, None]
            return jax.nn.silu(out).transpose(0, 2, 1)

        def _l2n(t):
            return t / jnp.maximum(jnp.linalg.norm(t, axis=-1, keepdims=True), 1e-06)
        key = jax.random.key(seed)
        ks = jax.random.split(key, 20)

        def w(i, shape, sc=0.02):
            return jax.random.normal(ks[i], shape, jnp.float32) * sc
        return {'x': jax.random.normal(ks[0], (B, T, D), jnp.float32), 'Wq': w(1, (D, H * DK)), 'Wk': w(2, (D, H * DK)), 'Wv': w(3, (D, H * DV)), 'Wo': w(4, (H * DV, D)), 'Wa': w(5, (D, H)), 'ba': jnp.full((H,), 2.0, jnp.float32), 'Wb': w(6, (D, H)), 'bb': jnp.zeros((H,), jnp.float32), 'Wgd': w(7, (D, H * DV // 2)), 'Wgu': w(8, (H * DV // 2, H * DV)), 'rms_w': jnp.ones((H, DV), jnp.float32), 'qcw': w(9, (H * DK, KS), 0.1), 'qcb': jnp.zeros((H * DK,), jnp.float32), 'kcw': w(10, (H * DK, KS), 0.1), 'kcb': jnp.zeros((H * DK,), jnp.float32), 'vcw': w(11, (H * DV, KS), 0.1), 'vcb': jnp.zeros((H * DV,), jnp.float32)}
    _L0_attn_all = _L0_attn_setup()
    _L0_attn_in = {k: v for k, v in _L0_attn_all.items() if k in ('Wq', 'Wk', 'Wv', 'Wo', 'Wa', 'ba', 'Wb', 'bb', 'Wgd', 'Wgu', 'rms_w', 'qcw', 'qcb', 'kcw', 'kcb', 'vcw', 'vcb')}
    del _L0_attn_all

    def _L0_xattn_setup():
        import jax, jax.numpy as jnp
        import numpy as np
        D_MODEL = 256
        N_HEAD = 16
        D_K = 64
        D_V = 64
        B, S = (4, 512)
        key = jax.random.key(seed)
        ks = jax.random.split(key, 7)
        scale = 1.0 / np.sqrt(D_MODEL)
        return {'q': jax.random.normal(ks[0], (B, S, D_MODEL), jnp.float32), 'k': jax.random.normal(ks[1], (B, S, D_MODEL), jnp.float32), 'v': jax.random.normal(ks[2], (B, S, D_MODEL), jnp.float32), 'Wq': jax.random.normal(ks[3], (D_MODEL, N_HEAD * D_K), jnp.float32) * scale, 'Wk': jax.random.normal(ks[4], (D_MODEL, N_HEAD * D_K), jnp.float32) * scale, 'Wv': jax.random.normal(ks[5], (D_MODEL, N_HEAD * D_V), jnp.float32) * scale, 'Wo': jax.random.normal(ks[6], (N_HEAD * D_V, D_MODEL), jnp.float32) * scale}
    _L0_xattn_all = _L0_xattn_setup()
    _L0_xattn_in = {k: v for k, v in _L0_xattn_all.items() if k in ('Wq', 'Wk', 'Wv', 'Wo')}
    del _L0_xattn_all

    def _L0_ffn_setup():
        import jax, jax.numpy as jnp
        import numpy as np
        N_HEADS = 16
        N_KV_HEADS = 4
        N_EMBD = 256
        HEAD_DIM = N_EMBD // N_HEADS
        N_EXPERTS = 8
        TOP_K = 2
        EPS = 1e-06

        def _rmsnorm(x, w):
            xf = x.astype(jnp.float32)
            n = xf * jax.lax.rsqrt(jnp.mean(xf * xf, axis=-1, keepdims=True) + EPS)
            return n.astype(x.dtype) * w

        def _gqa(x, wq, wk, wv, wo):
            B, S, C = x.shape
            n_rep = N_HEADS // N_KV_HEADS
            q = (x @ wq.T).reshape(B, S, N_HEADS, HEAD_DIM)
            k = (x @ wk.T).reshape(B, S, N_KV_HEADS, HEAD_DIM)
            v = (x @ wv.T).reshape(B, S, N_KV_HEADS, HEAD_DIM)
            k = jnp.repeat(k, n_rep, axis=2)
            v = jnp.repeat(v, n_rep, axis=2)
            scale = 1.0 / np.sqrt(HEAD_DIM).astype(np.float32)
            attn = jnp.einsum('bqhd,bkhd->bhqk', q, k) * scale
            causal = jnp.tril(jnp.ones((S, S), dtype=bool))
            attn = jnp.where(causal, attn, jnp.float32(-jnp.inf))
            attn = jax.nn.softmax(attn, axis=-1)
            out = jnp.einsum('bhqk,bkhd->bqhd', attn, v).reshape(B, S, C)
            return out @ wo.T

        def _moe(x, gate_w, expert_w):
            B, S, C = x.shape
            t = x.reshape(B * S, C)
            logits = t @ gate_w.T
            w, sel = jax.lax.top_k(logits, TOP_K)
            w = jax.nn.softmax(w.astype(jnp.float32), axis=1).astype(t.dtype)
            comb = jnp.sum(w[..., None] * jax.nn.one_hot(sel, N_EXPERTS, dtype=t.dtype), axis=1)
            out = jnp.zeros_like(t)
            for e in range(N_EXPERTS):
                out = out + comb[:, e, None] * (t @ expert_w[e].T)
            return out.reshape(B, S, C)
        key = jax.random.key(seed)
        ks = jax.random.split(key, 10)
        B, S, C = (4, 512, N_EMBD)
        s = 0.02
        return {'x': jax.random.normal(ks[0], (B, S, C), dtype=jnp.float32), 'attn_norm_w': jnp.ones((C,), dtype=jnp.float32), 'ffn_norm_w': jnp.ones((C,), dtype=jnp.float32), 'wq': jax.random.normal(ks[1], (C, C), dtype=jnp.float32) * s, 'wk': jax.random.normal(ks[2], (N_KV_HEADS * HEAD_DIM, C), dtype=jnp.float32) * s, 'wv': jax.random.normal(ks[3], (N_KV_HEADS * HEAD_DIM, C), dtype=jnp.float32) * s, 'wo': jax.random.normal(ks[4], (C, C), dtype=jnp.float32) * s, 'gate_w': jax.random.normal(ks[5], (N_EXPERTS, C), dtype=jnp.float32) * s, 'expert_w': jax.random.normal(ks[6], (N_EXPERTS, C, C), dtype=jnp.float32) * s}
    _L0_ffn_all = _L0_ffn_setup()
    _L0_ffn_in = {k: v for k, v in _L0_ffn_all.items() if k in ('attn_norm_w', 'ffn_norm_w', 'wq', 'wk', 'wv', 'wo', 'gate_w', 'expert_w')}
    del _L0_ffn_all
    return {'x': x, 'ctx_1024': ctx_1024, 'L0_attn_Wq': _L0_attn_in['Wq'], 'L0_attn_Wk': _L0_attn_in['Wk'], 'L0_attn_Wv': _L0_attn_in['Wv'], 'L0_attn_Wo': _L0_attn_in['Wo'], 'L0_attn_Wa': _L0_attn_in['Wa'], 'L0_attn_ba': _L0_attn_in['ba'], 'L0_attn_Wb': _L0_attn_in['Wb'], 'L0_attn_bb': _L0_attn_in['bb'], 'L0_attn_Wgd': _L0_attn_in['Wgd'], 'L0_attn_Wgu': _L0_attn_in['Wgu'], 'L0_attn_rms_w': _L0_attn_in['rms_w'], 'L0_attn_qcw': _L0_attn_in['qcw'], 'L0_attn_qcb': _L0_attn_in['qcb'], 'L0_attn_kcw': _L0_attn_in['kcw'], 'L0_attn_kcb': _L0_attn_in['kcb'], 'L0_attn_vcw': _L0_attn_in['vcw'], 'L0_attn_vcb': _L0_attn_in['vcb'], 'L0_xattn_Wq': _L0_xattn_in['Wq'], 'L0_xattn_Wk': _L0_xattn_in['Wk'], 'L0_xattn_Wv': _L0_xattn_in['Wv'], 'L0_xattn_Wo': _L0_xattn_in['Wo'], 'L0_ffn_attn_norm_w': _L0_ffn_in['attn_norm_w'], 'L0_ffn_ffn_norm_w': _L0_ffn_in['ffn_norm_w'], 'L0_ffn_wq': _L0_ffn_in['wq'], 'L0_ffn_wk': _L0_ffn_in['wk'], 'L0_ffn_wv': _L0_ffn_in['wv'], 'L0_ffn_wo': _L0_ffn_in['wo'], 'L0_ffn_gate_w': _L0_ffn_in['gate_w'], 'L0_ffn_expert_w': _L0_ffn_in['expert_w']}

def reference(x, ctx_1024, L0_attn_Wq, L0_attn_Wk, L0_attn_Wv, L0_attn_Wo, L0_attn_Wa, L0_attn_ba, L0_attn_Wb, L0_attn_bb, L0_attn_Wgd, L0_attn_Wgu, L0_attn_rms_w, L0_attn_qcw, L0_attn_qcb, L0_attn_kcw, L0_attn_kcb, L0_attn_vcw, L0_attn_vcb, L0_xattn_Wq, L0_xattn_Wk, L0_xattn_Wv, L0_xattn_Wo, L0_ffn_attn_norm_w, L0_ffn_ffn_norm_w, L0_ffn_wq, L0_ffn_wk, L0_ffn_wv, L0_ffn_wo, L0_ffn_gate_w, L0_ffn_expert_w):
    import jax
    import jax.numpy as jnp

    def _L0_attn_ref(x, Wq, Wk, Wv, Wo, Wa, ba, Wb, bb, Wgd, Wgu, rms_w, qcw, qcb, kcw, kcb, vcw, vcb):
        import jax, jax.numpy as jnp
        import numpy as np
        from jax import lax
        B, T, D, H = (2, 1024, 256, 16)
        DK = DV = D // H
        KS = 4
        ALPHA_MIN, BETA_MAX, EPS = (0.1, 1.0, 1e-06)

        def _causal_dwconv(x, w, b):
            C, K = w.shape
            xp = jnp.pad(x, ((0, 0), (K - 1, 0), (0, 0))).transpose(0, 2, 1)
            out = lax.conv_general_dilated(xp, w[:, None, :], (1,), 'VALID', feature_group_count=C, dimension_numbers=('NCH', 'OIH', 'NCH'))
            out = out + b[None, :, None]
            return jax.nn.silu(out).transpose(0, 2, 1)

        def _l2n(t):
            return t / jnp.maximum(jnp.linalg.norm(t, axis=-1, keepdims=True), 1e-06)
        Bx, Tx, _ = x.shape
        BH = Bx * H
        q = _causal_dwconv(x @ Wq, qcw, qcb)
        k = _causal_dwconv(x @ Wk, kcw, kcb)
        v = _causal_dwconv(x @ Wv, vcw, vcb)

        def heads(t, d):
            return t.reshape(Bx, Tx, H, d).transpose(0, 2, 1, 3).reshape(BH, Tx, d)
        Q = _l2n(heads(q, DK))
        Kh = _l2n(heads(k, DK))
        V = heads(v, DV)
        alpha = jnp.clip(jax.nn.sigmoid(x @ Wa + ba), ALPHA_MIN, 1.0)
        beta = jnp.minimum(jax.nn.sigmoid(x @ Wb + bb), BETA_MAX)
        alpha = alpha.transpose(0, 2, 1).reshape(BH, Tx)
        beta = beta.transpose(0, 2, 1).reshape(BH, Tx)

        def step(S, inp):
            qt, kt, vt, at, bt = inp
            v_hat = jnp.einsum('bij,bi->bj', S, kt)
            err = vt - v_hat
            S = at[:, None, None] * S + bt[:, None, None] * (kt[:, :, None] * err[:, None, :])
            o = jnp.einsum('bij,bi->bj', S, qt)
            return (S, o)
        S0 = jnp.zeros((BH, DK, DV), x.dtype)
        _, O = lax.scan(step, S0, (Q.swapaxes(0, 1), Kh.swapaxes(0, 1), V.swapaxes(0, 1), alpha.T, beta.T))
        O = O.transpose(1, 0, 2).reshape(Bx, H, Tx, DV)
        O = O * lax.rsqrt(jnp.mean(O * O, -1, keepdims=True) + EPS) * rms_w[None, :, None, :]
        g = jax.nn.sigmoid(jax.nn.silu(x @ Wgd) @ Wgu).reshape(Bx, Tx, H, DV).transpose(0, 2, 1, 3)
        O = (O * g).transpose(0, 2, 1, 3).reshape(Bx, Tx, H * DV)
        return O @ Wo

    def _L0_xattn_ref(q, k, v, Wq, Wk, Wv, Wo):
        import jax, jax.numpy as jnp
        import numpy as np
        D_MODEL = 256
        N_HEAD = 16
        D_K = 64
        D_V = 64
        B, S = (4, 512)
        B_, Sq, _ = q.shape
        Sk = k.shape[1]
        qh = (q @ Wq).reshape(B_, Sq, N_HEAD, D_K).transpose(0, 2, 1, 3)
        kh = (k @ Wk).reshape(B_, Sk, N_HEAD, D_K).transpose(0, 2, 1, 3)
        vh = (v @ Wv).reshape(B_, Sk, N_HEAD, D_V).transpose(0, 2, 1, 3)
        scores = jnp.einsum('bhqd,bhkd->bhqk', qh, kh) / jnp.sqrt(jnp.float32(D_K))
        attn = jax.nn.softmax(scores, axis=-1)
        ctx = jnp.einsum('bhqk,bhkd->bhqd', attn, vh)
        ctx = ctx.transpose(0, 2, 1, 3).reshape(B_, Sq, N_HEAD * D_V)
        return ctx @ Wo

    def _L0_ffn_ref(x, attn_norm_w, ffn_norm_w, wq, wk, wv, wo, gate_w, expert_w):
        import jax, jax.numpy as jnp
        import numpy as np
        N_HEADS = 16
        N_KV_HEADS = 4
        N_EMBD = 256
        HEAD_DIM = N_EMBD // N_HEADS
        N_EXPERTS = 8
        TOP_K = 2
        EPS = 1e-06

        def _rmsnorm(x, w):
            xf = x.astype(jnp.float32)
            n = xf * jax.lax.rsqrt(jnp.mean(xf * xf, axis=-1, keepdims=True) + EPS)
            return n.astype(x.dtype) * w

        def _gqa(x, wq, wk, wv, wo):
            B, S, C = x.shape
            n_rep = N_HEADS // N_KV_HEADS
            q = (x @ wq.T).reshape(B, S, N_HEADS, HEAD_DIM)
            k = (x @ wk.T).reshape(B, S, N_KV_HEADS, HEAD_DIM)
            v = (x @ wv.T).reshape(B, S, N_KV_HEADS, HEAD_DIM)
            k = jnp.repeat(k, n_rep, axis=2)
            v = jnp.repeat(v, n_rep, axis=2)
            scale = 1.0 / np.sqrt(HEAD_DIM).astype(np.float32)
            attn = jnp.einsum('bqhd,bkhd->bhqk', q, k) * scale
            causal = jnp.tril(jnp.ones((S, S), dtype=bool))
            attn = jnp.where(causal, attn, jnp.float32(-jnp.inf))
            attn = jax.nn.softmax(attn, axis=-1)
            out = jnp.einsum('bhqk,bkhd->bqhd', attn, v).reshape(B, S, C)
            return out @ wo.T

        def _moe(x, gate_w, expert_w):
            B, S, C = x.shape
            t = x.reshape(B * S, C)
            logits = t @ gate_w.T
            w, sel = jax.lax.top_k(logits, TOP_K)
            w = jax.nn.softmax(w.astype(jnp.float32), axis=1).astype(t.dtype)
            comb = jnp.sum(w[..., None] * jax.nn.one_hot(sel, N_EXPERTS, dtype=t.dtype), axis=1)
            out = jnp.zeros_like(t)
            for e in range(N_EXPERTS):
                out = out + comb[:, e, None] * (t @ expert_w[e].T)
            return out.reshape(B, S, C)
        h = x + _gqa(_rmsnorm(x, attn_norm_w), wq, wk, wv, wo)
        out = h + _moe(_rmsnorm(h, ffn_norm_w), gate_w, expert_w)
        return out
    x = _layernorm(x + _L0_attn_ref(x, L0_attn_Wq, L0_attn_Wk, L0_attn_Wv, L0_attn_Wo, L0_attn_Wa, L0_attn_ba, L0_attn_Wb, L0_attn_bb, L0_attn_Wgd, L0_attn_Wgu, L0_attn_rms_w, L0_attn_qcw, L0_attn_qcb, L0_attn_kcw, L0_attn_kcb, L0_attn_vcw, L0_attn_vcb), axis=-1)
    x = _layernorm(x + _L0_xattn_ref(x, ctx_1024, ctx_1024, L0_xattn_Wq, L0_xattn_Wk, L0_xattn_Wv, L0_xattn_Wo), axis=-1)
    x = _layernorm(x + _L0_ffn_ref(x, L0_ffn_attn_norm_w, L0_ffn_ffn_norm_w, L0_ffn_wq, L0_ffn_wk, L0_ffn_wv, L0_ffn_wo, L0_ffn_gate_w, L0_ffn_expert_w), axis=-1)
    return x

_drawn_inputs = setup_inputs


def setup_inputs(seed=0):
    import zlib

    import numpy as np

    out = dict(_drawn_inputs(seed))
    spreads = {'L0_attn_ba': (2.0, 0.6),
     'L0_attn_bb': (0.0, 0.8),
     'L0_attn_rms_w': (1.0, 0.2),
     'L0_attn_qcb': (0.0, 0.1),
     'L0_attn_kcb': (0.0, 0.1),
     'L0_attn_vcb': (0.0, 0.1),
     'L0_ffn_attn_norm_w': (1.0, 0.6),
     'L0_ffn_ffn_norm_w': (1.0, 0.2)}
    factors = {'L0_attn_Wa': 7.805,
     'L0_attn_Wb': 3.906,
     'L0_attn_Wgd': 8.0,
     'L0_attn_Wgu': 8.0,
     'L0_ffn_wq': 8.0,
     'L0_ffn_wk': 8.0}
    for name, (base, spread) in spreads.items():
        noise = np.random.default_rng([zlib.crc32(name.encode()), seed]).standard_normal(out[name].shape)
        drawn = base * np.exp(spread * noise) if base else spread * noise
        out[name] = jnp.asarray(drawn.astype(out[name].dtype))
    for name, factor in factors.items():
        out[name] = (out[name] * factor).astype(out[name].dtype)
    return out
```

```python
import concourse.bass as bass
from concourse import mybir
from contextlib import ExitStack


def decoder_layer(nc, x, xT, ctxT, dn_Wq, dn_Wk, dn_Wv, dn_Wo, dn_Wa, dn_ba, dn_Wb, dn_bb, dn_Wgd, dn_Wgu, dn_rms_w,
                  dn_qcw, dn_qcb, dn_kcw, dn_kcb, dn_vcw, dn_vcb, xa_Wq, xa_Wk, xa_Wv, xa_Wo,
                  ff_attn_norm_w, ff_ffn_norm_w, ff_wqT, ff_wkT, ff_wvT, ff_woT, ff_gateT, ff_expertT, out):
    ds = bass.ds
    fp32 = mybir.dt.float32
    ALU = mybir.AluOpType
    ACT = mybir.ActivationFunctionType
    X = mybir.AxisListType.X

    B, T, D = x.shape
    P = 128
    KC = D // P
    LN_EPS, RMS_EPS, NORM_FLOOR = 1e-5, 1e-6, 1e-6

    H, DK = 16, 16
    G = P // H
    NG = B // G
    GT = G * T
    HG = GT // 2
    CH = H * DK
    KS = 4
    PAD = KS - 1
    CT = 3 * CH // P
    AB, GD = 2 * CT, 2 * CT + 2
    GU = GD + 2
    PU = GU + 2 * KC

    S = ctxT.shape[2]
    XH, XD = 16, 64
    XC = XH * XD
    NP = XH // 2
    SC = 3
    SK = S // SC
    VH = XC // 512
    FQ, FK, FV = 1, 3, 3 + NP
    FU = FV + SC * VH

    FH, FD, KV = 16, 16, 4
    REP = FH // KV
    E = ff_gateT.shape[1]
    EU = E * D // 512
    MASKED = -1e30

    ctx = ExitStack()
    with ctx:
        def sb(name, shape, dt=fp32):
            return ctx.enter_context(nc.sbuf_tensor(name, shape, dt))

        def sem(name):
            return ctx.enter_context(nc.semaphore(name))

        def dram(name, shape):
            return nc.dram_tensor(name, shape, fp32, kind="Internal").ap()

        qkv_dram = dram("qkv_dram", (3, B, CH, T))
        ab_dram = dram("ab_dram", (2, B, H, T))
        o_dram = dram("o_dram", (B, CH, T))
        x1_dram = dram("x1_dram", (B, T, D))

        ident = sb("ident", [P, P])
        causal = sb("causal", [T, T])
        before = sb("before", [T, E, E])
        minus_half, ln_eps, rms_eps = sb("minus_half", [P, 1]), sb("ln_eps", [P, 1]), sb("rms_eps", [P, 1])
        w_qkv = sb("w_qkv", [P, KC, 3 * CH])
        w_ab = sb("w_ab", [P, KC, 2 * H])
        w_gd = sb("w_gd", [P, KC, CH // 2])
        w_gu = sb("w_gu", [P, 1, CH])
        w_dno = sb("w_dno", [P, KC, D])
        taps = sb("taps", [P, CT, KS])
        conv_bias = sb("conv_bias", [P, CT])
        ab_bias = sb("ab_bias", [2 * H, 1])
        ab_low = sb("ab_low", [2 * H, 1])
        rms_w = sb("rms_w", [P, DK])
        w_xq = sb("w_xq", [P, KC, XC])
        w_xk = sb("w_xk", [P, KC, XC])
        w_xv = sb("w_xv", [P, KC, XC])
        w_xo = sb("w_xo", [P, XC // P, D])
        attn_w = sb("attn_w", [P, KC])
        ffn_w = sb("ffn_w", [P, KC])
        w_fq = sb("w_fq", [P, KC, REP, P])
        w_fk = sb("w_fk", [P, KC, P])
        w_fv = sb("w_fv", [P, KC, KV * FD])
        w_fo = sb("w_fo", [P, KC, D])
        w_gate = sb("w_gate", [P, KC, E])
        w_exp = sb("w_exp", [P, KC, E * D])

        xT_in = sb("xT_in", [P, KC, GT])
        arena = sb("arena", [P, NP * S + SC * XC])
        raw = arena[:, 2 * DK * T:2 * DK * T + 2 * G * (T + PAD)].rearrange("p (a b t) -> p a b t", a=2, b=G)
        work = sb("work", [P, 4, GT])
        conv = work[:, 0:2]
        tanh_half = work[:, 2:4]
        act2 = sb("act2", [P, 2, GT])
        cx = sb("cx", [T, XC])
        ab = cx[0:2 * H, 0:GT]
        gate_mid = work[:, 3:4]
        gate_t = sb("gate_t", [P, KC, GT])
        oT = xT_in
        kq = sb("kq", [P, 2, DK, T])
        kn = sb("kn", [P, DK, T])
        val = sb("val", [P, DK, T])
        alpha = sb("alpha", [P, T])
        beta = sb("beta", [P, T])
        sq = arena[:, 0:2 * DK * T].rearrange("p (a d t) -> p a d t", a=2, d=DK)
        x_in = arena[0:T, 0:G * D].rearrange("p (b d) -> p b d", b=G)
        norm = sb("norm", [P, 2, T])
        rnorm = sb("rnorm", [P, 2, T])
        kdotq = sb("kdotq", [P, T])
        state = sb("state", [P, DK, DK])
        prod = sb("prod", [P, 2, DK, DK])
        outer = sb("outer", [P, DK, DK])
        read = work[:].rearrange("p a n -> p (a n)").rearrange("p (t s j) -> p t s j", s=2, j=DK)
        upd = act2[:].rearrange("p a n -> p (a n)").rearrange("p (t j) -> p t j", j=DK)
        sum1 = sb("sum1", [T, 2, D])
        stats1 = sb("stats1", [T, 2, 6])
        mv1 = sb("mv1", [T, 2, 2])
        rstd1 = sb("rstd1", [T, 2])
        x1 = sb("x1", [T, 2, D])

        xa_in = sb("xa_in", [T, D])
        xa_res = sb("xa_res", [T, D])
        xaT = sb("xaT", [P, KC, T])
        cT = sb("cT", [P, KC, S])
        qT = sb("qT", [P, NP, T])
        kT = arena[:, 0:NP * S].rearrange("p (m s) -> p m s", m=NP)
        v_sb = arena[0:SK, NP * S:].rearrange("p (c n) -> p c n", c=SC)
        negmax = sb("negmax", [T, XH])
        rowsum = sb("rowsum", [T, XH])
        rrow = sb("rrow", [T, XH])
        probs_flat = sb("probs_flat", [P, 4 * S])
        probs = probs_flat[0:T].rearrange("p (a s) -> p a s", a=4)
        probsT = sb("probsT", [SK, 2, 2, SC, T])
        cxT = probs_flat[:, 0:XC // P * T].rearrange("p (m t) -> p m t", t=T)
        sum2 = sb("sum2", [T, D])
        stats2 = sb("stats2", [T, 6])
        mv2 = sb("mv2", [T, 2])
        rstd2 = sb("rstd2", [T, 1])
        x2 = sb("x2", [T, D])
        junk = sb("junk", [T, D])
        ms2 = sb("ms2", [T, 1])
        rms2 = sb("rms2", [T, 1])
        xn = sb("xn", [T, D])
        xnT = sb("xnT", [P, KC, T])
        fq = sb("fq", [P, REP, T])
        fk = sb("fk", [P, T])
        fv = sb("fv", [T, KV * FD])
        fs = probs_flat[0:T, 0:2 * REP * T].rearrange("p (a m t) -> p a m t", a=2, m=REP)
        fmax = sb("fmax", [T, KV, REP])
        fsum = sb("fsum", [T, KV, REP])
        frow = sb("frow", [T, KV * REP])
        fp = cx[:, 0:2 * REP * T].rearrange("p (a m t) -> p a m t", a=2, m=REP)
        fpT = probsT[0:T].rearrange("p a b c t -> p (a b c t)")[:, 0:2 * REP * T].rearrange("p (a m t) -> p a m t", a=2, m=REP)
        fo = sb("fo", [T, D])
        foT = sb("foT", [P, KC, T])
        h_sb = sb("h_sb", [T, D])
        ms3 = sb("ms3", [T, 1])
        rms3 = sb("rms3", [T, 1])
        hn = sb("hn", [T, D])
        hnT = sb("hnT", [P, KC, T])
        logit = sb("logit", [T, E])
        neglmax = sb("neglmax", [T, 1])
        above = sb("above", [T, E, E])
        tied = sb("tied", [T, E, E])
        rank = sb("rank", [T, E])
        elog = sb("elog", [T, E])
        comb = sb("comb", [T, E])
        csum = sb("csum", [T, 1])
        rcsum = sb("rcsum", [T, 1])
        acc = sb("acc", [T, D])
        stats3 = sb("stats3", [T, 6])
        mv3 = sb("mv3", [T, 2])
        rstd3 = sb("rstd3", [T, 1])
        y_out = sb("y_out", [T, D])

        bank = [ctx.enter_context(nc.psum_tensor(f"bank{n}", [P, 512], fp32)) for n in range(4, 8)]
        score4 = ctx.enter_context(nc.psum_tensor("score4", [P, 4, 512], fp32))
        PT0, PT1, OV, MX = bank

        dn_w_in, conv_w_in, xa_w_in, ff_w_in = sem("dn_w_in"), sem("conv_w_in"), sem("xa_w_in"), sem("ff_w_in")
        dve_const, pool_const, scaled_w = sem("dve_const"), sem("pool_const"), sem("scaled_w")
        pads_zero = sem("pads_zero")
        xT_loaded, x_loaded = sem("xT_loaded"), sem("x_loaded")
        proj_ready, proj_taken = sem("proj_ready"), sem("proj_taken")
        tap_done, conv_ready, tanh_ready, act_ready = sem("tap_done"), sem("conv_ready"), sem("tanh_ready"), sem("act_ready")
        gate_raw = sem("gate_raw")
        act_stored, ab_half, ab_ready, ab_stored, gate_mid_ready = (
            [sem("act_stored0"), sem("act_stored1")], sem("ab_half"), sem("ab_ready"), sem("ab_stored"), sem("gate_mid_ready"))
        pair_in, squares, norm_ready, norm_floor, rnorm_ready = (
            sem("pair_in"), sem("squares"), sem("norm_ready"), sem("norm_floor"), sem("rnorm_ready"))
        pair_step = sem("pair_step")
        rec_step, state_ready = sem("rec_step"), sem("state_ready")
        o_raw, o_squares, o_norm, o_floor, o_rnorm, o_scaled, o_ready, o_stored, oT_loaded, o_gated = (
            sem("o_raw"), sem("o_squares"), sem("o_norm"), sem("o_floor"), sem("o_rnorm"), sem("o_scaled"), sem("o_ready"),
            sem("o_stored"), sem("oT_loaded"), sem("o_gated"))
        o_part = sem("o_part")
        dn_out, sum1_ready, stats1_ready, mv1_ready, var1_ready, rstd1_ready, x1_ready, x1_stored = (
            sem("dn_out"), sem("sum1_ready"), sem("stats1_ready"), sem("mv1_ready"), sem("var1_ready"), sem("rstd1_ready"),
            sem("x1_ready"), [sem("x1_stored0"), sem("x1_stored1")])

        xa_loaded, res_loaded, cT_loaded = sem("xa_loaded"), sem("res_loaded"), sem("cT_loaded")
        fill_ready, fill_taken, fill_taken_v = sem("fill_ready"), sem("fill_taken"), sem("fill_taken_v")
        scores_ready, max_ready, exp_ready = sem("scores_ready"), sem("max_ready"), sem("exp_ready")
        pT_ready, pT_copied_v, pT_copied_s, pv_ready = sem("pT_ready"), sem("pT_copied_v"), sem("pT_copied_s"), sem("pv_ready")
        rrow_ready, cx_ready, cxT_ready, cxT_copied_s, cxT_copied_v = (
            sem("rrow_ready"), sem("cx_ready"), sem("cxT_ready"), sem("cxT_copied_s"), sem("cxT_copied_v"))
        xo_ready, sum2_ready, stats2_ready, mv2_ready, var2_ready, rstd2_ready, x2_ready = (
            sem("xo_ready"), sem("sum2_ready"), sem("stats2_ready"), sem("mv2_ready"), sem("var2_ready"), sem("rstd2_ready"),
            sem("x2_ready"))
        ms2_ready, msv2_ready, rms2_ready, xn_ready, xnT_ready, xnT_copied = (
            sem("ms2_ready"), sem("msv2_ready"), sem("rms2_ready"), sem("xn_ready"), sem("xnT_ready"), sem("xnT_copied"))
        fq_ready, fkv_ready, fq_copied, fkv_copied = sem("fq_ready"), sem("fkv_ready"), sem("fq_copied"), sem("fkv_copied")
        fs_ready, fs_masked, fmax_ready, fexp_ready, fpT_ready, fpT_copied = (
            sem("fs_ready"), sem("fs_masked"), sem("fmax_ready"), sem("fexp_ready"), sem("fpT_ready"), sem("fpT_copied"))
        fpv_ready, frow_ready, fo_ready, foT_ready, foT_copied, fwo_ready, h_ready = (
            sem("fpv_ready"), sem("frow_ready"), sem("fo_ready"), sem("foT_ready"), sem("foT_copied"), sem("fwo_ready"),
            sem("h_ready"))
        ms3_ready, msv3_ready, rms3_ready, hn_ready, hnT_ready, hnT_copied = (
            sem("ms3_ready"), sem("msv3_ready"), sem("rms3_ready"), sem("hn_ready"), sem("hnT_ready"), sem("hnT_copied"))
        gate_ready, logit_ready, logit_max, ranks, elog_ready, comb_step, comb_ready, acc_start = (
            sem("gate_ready"), sem("logit_ready"), sem("logit_max"), sem("ranks"), sem("elog_ready"), sem("comb_step"),
            sem("comb_ready"), sem("acc_start"))
        expert_ready, expert_step, stats3_ready, mv3_ready, var3_ready, rstd3_ready, y_ready, y_stored = (
            sem("expert_ready"), sem("expert_step"), sem("stats3_ready"), sem("mv3_ready"), sem("var3_ready"),
            sem("rstd3_ready"), sem("y_ready"), sem("y_stored"))

        DN_W = 16 * 8
        CONV_W = 16 * (6 + 2 + G)
        XA_W = 16 * 4
        FF_W = 16 * (2 + 2 * KC * KV + 3 + 1)

        def chunks(w):
            return w.rearrange("(c p) n -> p c n", p=P)

        def column(w):
            return w.rearrange("(m p o) -> p m o", p=P, o=1)

        def over_channels(row):
            return row.rearrange("p (o t) -> p o t", o=1).broadcast_to([P, DK, T])

        block = ctx.enter_context(nc.Block())

        @block.sync
        def _(sp):
            def pre_loads(g):
                if not isinstance(g, int) or g > 0:
                    sp.wait_ge(sum1_ready, g * G)
                sp.dma_start(xT_in[:], chunks(xT)[:, :, ds(g * GT, GT)]).then_inc(xT_loaded, 16)

            def to_pairs(g):
                for m in range(CT):
                    sp.wait_ge(act_ready, g * CT + m + 1)
                    sp.dma_start(qkv_dram[m // KC, ds(g * G, G), P * (m % KC):P * (m % KC + 1)].rearrange("b p t -> p b t"),
                                 act2[:, m % 2].rearrange("p (b t) -> p b t", b=G)).then_inc(act_stored[m % 2], 16)
                sp.wait_ge(ab_ready, g + 1)
                for n in range(2):
                    sp.dma_start(ab_dram[n, ds(g * G, G)].rearrange("b h t -> h b t"),
                                 ab[H * n:H * (n + 1)].rearrange("p (b t) -> p b t", b=G)).then_inc(ab_stored, 16)
                for n in range(2):
                    sp.wait_ge(act_stored[n], (g + 1) * 16 * (CT // 2))
                for n, dst in enumerate((kq[:, 1], kn[:], val[:])):
                    sp.dma_start(dst.rearrange("p d t -> p (d t)"),
                                 qkv_dram[n, ds(g * G, G)].rearrange("b (h d) t -> (b h) (d t)", d=DK)).then_inc(pair_in, 16)
                sp.wait_ge(ab_stored, g * 32 + 32)
                for n, dst in enumerate((alpha, beta)):
                    sp.dma_start(dst[:], ab_dram[n, ds(g * G, G)].rearrange("b h t -> (b h) t")).then_inc(pair_in, 16)

            def to_channels(g):
                sp.wait_ge(o_norm, g + 1)
                sp.dma_start(x_in, x[ds(g * G, G)].rearrange("b t d -> t b d")).then_inc(x_loaded, 16)
                sp.wait_ge(o_ready, g + 1)
                sp.dma_start(o_dram[ds(g * G, G)].rearrange("b (h d) t -> (b h) (d t)", d=DK),
                             val[:].rearrange("p d t -> p (d t)")).then_inc(o_stored, 16)
                sp.wait_ge(o_stored, g * 16 + 16)
                for m in range(KC):
                    sp.dma_start(oT[:, m].rearrange("p (b t) -> p b t", b=G),
                                 o_dram[ds(g * G, G), P * m:P * (m + 1)].rearrange("b p t -> p b t")).then_inc(oT_loaded, 16)
                for b in range(G):
                    sp.wait_ge(x1_ready, g * G + b + 1)
                    sp.dma_start(x1_dram[ds(g * G + b, 1)].rearrange("o t d -> t (o d)"), x1[:, b % 2]).then_inc(x1_stored[b % 2], 16)

            def next_loads(i):
                if not isinstance(i, int):
                    sp.wait_ge(fill_ready, i * FU)
                sp.dma_start(xa_in[:], x1_dram[ds(i, 1)].rearrange("o t d -> t (o d)")).then_inc(xa_loaded, 16)
                sp.dma_start(cT[:], ctxT[ds(i, 1)].rearrange("o (c p) s -> p (o c) s", p=P)).then_inc(cT_loaded, 16)

            def residual_load(i):
                if not isinstance(i, int) or i > 0:
                    sp.wait_ge(sum2_ready, i)
                sp.dma_start(xa_res[:], x1_dram[ds(i, 1)].rearrange("o t d -> t (o d)")).then_inc(res_loaded, 16)

            def store(i):
                sp.wait_ge(y_ready, i + 1)
                sp.dma_start(out[ds(i, 1)].rearrange("o t d -> t (o d)"), y_out[:]).then_inc(y_stored, 16)

            for n, w in enumerate((dn_Wq, dn_Wk, dn_Wv)):
                sp.dma_start(w_qkv[:, :, CH * n:CH * (n + 1)], chunks(w)).then_inc(dn_w_in, 16)
            pre_loads(0)
            sp.dma_start(w_ab[:, :, 0:H], chunks(dn_Wa)).then_inc(dn_w_in, 16)
            sp.dma_start(w_ab[:, :, H:2 * H], chunks(dn_Wb)).then_inc(dn_w_in, 16)
            sp.dma_start(w_gd[:], chunks(dn_Wgd)).then_inc(dn_w_in, 16)
            sp.dma_start(w_gu[:], dn_Wgu.rearrange("(o p) n -> p o n", o=1)).then_inc(dn_w_in, 16)
            sp.dma_start(w_dno[:], chunks(dn_Wo)).then_inc(dn_w_in, 16)
            to_pairs(0)
            to_channels(0)
            if NG > 1:
                with sp.Fori(1, NG) as g:
                    pre_loads(g)
                    to_pairs(g)
                    to_channels(g)
            for n in range(2):
                sp.wait_ge(x1_stored[n], 16 * (B // 2))
            next_loads(0)
            residual_load(0)
            with sp.Fori(0, B - 1) as i:
                next_loads(i + 1)
                residual_load(i + 1)
                store(i)
            store(B - 1)
            sp.wait_ge(y_stored, 16 * B)

        @block.gpsimd
        def _(pool):
            nc.gpsimd.memset(ident[:], 0.0).then_inc(pool_const, 1)
            nc.gpsimd.memset(causal[:], 0.0).then_inc(pool_const, 1)
            nc.gpsimd.memset(before[:], 1.0).then_inc(pool_const, 1)
            nc.gpsimd.memset(minus_half[:], -0.5).then_inc(pool_const, 1)
            nc.gpsimd.memset(ln_eps[:], LN_EPS).then_inc(pool_const, 1)
            nc.gpsimd.memset(rms_eps[:], RMS_EPS).then_inc(pool_const, 1)
            pool.wait_ge(pool_const, 6)
            nc.gpsimd.affine_select(out=ident[:], in_=ident[:], compare_op=ALU.not_equal, fill=1.0, base=0,
                                    pattern=[[-1, P]], channel_multiplier=1).then_inc(pool_const, 1)
            nc.gpsimd.affine_select(out=causal[:], in_=causal[:], compare_op=ALU.is_ge, fill=MASKED, base=0,
                                    pattern=[[-1, T]], channel_multiplier=1).then_inc(pool_const, 1)
            nc.gpsimd.affine_select(out=before[:], in_=before[:], compare_op=ALU.is_gt, fill=0.0, base=0,
                                    pattern=[[1, E], [-1, E]], channel_multiplier=0).then_inc(pool_const, 1)
            pool.wait_ge(pool_const, 9)
            flat_norm, flat_rnorm = norm[:].rearrange("p s t -> p (s t)"), rnorm[:].rearrange("p s t -> p (s t)")

            def pair_norms(g):
                pool.wait_ge(norm_floor, g + 1)
                nc.gpsimd.tensor_tensor(flat_rnorm, flat_norm, minus_half[:].broadcast_to([P, 2 * T]), ALU.pow).then_inc(rnorm_ready, 1)

            def output_norms(g):
                pool.wait_ge(o_norm, g + 1)
                nc.gpsimd.tensor_tensor(norm[:, 0], norm[:, 0], rms_eps[:].broadcast_to([P, T]), ALU.add).then_inc(o_floor, 1)
                pool.wait_ge(o_floor, g + 1)
                nc.gpsimd.tensor_tensor(rnorm[:, 0], norm[:, 0], minus_half[:].broadcast_to([P, T]), ALU.pow).then_inc(o_rnorm, 1)
                for b in range(G):
                    n = g * G + b + 1
                    var = mv1[:, b % 2, 1:2]
                    pool.wait_ge(mv1_ready, n)
                    nc.gpsimd.tensor_tensor(var, var, ln_eps[0:T], ALU.add).then_inc(var1_ready, 1)
                    pool.wait_ge(var1_ready, n)
                    nc.gpsimd.tensor_tensor(rstd1[:, b % 2:b % 2 + 1], var, minus_half[0:T], ALU.pow).then_inc(rstd1_ready, 1)

            def sequence_norms(i):
                pool.wait_ge(mv2_ready, i + 1)
                nc.gpsimd.tensor_tensor(mv2[:, 1:2], mv2[:, 1:2], ln_eps[0:T], ALU.add).then_inc(var2_ready, 1)
                pool.wait_ge(var2_ready, i + 1)
                nc.gpsimd.tensor_tensor(rstd2[:], mv2[:, 1:2], minus_half[0:T], ALU.pow).then_inc(rstd2_ready, 1)
                pool.wait_ge(ms2_ready, i + 1)
                nc.gpsimd.tensor_tensor(ms2[:], ms2[:], rms_eps[0:T], ALU.add).then_inc(msv2_ready, 1)
                pool.wait_ge(msv2_ready, i + 1)
                nc.gpsimd.tensor_tensor(rms2[:], ms2[:], minus_half[0:T], ALU.pow).then_inc(rms2_ready, 1)
                pool.wait_ge(ms3_ready, i + 1)
                nc.gpsimd.tensor_tensor(ms3[:], ms3[:], rms_eps[0:T], ALU.add).then_inc(msv3_ready, 1)
                pool.wait_ge(msv3_ready, i + 1)
                nc.gpsimd.tensor_tensor(rms3[:], ms3[:], minus_half[0:T], ALU.pow).then_inc(rms3_ready, 1)
                pool.wait_ge(h_ready, i + 1)
                nc.gpsimd.tensor_tensor(acc[:], h_sb[:], x2[:], ALU.add).then_inc(acc_start, 1)
                pool.wait_ge(mv3_ready, i + 1)
                nc.gpsimd.tensor_tensor(mv3[:, 1:2], mv3[:, 1:2], ln_eps[0:T], ALU.add).then_inc(var3_ready, 1)
                pool.wait_ge(var3_ready, i + 1)
                nc.gpsimd.tensor_tensor(rstd3[:], mv3[:, 1:2], minus_half[0:T], ALU.pow).then_inc(rstd3_ready, 1)

            with pool.Fori(0, NG) as g:
                pair_norms(g)
                output_norms(g)
            with pool.Fori(0, B) as i:
                sequence_norms(i)

        @block.scalar
        def _(act):
            for n, (cw, cb) in enumerate(((dn_qcw, dn_qcb), (dn_kcw, dn_kcb), (dn_vcw, dn_vcb))):
                act.dma_start(taps[:, KC * n:KC * (n + 1)], cw.rearrange("(m p) k -> p m k", p=P)).then_inc(conv_w_in, 16)
                act.dma_start(conv_bias[:, KC * n:KC * (n + 1)].rearrange("p (m o) -> p m o", o=1), column(cb), allow_slow_non_contiguous=True).then_inc(conv_w_in, 16)
            act.dma_start(ab_bias[0:H], dn_ba.rearrange("(p o) -> p o", o=1)).then_inc(conv_w_in, 16)
            act.dma_start(ab_bias[H:2 * H], dn_bb.rearrange("(p o) -> p o", o=1)).then_inc(conv_w_in, 16)
            for b in range(G):
                act.dma_start(rms_w[H * b:H * (b + 1)], dn_rms_w).then_inc(conv_w_in, 16)
            for dst, w in ((w_xq, xa_Wq), (w_xk, xa_Wk), (w_xv, xa_Wv), (w_xo, xa_Wo)):
                act.dma_start(dst[:], chunks(w)).then_inc(xa_w_in, 16)
            act.dma_start(attn_w[:].rearrange("p (m o) -> p m o", o=1), column(ff_attn_norm_w), allow_slow_non_contiguous=True).then_inc(ff_w_in, 16)
            act.dma_start(ffn_w[:].rearrange("p (m o) -> p m o", o=1), column(ff_ffn_norm_w), allow_slow_non_contiguous=True).then_inc(ff_w_in, 16)
            act.dma_start(w_fv[:], chunks(ff_wvT)).then_inc(ff_w_in, 16)
            act.dma_start(w_fo[:], chunks(ff_woT)).then_inc(ff_w_in, 16)
            act.dma_start(w_gate[:], chunks(ff_gateT)).then_inc(ff_w_in, 16)
            act.dma_start(w_exp[:], chunks(ff_expertT)).then_inc(ff_w_in, 16)
            act.wait_ge(pads_zero, 2)
            for j in range(KV):
                for k in range(KC):
                    act.dma_start(w_fq[:, k, :, 32 * j:32 * j + FD],
                                  ff_wqT[P * k:P * (k + 1), REP * FD * j:REP * FD * (j + 1)].rearrange("p (m d) -> p m d", d=FD)
                                  ).then_inc(ff_w_in, 16)
                    act.dma_start(w_fk[:, k, 32 * j:32 * j + FD], ff_wkT[P * k:P * (k + 1), FD * j:FD * (j + 1)]).then_inc(ff_w_in, 16)
            act.wait_ge(dve_const, 1)

            def projections(g):
                def tanh_of(m):
                    act.wait_ge(conv_ready, g * CT + m + 1)
                    nc.scalar.activation(tanh_half[:, m % 2], conv[:, m % 2], ACT.Tanh, scale=0.5).then_inc(tanh_ready, 1)
                for m in range(CT):
                    for h in range(2):
                        u = 2 * m + h
                        act.wait_ge(proj_ready, g * PU + u + 1)
                        if m >= 2 and h == 0:
                            act.wait_ge(conv_ready, g * CT + m - 1)
                        nc.scalar.activation(raw[:, m % 2, G // 2 * h:G // 2 * (h + 1), PAD:],
                                             bank[u % 2][:, 0:HG].rearrange("p (b t) -> p b t", t=T), ACT.Copy).then_inc(proj_taken, 1)
                    if m >= 1:
                        if m >= 3:
                            act.wait_ge(act_ready, g * CT + m - 2)
                        tanh_of(m - 1)
                act.wait_ge(act_ready, g * CT + CT - 2)
                tanh_of(CT - 1)
                for h in range(2):
                    act.wait_ge(proj_ready, g * PU + AB + h + 1)
                    nc.scalar.activation(ab[:, HG * h:HG * (h + 1)], bank[(AB + h) % 2][0:2 * H, 0:HG], ACT.Tanh, scale=0.5,
                                         bias=ab_bias[:]).then_inc(proj_taken, 1)
                act.wait_ge(act_ready, g * CT + CT)
                for h in range(2):
                    act.wait_ge(proj_ready, g * PU + GD + h + 1)
                    nc.scalar.activation(conv[:, 0, HG * h:HG * (h + 1)], bank[(GD + h) % 2][:, 0:HG], ACT.Copy).then_inc(proj_taken, 1)
                act.wait_ge(proj_taken, g * PU + GU)
                nc.scalar.activation(tanh_half[:, 0], conv[:, 0], ACT.Tanh, scale=0.5).then_inc(gate_raw, 1)
                for m in range(KC):
                    for h in range(2):
                        u = GU + 2 * m + h
                        act.wait_ge(proj_ready, g * PU + u + 1)
                        nc.scalar.activation(gate_t[:, m, HG * h:HG * (h + 1)], bank[u % 2][:, 0:HG], ACT.Tanh,
                                             scale=0.25).then_inc(proj_taken, 1)
                act.wait_ge(pair_in, g * 80 + 80)
                nc.scalar.activation(sq[:, 0], kn[:], ACT.Square)
                nc.scalar.activation(sq[:, 1], kq[:, 1], ACT.Square).then_inc(squares, 1)

            def output_squares(g):
                act.wait_ge(o_raw, g + 1)
                nc.scalar.activation(sq[:, 0], val[:], ACT.Square, scale=DK ** -0.5).then_inc(o_squares, 1)

            def take(i, u):
                src = score4[:, u % 4]
                act.wait_ge(fill_ready, i * FU + u + 1)
                if u < FQ:
                    nc.scalar.activation(xaT[:].rearrange("p c t -> p (c t)"), src[:, 0:KC * T], ACT.Copy).then_inc(fill_taken, 1)
                elif u < FK:
                    n = NP // 2 * (u - FQ)
                    nc.scalar.activation(qT[:, n:n + NP // 2].rearrange("p m t -> p (m t)"), src[:, 0:NP // 2 * T], ACT.Copy,
                                         scale=XD ** -0.5).then_inc(fill_taken, 1)
                elif u < FV:
                    nc.scalar.activation(kT[:, u - FK], src[:, 0:S], ACT.Copy).then_inc(fill_taken, 1)
                else:
                    c, h = divmod(u - FV, VH)
                    nc.scalar.activation(v_sb[:, c, 512 * h:512 * (h + 1)], src[0:SK, :], ACT.Copy).then_inc(fill_taken, 1)

            def attention(i):
                def copy_second(p):
                    act.wait_ge(pT_ready, i * NP + p + 1)
                    if p >= 2:
                        act.wait_ge(pv_ready, i * NP + p - 1)
                    nc.scalar.activation(probsT[:, p % 2, 1].rearrange("p c t -> p (c t)"), PT1[0:SK, 0:SC * T], ACT.Copy
                                         ).then_inc(pT_copied_s, 1)
                for p in range(NP):
                    act.wait_ge(max_ready, i * NP + p + 1)
                    for a in range(2):
                        h = 2 * p + a
                        nc.scalar.activation(probs[:, 2 * (p % 2) + a], score4[0:T, 2 * (p % 2) + a, 0:S], ACT.Exp,
                                             bias=negmax[:, h:h + 1], accum_out=rowsum[:, h:h + 1]).then_inc(exp_ready, 1)
                    if p >= 1:
                        copy_second(p - 1)
                copy_second(NP - 1)

            def chain(i, fill):
                def take_next(*us):
                    if fill:
                        for u in us:
                            take(i + 1, u)
                take_next(0)
                act.wait_ge(cxT_ready, i * 2 + 1)
                nc.scalar.activation(cxT[:, 0:4].rearrange("p m t -> p (m t)"), PT0[:, 0:4 * T], ACT.Copy).then_inc(cxT_copied_s, 1)
                take_next(1, 2, 3, 4, 5)
                act.wait_ge(x2_ready, i + 1)
                nc.scalar.activation(junk[:], x2[:], ACT.Square, scale=D ** -0.5, accum_out=ms2[:]).then_inc(ms2_ready, 1)
                take_next(6)
                act.wait_ge(xnT_ready, i + 1)
                nc.scalar.activation(xnT[:].rearrange("p c t -> p (c t)"), MX[:, 0:KC * T], ACT.Copy).then_inc(xnT_copied, 1)
                take_next(7)
                act.wait_ge(fq_ready, i + 1)
                nc.scalar.activation(fq[:].rearrange("p m t -> p (m t)"), PT0[:, 0:REP * T], ACT.Copy, scale=FD ** -0.5
                                     ).then_inc(fq_copied, 1)
                take_next(8)
                for j in range(KV):
                    act.wait_ge(fmax_ready, i * KV + j + 1)
                    if j >= 2:
                        act.wait_ge(fpT_ready, i * KV + j - 1)
                    for m in range(REP):
                        last = nc.scalar.activation(fp[:, j % 2, m], fs[:, j % 2, m], ACT.Exp, bias=fmax[:, j, m:m + 1],
                                                    accum_out=fsum[:, j, m:m + 1])
                    last.then_inc(fexp_ready, 1)
                    take_next(9 + j)
                take_next(13)
                act.wait_ge(foT_ready, i + 1)
                nc.scalar.activation(foT[:].rearrange("p c t -> p (c t)"), OV[:, 0:KC * T], ACT.Copy).then_inc(foT_copied, 1)
                take_next(14)
                act.wait_ge(h_ready, i + 1)
                nc.scalar.activation(junk[:], h_sb[:], ACT.Square, scale=D ** -0.5, accum_out=ms3[:]).then_inc(ms3_ready, 1)
                take_next(15, 16)
                act.wait_ge(hnT_ready, i + 1)
                nc.scalar.activation(hnT[:].rearrange("p c t -> p (c t)"), MX[:, 0:KC * T], ACT.Copy).then_inc(hnT_copied, 1)
                act.wait_ge(logit_max, i + 1)
                nc.scalar.activation(elog[:], logit[:], ACT.Exp, bias=neglmax[:]).then_inc(elog_ready, 1)

            with act.Fori(0, NG) as g:
                projections(g)
                output_squares(g)
            for u in range(FU):
                take(0, u)
            with act.Fori(0, B - 1) as i:
                attention(i)
                chain(i, True)
            attention(B - 1)
            chain(B - 1, False)

        @block.tensor
        def _(pe):
            def projections(g):
                def unit(u, w, m0, mw, src):
                    if u >= 2:
                        pe.wait_ge(proj_taken, g * PU + u - 1)
                    nk = w.shape[1]
                    cols = slice(HG * (u % 2), HG * (u % 2 + 1))
                    for k in range(nk):
                        last = nc.tensor.matmul(bank[u % 2][0:mw, 0:HG], w[:, k, m0:m0 + mw], src[:, k, cols], start=k == 0, stop=k == nk - 1)
                    last.then_inc(proj_ready, 1)
                pe.wait_ge(xT_loaded, g * 16 + 16)
                if not isinstance(g, int):
                    pe.wait_ge(sum1_ready, g * G)
                for m in range(CT):
                    for h in range(2):
                        unit(2 * m + h, w_qkv, P * m, P, xT_in)
                for h in range(2):
                    unit(AB + h, w_ab, 0, 2 * H, xT_in)
                for h in range(2):
                    unit(GD + h, w_gd, 0, P, xT_in)
                pe.wait_ge(gate_mid_ready, g + 1)
                for m in range(KC):
                    for h in range(2):
                        unit(GU + 2 * m + h, w_gu, P * m, P, gate_mid)

            def output_rows(g):
                pe.wait_ge(o_gated, g + 1)
                for b in range(G):
                    if b >= 2:
                        pe.wait_ge(sum1_ready, g * G + b - 1)
                    for k in range(KC):
                        last = nc.tensor.matmul(bank[b % 2][0:T, 0:D], oT[:, k, T * b:T * (b + 1)], w_dno[:, k], start=k == 0, stop=k == KC - 1)
                    last.then_inc(dn_out, 1)

            def fill(i, u):
                dst = score4[:, u % 4]
                if u >= 4:
                    pe.wait_ge(fill_taken, i * FU + u - 3)
                if u < FQ:
                    pe.wait_ge(xa_loaded, i * 16 + 16)
                    for k in range(KC):
                        last = nc.tensor.transpose(dst[:, T * k:T * (k + 1)], xa_in[:, P * k:P * (k + 1)], ident[0:T, 0:T])
                elif u < FK:
                    pe.wait_ge(fill_taken, i * FU + FQ)
                    for n in range(NP // 2):
                        m = NP // 2 * (u - FQ) + n
                        for k in range(KC):
                            last = nc.tensor.matmul(dst[:, T * n:T * (n + 1)], w_xq[:, k, P * m:P * (m + 1)], xaT[:, k], start=k == 0, stop=k == KC - 1)
                elif u < FV:
                    pe.wait_ge(cT_loaded, i * 16 + 16)
                    for k in range(KC):
                        last = nc.tensor.matmul(dst[:, 0:S], w_xk[:, k, P * (u - FK):P * (u - FK + 1)], cT[:, k], start=k == 0, stop=k == KC - 1)
                else:
                    c, h = divmod(u - FV, VH)
                    for k in range(KC):
                        last = nc.tensor.matmul(dst[0:SK, :], cT[:, k, SK * c:SK * (c + 1)], w_xv[:, k, 512 * h:512 * (h + 1)], start=k == 0, stop=k == KC - 1)
                last.then_inc(fill_ready, 1)

            def attention(i):
                def scores(p):
                    if p >= 2:
                        pe.wait_ge(exp_ready, i * XH + 2 * p - 2)
                    for a in range(2):
                        r = slice(XD * a, XD * (a + 1))
                        last = nc.tensor.matmul(score4[0:T, 2 * (p % 2) + a, 0:S], qT[r, p], kT[r, p], start=True, stop=True)
                    last.then_inc(scores_ready, 1)

                def transposes(p):
                    pe.wait_ge(exp_ready, i * XH + 2 * p + 2)
                    if p >= 1:
                        pe.wait_ge(pT_copied_v, i * NP + p)
                        pe.wait_ge(pT_copied_s, i * NP + p)
                    for a in range(2):
                        for c in range(SC):
                            last = nc.tensor.transpose((PT0, PT1)[a][0:SK, T * c:T * (c + 1)], probs[:, 2 * (p % 2) + a, SK * c:SK * (c + 1)],
                                                       ident[0:T, 0:T])
                    last.then_inc(pT_ready, 1)

                def values(p):
                    pe.wait_ge(pT_copied_v, i * NP + p + 1)
                    pe.wait_ge(pT_copied_s, i * NP + p + 1)
                    dst = OV if p < NP // 2 else MX
                    for a in range(2):
                        h = 2 * p + a
                        col = XD * (h % (XH // 2))
                        for c in range(SC):
                            last = nc.tensor.matmul(dst[0:T, col:col + XD], probsT[:, p % 2, a, c], v_sb[:, c, XD * h:XD * (h + 1)],
                                                    start=c == 0, stop=c == SC - 1)
                    last.then_inc(pv_ready, 1)

                pe.wait_ge(fill_taken, i * FU + FU)
                scores(0)
                scores(1)
                if not isinstance(i, int) or i > 0:
                    pe.wait_ge(expert_step, i * E)
                for p in range(NP):
                    transposes(p)
                    if p >= 1:
                        values(p - 1)
                    if p + 2 < NP:
                        scores(p + 2)
                values(NP - 1)

            def chain(i, with_fill):
                def fill_next(*us):
                    if with_fill:
                        for u in us:
                            fill(i + 1, u)

                def gqa_scores(j):
                    if j >= 2:
                        pe.wait_ge(fs_masked, i * KV + j - 1)
                    r = slice(32 * j, 32 * j + FD)
                    for m in range(REP):
                        last = nc.tensor.matmul((MX, OV)[j % 2][0:T, T * m:T * (m + 1)], fq[r, m], fk[r], start=True, stop=True)
                    last.then_inc(fs_ready, 1)

                def gqa_transposes(j):
                    pe.wait_ge(fexp_ready, i * KV + j + 1)
                    if j >= 2:
                        pe.wait_ge(fpT_copied, i * KV + j - 1)
                    for m in range(REP):
                        last = nc.tensor.transpose((PT0, PT1)[j % 2][0:T, T * m:T * (m + 1)], fp[:, j % 2, m], ident[0:T, 0:T])
                    last.then_inc(fpT_ready, 1)

                def gqa_values(j):
                    pe.wait_ge(fpT_copied, i * KV + j + 1)
                    for m in range(REP):
                        h = REP * j + m
                        last = nc.tensor.matmul(MX[0:T, FD * h:FD * (h + 1)], fpT[:, j % 2, m], fv[:, FD * j:FD * (j + 1)], start=True, stop=True)
                    last.then_inc(fpv_ready, 1)

                fill_next(0)
                for half in range(2):
                    pe.wait_ge(cx_ready, i * 2 + half + 1)
                    for m in range(4):
                        c = 4 * half + m
                        last = nc.tensor.transpose((PT0, PT1)[half][:, T * m:T * (m + 1)], cx[:, P * c:P * (c + 1)], ident[0:T, 0:T])
                    last.then_inc(cxT_ready, 1)
                    fill_next(1 + half)
                pe.wait_ge(cxT_copied_s, i + 1)
                pe.wait_ge(cxT_copied_v, i + 1)
                for m in range(XC // P):
                    last = nc.tensor.matmul(OV[0:T, 0:D], cxT[:, m], w_xo[:, m], start=m == 0, stop=m == XC // P - 1)
                last.then_inc(xo_ready, 1)
                fill_next(3, 4, 5, 6)
                pe.wait_ge(xn_ready, i + 1)
                for k in range(KC):
                    last = nc.tensor.transpose(MX[:, T * k:T * (k + 1)], xn[:, P * k:P * (k + 1)], ident[0:T, 0:T])
                last.then_inc(xnT_ready, 1)
                fill_next(7)
                pe.wait_ge(xnT_copied, i + 1)
                for m in range(REP):
                    for k in range(KC):
                        last = nc.tensor.matmul(PT0[:, T * m:T * (m + 1)], w_fq[:, k, m], xnT[:, k], start=k == 0, stop=k == KC - 1)
                last.then_inc(fq_ready, 1)
                for k in range(KC):
                    nc.tensor.matmul(PT1[:, 0:T], w_fk[:, k], xnT[:, k], start=k == 0, stop=k == KC - 1)
                for k in range(KC):
                    last = nc.tensor.matmul(PT1[0:T, T:T + KV * FD], xnT[:, k], w_fv[:, k], start=k == 0, stop=k == KC - 1)
                last.then_inc(fkv_ready, 1)
                fill_next(8)
                pe.wait_ge(fq_copied, i + 1)
                pe.wait_ge(fkv_copied, i + 1)
                gqa_scores(0)
                gqa_scores(1)
                fill_next(9)
                gqa_scores(2)
                gqa_transposes(0)
                gqa_scores(3)
                fill_next(10)
                gqa_transposes(1)
                fill_next(11)
                pe.wait_ge(fs_masked, i * KV + KV)
                gqa_values(0)
                gqa_transposes(2)
                gqa_values(1)
                fill_next(12)
                gqa_transposes(3)
                gqa_values(2)
                fill_next(13)
                gqa_values(3)
                pe.wait_ge(fo_ready, i + 1)
                for k in range(KC):
                    last = nc.tensor.transpose(OV[:, T * k:T * (k + 1)], fo[:, P * k:P * (k + 1)], ident[0:T, 0:T])
                last.then_inc(foT_ready, 1)
                fill_next(14)
                pe.wait_ge(foT_copied, i + 1)
                for k in range(KC):
                    last = nc.tensor.matmul(PT0[0:T, 0:D], foT[:, k], w_fo[:, k], start=k == 0, stop=k == KC - 1)
                last.then_inc(fwo_ready, 1)
                fill_next(15, 16)
                pe.wait_ge(hn_ready, i + 1)
                for k in range(KC):
                    last = nc.tensor.transpose(MX[:, T * k:T * (k + 1)], hn[:, P * k:P * (k + 1)], ident[0:T, 0:T])
                last.then_inc(hnT_ready, 1)
                pe.wait_ge(hnT_copied, i + 1)
                for k in range(KC):
                    last = nc.tensor.matmul(PT1[0:T, 0:E], hnT[:, k], w_gate[:, k], start=k == 0, stop=k == KC - 1)
                last.then_inc(gate_ready, 1)
                for u in range(EU):
                    if u == EU - 1:
                        pe.wait_ge(logit_ready, i + 1)
                    for k in range(KC):
                        last = nc.tensor.matmul((OV, PT0, MX, PT1)[u][0:T, :], hnT[:, k], w_exp[:, k, 512 * u:512 * (u + 1)], start=k == 0, stop=k == KC - 1)
                    last.then_inc(expert_ready, 1)

            pe.wait_ge(dn_w_in, DN_W)
            pe.wait_ge(pool_const, 9)
            projections(0)
            output_rows(0)
            if NG > 1:
                with pe.Fori(1, NG) as g:
                    projections(g)
                    output_rows(g)
            pe.wait_ge(xa_w_in, XA_W)
            pe.wait_ge(ff_w_in, FF_W)
            pe.wait_ge(scaled_w, 5)
            pe.wait_ge(sum1_ready, B)
            for u in range(FU):
                fill(0, u)
            with pe.Fori(0, B - 1) as i:
                attention(i)
                chain(i, True)
            attention(B - 1)
            chain(B - 1, False)

        @block.vector
        def _(dve):
            nc.vector.memset(w_fq[:], 0.0).then_inc(pads_zero, 1)
            nc.vector.memset(w_fk[:], 0.0).then_inc(pads_zero, 1)
            nc.vector.memset(raw, 0.0)
            nc.vector.memset(state[:], 0.0).then_inc(state_ready, 1)
            nc.vector.memset(ab_low[:], 0.0).then_inc(pads_zero, 1)
            dve.wait_ge(conv_w_in, CONV_W)
            dve.wait_ge(pads_zero, 3)
            nc.vector.memset(ab_low[0:H], 0.1)
            nc.vector.tensor_scalar(rms_w[:], rms_w[:], 0.5, None, ALU.mult)
            nc.vector.tensor_scalar(ab_bias[:], ab_bias[:], 0.5, None, ALU.mult).then_inc(dve_const, 1)

            def scale_weights():
                dve.wait_ge(ff_w_in, FF_W)
                for w, norm_w in ((w_fq, attn_w), (w_fk, attn_w), (w_fv, attn_w), (w_gate, ffn_w), (w_exp, ffn_w)):
                    for k in range(KC):
                        last = nc.vector.tensor_scalar(w[:, k], w[:, k], norm_w[:, k:k + 1], None, ALU.mult)
                    last.then_inc(scaled_w, 1)

            def convolutions(g):
                def twice_silu(m):
                    dve.wait_ge(tanh_ready, g * CT + m + 1)
                    if m >= 2:
                        dve.wait_ge(act_stored[m % 2], g * 16 * (CT // 2) + 16 * (m // 2))
                    nc.vector.scalar_tensor_tensor(act2[:, m % 2], tanh_half[:, m % 2], 1.0, conv[:, m % 2], ALU.add, ALU.mult
                                                   ).then_inc(act_ready, 1)
                for m in range(CT):
                    dve.wait_ge(proj_taken, g * PU + 2 * m + 2)
                    if m >= 2:
                        dve.wait_ge(act_ready, g * CT + m - 1)
                    r = raw[:, m % 2]
                    q = conv[:, m % 2].rearrange("p (b t) -> p b t", t=T)
                    at = (g * CT + m) * PAD
                    nc.vector.tensor_scalar(q, r[:, :, PAD:], taps[:, m, PAD:KS], conv_bias[:, m:m + 1], ALU.mult, ALU.add).then_inc(tap_done, 1)
                    for k in range(PAD - 1, 0, -1):
                        dve.wait_ge(tap_done, at + PAD - k)
                        nc.vector.scalar_tensor_tensor(q, r[:, :, k:k + T], taps[:, m, k:k + 1], q, ALU.mult, ALU.add).then_inc(tap_done, 1)
                    dve.wait_ge(tap_done, at + PAD)
                    nc.vector.scalar_tensor_tensor(q, r[:, :, 0:T], taps[:, m, 0:1], q, ALU.mult, ALU.add).then_inc(conv_ready, 1)
                    if m >= 1:
                        twice_silu(m - 1)
                twice_silu(CT - 1)
                dve.wait_ge(proj_taken, g * PU + AB + 2)
                nc.vector.tensor_scalar(ab[:], ab[:], 0.5, 0.5, ALU.mult, ALU.add).then_inc(ab_half, 1)
                dve.wait_ge(ab_half, g + 1)
                nc.vector.tensor_scalar(ab[:], ab[:], ab_low[:], 1.0, ALU.max, ALU.min).then_inc(ab_ready, 1)
                dve.wait_ge(gate_raw, g + 1)
                nc.vector.scalar_tensor_tensor(gate_mid[:, 0], tanh_half[:, 0], 1.0, conv[:, 0], ALU.add, ALU.mult).then_inc(gate_mid_ready, 1)

            def pairs(g):
                dve.wait_ge(squares, g + 1)
                nc.vector.tensor_reduce(norm[:], sq[:].rearrange("p s d t -> p s t d"), X, ALU.add).then_inc(norm_ready, 1)
                dve.wait_ge(norm_ready, g + 1)
                nc.vector.tensor_scalar(norm[:], norm[:], (2 * NORM_FLOOR) ** 2, None, ALU.max).then_inc(norm_floor, 1)
                dve.wait_ge(pair_in, g * 80 + 80)
                nc.vector.scalar_tensor_tensor(val[:], val[:], 0.5, over_channels(beta[:]), ALU.mult, ALU.mult)
                dve.wait_ge(rnorm_ready, g + 1)
                at = g * 3
                nc.vector.tensor_tensor(kn[:], kn[:], over_channels(rnorm[:, 0]), ALU.mult)
                nc.vector.tensor_tensor(kq[:, 1], kq[:, 1], over_channels(rnorm[:, 1]), ALU.mult).then_inc(pair_step, 1)
                dve.wait_ge(pair_step, at + 1)
                nc.vector.scalar_tensor_tensor(kq[:, 0], kn[:], -1.0, over_channels(beta[:]), ALU.mult, ALU.mult)
                nc.vector.tensor_tensor(sq[:, 1], kn[:], kq[:, 1], ALU.mult).then_inc(pair_step, 1)
                dve.wait_ge(pair_step, at + 2)
                dve.wait_ge(proj_ready, g * PU + PU)
                nc.vector.tensor_reduce(kdotq[:], sq[:, 1].rearrange("p d t -> p t d"), X, ALU.add).then_inc(pair_step, 1)

            def recurrence_step(g, t):
                at = (g * T + t) * 4
                dve.wait_ge(state_ready, g * (T + 1) + t + 1)
                nc.vector.tensor_tensor(prod[:], state[:].rearrange("p (o j) i -> p o j i", o=1).broadcast_to([P, 2, DK, DK]),
                                        kq[:, :, :, ds(t, 1)].rearrange("p s i o -> p s o i").broadcast_to([P, 2, DK, DK]), ALU.mult
                                        ).then_inc(rec_step, 1)
                dve.wait_ge(rec_step, at + 1)
                nc.vector.tensor_reduce(read[:, ds(t, 1)].rearrange("p o s j -> p (o s) j"), prod[:], X, ALU.add).then_inc(rec_step, 1)
                dve.wait_ge(rec_step, at + 2)
                nc.vector.tensor_tensor(upd[:, ds(t, 1)].rearrange("p o j -> p (o j)"), val[:, :, ds(t, 1)].rearrange("p j o -> p (j o)"),
                                        read[:, ds(t, 1), 0].rearrange("p o j -> p (o j)"), ALU.add).then_inc(rec_step, 1)
                dve.wait_ge(rec_step, at + 3)
                nc.vector.tensor_tensor(outer[:], upd[:, ds(t, 1)].rearrange("p o j -> p j o").broadcast_to([P, DK, DK]),
                                        kn[:, :, ds(t, 1)].rearrange("p i o -> p o i").broadcast_to([P, DK, DK]), ALU.mult).then_inc(rec_step, 1)
                dve.wait_ge(rec_step, at + 4)
                flat = state[:].rearrange("p j i -> p (j i)")
                nc.vector.scalar_tensor_tensor(flat, flat, alpha[:, ds(t, 1)], outer[:].rearrange("p j i -> p (j i)"), ALU.mult, ALU.add
                                               ).then_inc(state_ready, 1)

            def outputs(g):
                dve.wait_ge(state_ready, g * (T + 1) + T + 1)
                nc.vector.memset(state[:], 0.0).then_inc(state_ready, 1)
                nc.vector.tensor_tensor(sq[:, 0], read[:, :, 1].rearrange("p t j -> p j t"), over_channels(alpha[:]), ALU.mult)
                nc.vector.tensor_tensor(sq[:, 1], upd[:].rearrange("p t j -> p j t"), over_channels(kdotq[:]), ALU.mult).then_inc(o_part, 1)
                dve.wait_ge(o_part, g + 1)
                nc.vector.tensor_tensor(val[:], sq[:, 0], sq[:, 1], ALU.add).then_inc(o_raw, 1)
                dve.wait_ge(o_squares, g + 1)
                nc.vector.tensor_reduce(norm[:, 0], sq[:, 0].rearrange("p d t -> p t d"), X, ALU.add).then_inc(o_norm, 1)
                dve.wait_ge(o_rnorm, g + 1)
                nc.vector.tensor_tensor(val[:], val[:], over_channels(rnorm[:, 0]), ALU.mult).then_inc(o_scaled, 1)
                dve.wait_ge(o_scaled, g + 1)
                nc.vector.tensor_tensor(val[:], val[:], rms_w[:].rearrange("p (j o) -> p j o", o=1).broadcast_to([P, DK, T]), ALU.mult
                                        ).then_inc(o_ready, 1)
                dve.wait_ge(oT_loaded, g * 32 + 32)
                dve.wait_ge(proj_taken, g * PU + PU)
                nc.vector.scalar_tensor_tensor(oT[:], gate_t[:], 1.0, oT[:], ALU.add, ALU.mult).then_inc(o_gated, 1)
                dve.wait_ge(x_loaded, g * 16 + 16)
                def finish(b):
                    dve.wait_ge(rstd1_ready, g * G + b + 1)
                    if b >= 2:
                        dve.wait_ge(x1_stored[b % 2], 16 * (G // 2) * g + 16 * (b // 2))
                    elif not isinstance(g, int):
                        dve.wait_ge(x1_stored[b % 2], 16 * (G // 2) * g)
                    nc.vector.tensor_scalar(x1[:, b % 2], sum1[:, b % 2], mv1[:, b % 2, 0:1], rstd1[:, b % 2:b % 2 + 1],
                                            ALU.subtract, ALU.mult).then_inc(x1_ready, 1)
                for b in range(G):
                    n = g * G + b + 1
                    dve.wait_ge(dn_out, n)
                    if b >= 2:
                        dve.wait_ge(x1_ready, n - 2)
                    nc.vector.tensor_tensor(sum1[:, b % 2], bank[b % 2][0:T, 0:D], x_in[:, b], ALU.add).then_inc(sum1_ready, 1)
                    dve.wait_ge(sum1_ready, n)
                    nc.vector.bn_stats(stats1[:, b % 2], sum1[:, b % 2]).then_inc(stats1_ready, 1)
                    dve.wait_ge(dve_const, 1)
                    dve.wait_ge(stats1_ready, n)
                    nc.vector.bn_aggr(mv1[:, b % 2], stats1[:, b % 2]).then_inc(mv1_ready, 1)
                    if b >= 1:
                        finish(b - 1)
                finish(G - 1)

            def attention(i):
                def copy_first(p):
                    dve.wait_ge(pT_ready, i * NP + p + 1)
                    if p >= 2:
                        dve.wait_ge(pv_ready, i * NP + p - 1)
                    nc.vector.tensor_copy(probsT[:, p % 2, 0].rearrange("p c t -> p (c t)"), PT0[0:SK, 0:SC * T]).then_inc(pT_copied_v, 1)

                def normalise(half):
                    n = XH // 2
                    dve.wait_ge(exp_ready, i * XH + n * (half + 1))
                    nc.vector.reciprocal(rrow[:, n * half:n * (half + 1)], rowsum[:, n * half:n * (half + 1)]).then_inc(rrow_ready, 1)
                    dve.wait_ge(rrow_ready, i * 2 + half + 1)
                    dve.wait_ge(pv_ready, i * NP + NP // 2 * (half + 1))
                    nc.vector.tensor_tensor(cx[:, 512 * half:512 * (half + 1)].rearrange("p (h d) -> p h d", d=XD),
                                            (OV, MX)[half][0:T, :].rearrange("p (h d) -> p h d", d=XD),
                                            rrow[:, n * half:n * (half + 1)].rearrange("p (h o) -> p h o", o=1).broadcast_to([T, n, XD]),
                                            ALU.mult).then_inc(cx_ready, 1)
                for p in range(NP):
                    dve.wait_ge(scores_ready, i * NP + p + 1)
                    nc.vector.tensor_reduce(negmax[:, 2 * p:2 * p + 2], score4[0:T, 2 * (p % 2):2 * (p % 2) + 2, 0:S], X, ALU.max,
                                            negate=True).then_inc(max_ready, 1)
                    if p >= 1:
                        copy_first(p - 1)
                    if p == NP // 2 + 2:
                        normalise(0)
                copy_first(NP - 1)
                normalise(1)

            def chain(i):
                dve.wait_ge(cxT_ready, i * 2 + 2)
                nc.vector.tensor_copy(cxT[:, 4:8].rearrange("p m t -> p (m t)"), PT1[:, 0:4 * T]).then_inc(cxT_copied_v, 1)
                dve.wait_ge(xo_ready, i + 1)
                dve.wait_ge(res_loaded, i * 16 + 16)
                nc.vector.tensor_tensor(sum2[:], OV[0:T, 0:D], xa_res[:], ALU.add).then_inc(sum2_ready, 1)
                dve.wait_ge(sum2_ready, i + 1)
                nc.vector.bn_stats(stats2[:], sum2[:]).then_inc(stats2_ready, 1)
                dve.wait_ge(dve_const, 1)
                dve.wait_ge(stats2_ready, i + 1)
                nc.vector.bn_aggr(mv2[:], stats2[:]).then_inc(mv2_ready, 1)
                dve.wait_ge(rstd2_ready, i + 1)
                nc.vector.tensor_scalar(x2[:], sum2[:], mv2[:, 0:1], rstd2[:], ALU.subtract, ALU.mult).then_inc(x2_ready, 1)
                dve.wait_ge(rms2_ready, i + 1)
                nc.vector.tensor_scalar(xn[:], x2[:], rms2[:], None, ALU.mult).then_inc(xn_ready, 1)
                dve.wait_ge(fkv_ready, i + 1)
                nc.vector.tensor_copy(fk[:], PT1[:, 0:T])
                nc.vector.tensor_copy(fv[:], PT1[0:T, T:T + KV * FD]).then_inc(fkv_copied, 1)

                def masked_max(j):
                    dve.wait_ge(fs_ready, i * KV + j + 1)
                    if j >= 2:
                        dve.wait_ge(fexp_ready, i * KV + j - 1)
                    nc.vector.tensor_tensor(fs[:, j % 2], (MX, OV)[j % 2][0:T, 0:REP * T].rearrange("p (m t) -> p m t", t=T),
                                            causal[:].rearrange("p (o t) -> p o t", o=1).broadcast_to([T, REP, T]), ALU.add).then_inc(fs_masked, 1)
                    dve.wait_ge(fs_masked, i * KV + j + 1)
                    nc.vector.tensor_reduce(fmax[:, j], fs[:, j % 2], X, ALU.max, negate=True).then_inc(fmax_ready, 1)

                def copy_transposes(j):
                    dve.wait_ge(fpT_ready, i * KV + j + 1)
                    if j >= 2:
                        dve.wait_ge(fpv_ready, i * KV + j - 1)
                    nc.vector.tensor_copy(fpT[:, j % 2].rearrange("p m t -> p (m t)"), (PT0, PT1)[j % 2][0:T, 0:REP * T]).then_inc(fpT_copied, 1)
                masked_max(0)
                masked_max(1)
                masked_max(2)
                copy_transposes(0)
                masked_max(3)
                copy_transposes(1)
                copy_transposes(2)
                copy_transposes(3)
                dve.wait_ge(fexp_ready, i * KV + KV)
                nc.vector.reciprocal(frow[:], fsum[:].rearrange("p j m -> p (j m)")).then_inc(frow_ready, 1)
                dve.wait_ge(frow_ready, i + 1)
                dve.wait_ge(fpv_ready, i * KV + KV)
                nc.vector.tensor_tensor(fo[:].rearrange("p (h d) -> p h d", d=FD), MX[0:T, 0:D].rearrange("p (h d) -> p h d", d=FD),
                                        frow[:].rearrange("p (h o) -> p h o", o=1).broadcast_to([T, FH, FD]), ALU.mult).then_inc(fo_ready, 1)
                dve.wait_ge(fwo_ready, i + 1)
                nc.vector.tensor_tensor(h_sb[:], PT0[0:T, 0:D], x2[:], ALU.add).then_inc(h_ready, 1)
                dve.wait_ge(rms3_ready, i + 1)
                nc.vector.tensor_scalar(hn[:], h_sb[:], rms3[:], None, ALU.mult).then_inc(hn_ready, 1)
                dve.wait_ge(gate_ready, i + 1)
                nc.vector.tensor_copy(logit[:], PT1[0:T, 0:E]).then_inc(logit_ready, 1)
                dve.wait_ge(logit_ready, i + 1)
                nc.vector.tensor_reduce(neglmax[:], logit[:], X, ALU.max, negate=True).then_inc(logit_max, 1)
                other = logit[:].rearrange("p (o f) -> p o f", o=1).broadcast_to([T, E, E])
                own = logit[:].rearrange("p (e o) -> p e o", o=1).broadcast_to([T, E, E])
                at = i * 5
                nc.vector.tensor_tensor(tied[:], other, own, ALU.is_equal).then_inc(ranks, 1)
                nc.vector.tensor_tensor(above[:], other, own, ALU.is_gt)
                dve.wait_ge(ranks, at + 1)
                nc.vector.tensor_tensor(tied[:], tied[:], before[:], ALU.mult).then_inc(ranks, 1)
                dve.wait_ge(ranks, at + 2)
                nc.vector.tensor_tensor(above[:], above[:], tied[:], ALU.add).then_inc(ranks, 1)
                dve.wait_ge(ranks, at + 3)
                nc.vector.tensor_reduce(rank[:], above[:], X, ALU.add).then_inc(ranks, 1)
                dve.wait_ge(ranks, at + 4)
                dve.wait_ge(elog_ready, i + 1)
                nc.vector.scalar_tensor_tensor(comb[:], rank[:], 2.0, elog[:], ALU.is_lt, ALU.mult).then_inc(ranks, 1)
                dve.wait_ge(ranks, at + 5)
                nc.vector.tensor_reduce(csum[:], comb[:], X, ALU.add).then_inc(comb_step, 1)
                dve.wait_ge(comb_step, i * 2 + 1)
                nc.vector.reciprocal(rcsum[:], csum[:]).then_inc(comb_step, 1)
                dve.wait_ge(comb_step, i * 2 + 2)
                nc.vector.tensor_scalar(comb[:], comb[:], rcsum[:], None, ALU.mult).then_inc(comb_ready, 1)
                dve.wait_ge(comb_ready, i + 1)
                dve.wait_ge(acc_start, i + 1)
                for e in range(E):
                    u = e // 2
                    if e % 2 == 0:
                        dve.wait_ge(expert_ready, i * EU + u + 1)
                    if e > 0:
                        dve.wait_ge(expert_step, i * E + e)
                    nc.vector.scalar_tensor_tensor(acc[:], (OV, PT0, MX, PT1)[u][0:T, D * (e % 2):D * (e % 2 + 1)], comb[:, e:e + 1], acc[:],
                                                   ALU.mult, ALU.add).then_inc(expert_step, 1)
                dve.wait_ge(expert_step, i * E + E)
                nc.vector.bn_stats(stats3[:], acc[:]).then_inc(stats3_ready, 1)
                dve.wait_ge(dve_const, 1)
                dve.wait_ge(stats3_ready, i + 1)
                nc.vector.bn_aggr(mv3[:], stats3[:]).then_inc(mv3_ready, 1)
                dve.wait_ge(rstd3_ready, i + 1)
                if not isinstance(i, int) or i > 0:
                    dve.wait_ge(y_stored, i * 16)
                nc.vector.tensor_scalar(y_out[:], acc[:], mv3[:, 0:1], rstd3[:], ALU.subtract, ALU.mult).then_inc(y_ready, 1)

            def first_layer(g):
                convolutions(g)
                pairs(g)
                with dve.Fori(0, T) as t:
                    recurrence_step(g, t)
                outputs(g)

            first_layer(0)
            scale_weights()
            if NG > 1:
                with dve.Fori(1, NG) as g:
                    first_layer(g)
            with dve.Fori(0, B - 1) as i:
                attention(i)
                chain(i)
            attention(B - 1)
            chain(B - 1)


_OUT = "out_0_dram"


def kernel(**inputs):
    import numpy as _np
    import concourse.bacc as _bacc
    from concourse import mybir as _mybir
    from concourse.bass_utils import run_bass_kernel_spmd as _run

    a = {k: _np.asarray(v) for k, v in inputs.items()}
    B, T, D = a["x"].shape
    E = a["L0_ffn_expert_w"].shape[0]
    layout = dict(
        x=a["x"], xT=a["x"].reshape(B * T, D).T, ctxT=a["ctx_1024"].transpose(0, 2, 1),
        dn_Wq=a["L0_attn_Wq"], dn_Wk=a["L0_attn_Wk"], dn_Wv=a["L0_attn_Wv"], dn_Wo=a["L0_attn_Wo"],
        dn_Wa=a["L0_attn_Wa"], dn_ba=a["L0_attn_ba"], dn_Wb=a["L0_attn_Wb"], dn_bb=a["L0_attn_bb"],
        dn_Wgd=a["L0_attn_Wgd"], dn_Wgu=a["L0_attn_Wgu"], dn_rms_w=a["L0_attn_rms_w"],
        dn_qcw=a["L0_attn_qcw"], dn_qcb=a["L0_attn_qcb"], dn_kcw=a["L0_attn_kcw"], dn_kcb=a["L0_attn_kcb"],
        dn_vcw=a["L0_attn_vcw"], dn_vcb=a["L0_attn_vcb"],
        xa_Wq=a["L0_xattn_Wq"], xa_Wk=a["L0_xattn_Wk"], xa_Wv=a["L0_xattn_Wv"], xa_Wo=a["L0_xattn_Wo"],
        ff_attn_norm_w=a["L0_ffn_attn_norm_w"], ff_ffn_norm_w=a["L0_ffn_ffn_norm_w"],
        ff_wqT=a["L0_ffn_wq"].T, ff_wkT=a["L0_ffn_wk"].T, ff_wvT=a["L0_ffn_wv"].T, ff_woT=a["L0_ffn_wo"].T,
        ff_gateT=a["L0_ffn_gate_w"].T, ff_expertT=a["L0_ffn_expert_w"].transpose(2, 0, 1).reshape(D, E * D))
    nc = _bacc.Bacc("TRN2", target_bir_lowering=False, num_devices=1)
    arrays, args = {}, {}
    for name, value in layout.items():
        value = _np.ascontiguousarray(value)
        arrays[f"in_{name}_dram"] = value
        args[name] = nc.dram_tensor(f"in_{name}_dram", value.shape, _mybir.dt.from_np(value.dtype), kind="ExternalInput").ap()
    args["out"] = nc.dram_tensor(_OUT, (B, T, D), _mybir.dt.float32, kind="ExternalOutput").ap()
    decoder_layer(nc, **args)
    r = _run(nc, [arrays], core_ids=[0])
    return r.results[0][_OUT]
```

```python
import concourse.bass as bass
from concourse import mybir
from contextlib import ExitStack


def decoder_layer(nc, x, xT, ctxT, dn_Wq, dn_Wk, dn_Wv, dn_Wo, dn_Wa, dn_ba, dn_Wb, dn_bb, dn_Wgd, dn_Wgu, dn_rms_w,
                  dn_qcw, dn_qcb, dn_kcw, dn_kcb, dn_vcw, dn_vcb, xa_Wq, xa_Wk, xa_Wv, xa_Wo,
                  ff_attn_norm_w, ff_ffn_norm_w, ff_wqT, ff_wkT, ff_wvT, ff_woT, ff_gateT, ff_expertT, out):
    ds = bass.ds
    fp32 = mybir.dt.float32
    ALU = mybir.AluOpType
    ACT = mybir.ActivationFunctionType
    X = mybir.AxisListType.X

    B, T, D = x.shape
    P = 128
    KC = D // P
    LN_EPS, RMS_EPS, NORM_FLOOR = 1e-5, 1e-6, 1e-6

    H, DK = 16, 16
    G = P // H
    NG = B // G
    GT = G * T
    HG = GT // 2
    CH = H * DK
    KS = 4
    PAD = KS - 1
    CT = 3 * CH // P
    AB, GD = 2 * CT, 2 * CT + 2
    GU = GD + 2
    PU = GU + 2 * KC
    STEPS = T // (G - 1)
    STEPS_IN_PAIRS = (0, 1, 2, 3, 4, 5, 6, 7)

    S = ctxT.shape[2]
    XH, XD = 16, 64
    XC = XH * XD
    NP = XH // 2
    SC = 3
    SK = S // SC
    VH = XC // 512
    FV = NP
    FX = FV + SC * VH
    FQ = FX + 1
    FU = FQ + 2

    FH, FD, KV = 16, 16, 4
    REP = FH // KV
    E = ff_gateT.shape[1]
    EU = E * D // 512
    MASKED = -1e30

    ctx = ExitStack()
    with ctx:
        def sb(name, shape, dt=fp32):
            return ctx.enter_context(nc.sbuf_tensor(name, shape, dt))

        def sem(name):
            return ctx.enter_context(nc.semaphore(name))

        def dram(name, shape):
            return nc.dram_tensor(name, shape, fp32, kind="Internal").ap()

        qkv_dram = dram("qkv_dram", (3, B, CH, T))
        ab_dram = dram("ab_dram", (2, B, H, T))
        gate_dram = dram("gate_dram", (B, CH, T))
        o_dram = dram("o_dram", (B, CH, T))

        ident = sb("ident", [P, P])
        causal = sb("causal", [T, T])
        before = sb("before", [T, E, E])
        minus_half, ln_eps, rms_eps = sb("minus_half", [P, 1]), sb("ln_eps", [P, 1]), sb("rms_eps", [P, 1])
        w_qkv = sb("w_qkv", [P, KC, 3 * CH])
        w_ab = sb("w_ab", [P, KC, 2 * H])
        w_gd = sb("w_gd", [P, KC, CH // 2])
        w_gu = sb("w_gu", [P, 1, CH])
        w_dno = sb("w_dno", [P, KC, D])
        taps = sb("taps", [P, CT, KS])
        conv_bias = sb("conv_bias", [P, CT])
        ab_bias = sb("ab_bias", [2 * H, 1])
        ab_low = sb("ab_low", [2 * H, 1])
        rms_w = sb("rms_w", [P, DK])
        w_xq = sb("w_xq", [P, KC, XC])
        w_xk = sb("w_xk", [P, KC, XC])
        w_xv = sb("w_xv", [P, KC, XC])
        w_xo = sb("w_xo", [P, XC // P, D])
        attn_w = sb("attn_w", [P, KC])
        ffn_w = sb("ffn_w", [P, KC])
        w_fq = sb("w_fq", [P, KC, REP, P])
        w_fk = sb("w_fk", [P, KC, P])
        w_fv = sb("w_fv", [P, KC, KV * FD])
        w_fo = sb("w_fo", [P, KC, D])
        w_gate = sb("w_gate", [P, KC, E])
        w_exp = sb("w_exp", [P, KC, E * D])

        xT_in = sb("xT_in", [P, KC, GT])
        raw = sb("raw", [P, 2, G, T + PAD])
        work = sb("work", [P, 4, GT])
        conv = work[:, 0:2]
        tanh_half = work[:, 2:4]
        gate_mid = work[:, 3:4]
        act2 = sb("act2", [P, 2, GT])
        gate_t = act2
        kq = sb("kq", [P, 2, DK, T])
        kn = sb("kn", [P, DK, T])
        val = sb("val", [P, DK, T])
        ab = val[:].rearrange("p d t -> p (d t)")[0:2 * H, 0:GT]
        alpha = sb("alpha", [P, T])
        beta = sb("beta", [P, T])
        sq = sb("sq", [P, DK, T])
        norm = sb("norm", [P, 2, T])
        rnorm = sb("rnorm", [P, 2, T])
        kdotq = sb("kdotq", [P, T])
        state = sb("state", [P, DK, DK])
        prod = sb("prod", [P, 2, DK, DK])
        outer = sb("outer", [P, DK, DK])
        read = work[:].rearrange("p a n -> p (a n)").rearrange("p (t s j) -> p t s j", s=2, j=DK)
        upd = act2[:].rearrange("p a n -> p (a n)").rearrange("p (t j) -> p t j", j=DK)
        o_seq = sb("o_seq", [P, KC, T])
        gate_seq = sb("gate_seq", [P, KC, T])
        gated = o_seq
        x_seq = sb("x_seq", [T, D])
        sum1 = x_seq
        stats1 = sb("stats1", [T, 6])
        mv1 = sb("mv1", [T, 2])
        rstd1 = sb("rstd1", [T, 1])
        x1 = sb("x1", [T, D])

        xaT = sb("xaT", [P, KC, T])
        cT = sb("cT", [P, KC, S])
        qT = sb("qT", [P, NP, T])
        kT = sb("kT", [P, NP, S])
        v_sb = sb("v_sb", [SK, SC, XC])
        cx = sb("cx", [T, XC])
        negmax = sb("negmax", [T, XH])
        rowsum = sb("rowsum", [T, XH])
        rrow = sb("rrow", [T, XH])
        probs_flat = sb("probs_flat", [P, 4 * S])
        probs = probs_flat[0:T].rearrange("p (a s) -> p a s", a=4)
        probsT = sb("probsT", [SK, 2, 2, SC, T])
        cxT = probs_flat[:, 0:XC // P * T].rearrange("p (m t) -> p m t", t=T)
        sum2 = sb("sum2", [T, D])
        stats2 = sb("stats2", [T, 6])
        mv2 = sb("mv2", [T, 2])
        rstd2 = sb("rstd2", [T, 1])
        x2 = sb("x2", [T, D])
        junk = sum2
        ms2 = sb("ms2", [T, 1])
        rms2 = sb("rms2", [T, 1])
        xn = sb("xn", [T, D])
        xnT = sb("xnT", [P, KC, T])
        fq = sb("fq", [P, REP, T])
        fk = sb("fk", [P, T])
        fv = sb("fv", [T, KV * FD])
        fs = probs_flat[0:T, 0:2 * REP * T].rearrange("p (a m t) -> p a m t", a=2, m=REP)
        fmax = sb("fmax", [T, KV, REP])
        fsum = sb("fsum", [T, KV, REP])
        frow = sb("frow", [T, KV * REP])
        fp = cx[:, 0:2 * REP * T].rearrange("p (a m t) -> p a m t", a=2, m=REP)
        fpT = probsT[0:T].rearrange("p a b c t -> p (a b c t)")[:, 0:2 * REP * T].rearrange("p (a m t) -> p a m t", a=2, m=REP)
        fo = sum2
        foT = xnT
        h_sb = sb("h_sb", [T, D])
        ms3 = sb("ms3", [T, 1])
        rms3 = sb("rms3", [T, 1])
        hn = xn
        hnT = xnT
        logit = sb("logit", [T, E])
        neglmax = sb("neglmax", [T, 1])
        above = sb("above", [T, E, E])
        tied = sb("tied", [T, E, E])
        rank = sb("rank", [T, E])
        elog = sb("elog", [T, E])
        comb = sb("comb", [T, E])
        csum = sb("csum", [T, 1])
        rcsum = sb("rcsum", [T, 1])
        acc = sb("acc", [T, D])
        stats3 = sb("stats3", [T, 6])
        mv3 = sb("mv3", [T, 2])
        rstd3 = sb("rstd3", [T, 1])
        y_out = sb("y_out", [T, D])

        bank = [ctx.enter_context(nc.psum_tensor(f"bank{n}", [P, 512], fp32)) for n in range(4, 8)]
        score4 = ctx.enter_context(nc.psum_tensor("score4", [P, 4, 512], fp32))
        PT0, PT1, OV, MX = bank

        dn_w_in, conv_w_in, xa_w_in, ff_w_in = sem("dn_w_in"), sem("conv_w_in"), sem("xa_w_in"), sem("ff_w_in")
        dve_const, pool_const, scaled_w = sem("dve_const"), sem("pool_const"), sem("scaled_w")
        pads_zero = sem("pads_zero")
        xT_loaded = sem("xT_loaded")
        proj_ready, proj_taken = sem("proj_ready"), sem("proj_taken")
        tap_done, conv_ready, tanh_ready, act_ready = sem("tap_done"), sem("conv_ready"), sem("tanh_ready"), sem("act_ready")
        act_stored = [sem("act_stored0"), sem("act_stored1")]
        ab_half, ab_ready, ab_stored = sem("ab_half"), sem("ab_ready"), sem("ab_stored")
        gate_raw, gate_mid_ready, gate_stored = sem("gate_raw"), sem("gate_mid_ready"), sem("gate_stored")
        k_in, q_in, vab_in = sem("k_in"), sem("q_in"), sem("vab_in")
        squares, norm_ready, norm_floor, rnorm_ready, pair_step = (
            sem("squares"), sem("norm_ready"), sem("norm_floor"), sem("rnorm_ready"), sem("pair_step"))
        rec_step, state_ready = sem("rec_step"), sem("state_ready")
        o_part, o_raw, o_squares, o_weighted, o_norm, o_floor, o_rnorm, o_ready, o_stored = (
            sem("o_part"), sem("o_raw"), sem("o_squares"), sem("o_weighted"), sem("o_norm"), sem("o_floor"), sem("o_rnorm"),
            sem("o_ready"), sem("o_stored"))
        seq_loaded, gated_ready, dn_out, sum1_ready, stats1_ready, mv1_ready, var1_ready, rstd1_ready, x1_ready = (
            sem("seq_loaded"), sem("gated_ready"), sem("dn_out"), sem("sum1_ready"), sem("stats1_ready"), sem("mv1_ready"),
            sem("var1_ready"), sem("rstd1_ready"), sem("x1_ready"))

        cT_loaded, fill_ready, fill_taken = sem("cT_loaded"), sem("fill_ready"), sem("fill_taken")
        scores_ready, max_ready, exp_ready = sem("scores_ready"), sem("max_ready"), sem("exp_ready")
        pT_ready, pT_copied_v, pT_copied_s, pv_ready = sem("pT_ready"), sem("pT_copied_v"), sem("pT_copied_s"), sem("pv_ready")
        rrow_ready, cx_ready, cxT_ready, cxT_copied_s, cxT_copied_v = (
            sem("rrow_ready"), sem("cx_ready"), sem("cxT_ready"), sem("cxT_copied_s"), sem("cxT_copied_v"))
        xo_ready, sum2_ready, stats2_ready, mv2_ready, var2_ready, rstd2_ready, x2_ready = (
            sem("xo_ready"), sem("sum2_ready"), sem("stats2_ready"), sem("mv2_ready"), sem("var2_ready"), sem("rstd2_ready"),
            sem("x2_ready"))
        ms2_ready, msv2_ready, rms2_ready, xn_ready, xnT_ready, xnT_copied = (
            sem("ms2_ready"), sem("msv2_ready"), sem("rms2_ready"), sem("xn_ready"), sem("xnT_ready"), sem("xnT_copied"))
        fq_ready, fkv_ready, fq_copied, fkv_copied = sem("fq_ready"), sem("fkv_ready"), sem("fq_copied"), sem("fkv_copied")
        fs_ready, fs_masked, fmax_ready, fexp_ready, fpT_ready, fpT_copied = (
            sem("fs_ready"), sem("fs_masked"), sem("fmax_ready"), sem("fexp_ready"), sem("fpT_ready"), sem("fpT_copied"))
        fpv_ready, frow_ready, fo_ready, foT_ready, foT_copied, fwo_ready, h_ready = (
            sem("fpv_ready"), sem("frow_ready"), sem("fo_ready"), sem("foT_ready"), sem("foT_copied"), sem("fwo_ready"),
            sem("h_ready"))
        ms3_ready, msv3_ready, rms3_ready, hn_ready, hnT_ready, hnT_copied = (
            sem("ms3_ready"), sem("msv3_ready"), sem("rms3_ready"), sem("hn_ready"), sem("hnT_ready"), sem("hnT_copied"))
        gate_ready, logit_ready, logit_max, ranks, elog_ready, comb_step, comb_ready, acc_start = (
            sem("gate_ready"), sem("logit_ready"), sem("logit_max"), sem("ranks"), sem("elog_ready"), sem("comb_step"),
            sem("comb_ready"), sem("acc_start"))
        expert_ready, expert_step, stats3_ready, mv3_ready, var3_ready, rstd3_ready, y_ready, y_stored = (
            sem("expert_ready"), sem("expert_step"), sem("stats3_ready"), sem("mv3_ready"), sem("var3_ready"),
            sem("rstd3_ready"), sem("y_ready"), sem("y_stored"))

        DN_W = 16 * 8
        CONV_W = 16 * (6 + 2 + G)
        XA_W = 16 * 4
        FF_W = 16 * (2 + 2 * KC * KV + 3 + 1)

        def chunks(w):
            return w.rearrange("(c p) n -> p c n", p=P)

        def column(w):
            return w.rearrange("(m p o) -> p m o", p=P, o=1)

        def over_channels(row):
            return row.rearrange("p (o t) -> p o t", o=1).broadcast_to([P, DK, T])

        block = ctx.enter_context(nc.Block())

        @block.sync
        def _(sp):
            def input_load(g):
                if not isinstance(g, int) or g > 0:
                    sp.wait_ge(proj_ready, g * PU)
                sp.dma_start(xT_in[:], chunks(xT)[:, :, ds(g * GT, GT)]).then_inc(xT_loaded, 16)

            def to_pairs(g):
                def load(n, dst, loaded):
                    for parity in range(2):
                        sp.wait_ge(act_stored[parity], g * 16 * (CT // 2) + 16 * (n + 1))
                    if n == 2:
                        sp.wait_ge(ab_stored, g * 32 + 32)
                    sp.dma_start(dst.rearrange("p d t -> p (d t)"),
                                 qkv_dram[n, ds(g * G, G)].rearrange("b (h d) t -> (b h) (d t)", d=DK)).then_inc(loaded, 16)
                for m in range(CT):
                    sp.wait_ge(act_ready, g * CT + m + 1)
                    sp.dma_start(qkv_dram[m // KC, ds(g * G, G), P * (m % KC):P * (m % KC + 1)].rearrange("b p t -> p b t"),
                                 act2[:, m % 2].rearrange("p (b t) -> p b t", b=G)).then_inc(act_stored[m % 2], 16)
                    if m == 2:
                        load(0, kn[:], k_in)
                    if m == 4:
                        load(1, kq[:, 1], q_in)
                sp.wait_ge(ab_ready, g + 1)
                for n in range(2):
                    sp.dma_start(ab_dram[n, ds(g * G, G)].rearrange("b h t -> h b t"),
                                 ab[H * n:H * (n + 1)].rearrange("p (b t) -> p b t", b=G)).then_inc(ab_stored, 16)
                load(2, val[:], vab_in)
                for n, dst in enumerate((alpha, beta)):
                    sp.dma_start(dst[:], ab_dram[n, ds(g * G, G)].rearrange("b h t -> (b h) t")).then_inc(vab_in, 16)

            def gate_store(g):
                for m in range(KC):
                    sp.wait_ge(proj_taken, g * PU + GU + 2 * (m + 1))
                    sp.dma_start(gate_dram[ds(g * G, G), P * m:P * (m + 1)].rearrange("b p t -> p b t"),
                                 gate_t[:, m].rearrange("p (b t) -> p b t", b=G)).then_inc(gate_stored, 16)

            def output_store(g):
                sp.wait_ge(o_ready, g + 1)
                sp.dma_start(o_dram[ds(g * G, G)].rearrange("b (h d) t -> (b h) (d t)", d=DK),
                             val[:].rearrange("p d t -> p (d t)")).then_inc(o_stored, 16)
                sp.wait_ge(o_stored, g * 16 + 16)
                sp.wait_ge(gate_stored, g * 32 + 32)

            def context_load(i):
                if not isinstance(i, int):
                    sp.wait_ge(fill_ready, i * FU + (FX - FU))
                sp.dma_start(cT[:], ctxT[ds(i, 1)].rearrange("o (c p) s -> p (o c) s", p=P)).then_inc(cT_loaded, 16)

            def sequence_load(i):
                if not isinstance(i, int) or i > 0:
                    sp.wait_ge(x1_ready, i)
                sp.dma_start(o_seq[:], o_dram[ds(i, 1)].rearrange("o (c p) t -> p (o c) t", p=P)).then_inc(seq_loaded, 16)
                sp.dma_start(gate_seq[:], gate_dram[ds(i, 1)].rearrange("o (c p) t -> p (o c) t", p=P)).then_inc(seq_loaded, 16)
                sp.dma_start(x_seq[:], x[ds(i, 1)].rearrange("o t d -> t (o d)")).then_inc(seq_loaded, 16)

            def store(i):
                sp.wait_ge(y_ready, i + 1)
                sp.dma_start(out[ds(i, 1)].rearrange("o t d -> t (o d)"), y_out[:]).then_inc(y_stored, 16)

            def sequence(i, fill=True, post=None, pre=None):
                if fill:
                    context_load(i + 1)
                if pre is not None:
                    input_load(pre)
                if post is not None:
                    output_store(post)
                if fill:
                    sequence_load(i + 1)
                if pre is not None:
                    to_pairs(pre)
                store(i)
                if pre is not None:
                    gate_store(pre)

            for n, w in enumerate((dn_Wk, dn_Wq, dn_Wv)):
                sp.dma_start(w_qkv[:, :, CH * n:CH * (n + 1)], chunks(w)).then_inc(dn_w_in, 16)
            input_load(0)
            sp.dma_start(w_ab[:, :, 0:H], chunks(dn_Wa)).then_inc(dn_w_in, 16)
            sp.dma_start(w_ab[:, :, H:2 * H], chunks(dn_Wb)).then_inc(dn_w_in, 16)
            sp.dma_start(w_gd[:], chunks(dn_Wgd)).then_inc(dn_w_in, 16)
            sp.dma_start(w_gu[:], dn_Wgu.rearrange("(o p) n -> p o n", o=1)).then_inc(dn_w_in, 16)
            sp.dma_start(w_dno[:], chunks(dn_Wo)).then_inc(dn_w_in, 16)
            to_pairs(0)
            gate_store(0)
            context_load(0)
            output_store(0)
            sequence_load(0)
            input_load(1)
            to_pairs(1)
            gate_store(1)
            if NG > 2:
                with sp.Fori(0, NG - 2) as g:
                    with sp.Fori(0, G - 1) as s:
                        sequence(g * G + s)
                    sequence(g * G + (G - 1), post=g + 1, pre=g + 2)
            with sp.Fori(0, G - 1) as s:
                sequence((NG - 2) * G + s)
            sequence((NG - 1) * G - 1, post=NG - 1)
            with sp.Fori((NG - 1) * G, B - 1) as i:
                sequence(i)
            sequence(B - 1, fill=False)
            sp.wait_ge(y_stored, 16 * B)

        @block.gpsimd
        def _(pool):
            nc.gpsimd.memset(ident[:], 0.0).then_inc(pool_const, 1)
            nc.gpsimd.memset(causal[:], 0.0).then_inc(pool_const, 1)
            nc.gpsimd.memset(before[:], 1.0).then_inc(pool_const, 1)
            nc.gpsimd.memset(minus_half[:], -0.5).then_inc(pool_const, 1)
            nc.gpsimd.memset(ln_eps[:], LN_EPS).then_inc(pool_const, 1)
            nc.gpsimd.memset(rms_eps[:], RMS_EPS).then_inc(pool_const, 1)
            pool.wait_ge(pool_const, 6)
            nc.gpsimd.affine_select(out=ident[:], in_=ident[:], compare_op=ALU.not_equal, fill=1.0, base=0,
                                    pattern=[[-1, P]], channel_multiplier=1).then_inc(pool_const, 1)
            nc.gpsimd.affine_select(out=causal[:], in_=causal[:], compare_op=ALU.is_ge, fill=MASKED, base=0,
                                    pattern=[[-1, T]], channel_multiplier=1).then_inc(pool_const, 1)
            nc.gpsimd.affine_select(out=before[:], in_=before[:], compare_op=ALU.is_gt, fill=0.0, base=0,
                                    pattern=[[1, E], [-1, E]], channel_multiplier=0).then_inc(pool_const, 1)
            pool.wait_ge(pool_const, 9)

            def pair_norms(g):
                for n in range(2):
                    pool.wait_ge(norm_floor, g * 2 + n + 1)
                    nc.gpsimd.tensor_tensor(rnorm[:, n], norm[:, n], minus_half[:].broadcast_to([P, T]), ALU.pow).then_inc(rnorm_ready, 1)

            def output_norms(g):
                pool.wait_ge(o_norm, g + 1)
                nc.gpsimd.tensor_tensor(norm[:, 0], norm[:, 0], rms_eps[:].broadcast_to([P, T]), ALU.add).then_inc(o_floor, 1)
                pool.wait_ge(o_floor, g + 1)
                nc.gpsimd.tensor_tensor(rnorm[:, 0], norm[:, 0], minus_half[:].broadcast_to([P, T]), ALU.pow).then_inc(o_rnorm, 1)

            def first_norm(i):
                pool.wait_ge(mv1_ready, i + 1)
                nc.gpsimd.tensor_tensor(mv1[:, 1:2], mv1[:, 1:2], ln_eps[0:T], ALU.add).then_inc(var1_ready, 1)
                pool.wait_ge(var1_ready, i + 1)
                nc.gpsimd.tensor_tensor(rstd1[:], mv1[:, 1:2], minus_half[0:T], ALU.pow).then_inc(rstd1_ready, 1)

            def second_norms(i):
                pool.wait_ge(mv2_ready, i + 1)
                nc.gpsimd.tensor_tensor(mv2[:, 1:2], mv2[:, 1:2], ln_eps[0:T], ALU.add).then_inc(var2_ready, 1)
                pool.wait_ge(var2_ready, i + 1)
                nc.gpsimd.tensor_tensor(rstd2[:], mv2[:, 1:2], minus_half[0:T], ALU.pow).then_inc(rstd2_ready, 1)
                pool.wait_ge(ms2_ready, i + 1)
                nc.gpsimd.tensor_tensor(ms2[:], ms2[:], rms_eps[0:T], ALU.add).then_inc(msv2_ready, 1)
                pool.wait_ge(msv2_ready, i + 1)
                nc.gpsimd.tensor_tensor(rms2[:], ms2[:], minus_half[0:T], ALU.pow).then_inc(rms2_ready, 1)

            def third_norms(i):
                pool.wait_ge(ms3_ready, i + 1)
                nc.gpsimd.tensor_tensor(ms3[:], ms3[:], rms_eps[0:T], ALU.add).then_inc(msv3_ready, 1)
                pool.wait_ge(msv3_ready, i + 1)
                nc.gpsimd.tensor_tensor(rms3[:], ms3[:], minus_half[0:T], ALU.pow).then_inc(rms3_ready, 1)
                pool.wait_ge(h_ready, i + 1)
                nc.gpsimd.tensor_tensor(acc[:], h_sb[:], x2[:], ALU.add).then_inc(acc_start, 1)
                pool.wait_ge(mv3_ready, i + 1)
                nc.gpsimd.tensor_tensor(mv3[:, 1:2], mv3[:, 1:2], ln_eps[0:T], ALU.add).then_inc(var3_ready, 1)
                pool.wait_ge(var3_ready, i + 1)
                nc.gpsimd.tensor_tensor(rstd3[:], mv3[:, 1:2], minus_half[0:T], ALU.pow).then_inc(rstd3_ready, 1)

            def sequence(i, fill=True, post=None, pre=None):
                if post is not None:
                    output_norms(post)
                second_norms(i)
                if fill:
                    first_norm(i + 1)
                third_norms(i)
                if pre is not None:
                    pair_norms(pre)

            pair_norms(0)
            output_norms(0)
            first_norm(0)
            pair_norms(1)
            if NG > 2:
                with pool.Fori(0, NG - 2) as g:
                    with pool.Fori(0, G - 1) as s:
                        sequence(g * G + s)
                    sequence(g * G + (G - 1), post=g + 1, pre=g + 2)
            with pool.Fori(0, G - 1) as s:
                sequence((NG - 2) * G + s)
            sequence((NG - 1) * G - 1, post=NG - 1)
            with pool.Fori((NG - 1) * G, B - 1) as i:
                sequence(i)
            sequence(B - 1, fill=False)

        @block.scalar
        def _(act):
            for n, (cw, cb) in enumerate(((dn_kcw, dn_kcb), (dn_qcw, dn_qcb), (dn_vcw, dn_vcb))):
                act.dma_start(taps[:, KC * n:KC * (n + 1)], cw.rearrange("(m p) k -> p m k", p=P)).then_inc(conv_w_in, 16)
                act.dma_start(conv_bias[:, KC * n:KC * (n + 1)].rearrange("p (m o) -> p m o", o=1), column(cb), allow_slow_non_contiguous=True).then_inc(conv_w_in, 16)
            act.dma_start(ab_bias[0:H], dn_ba.rearrange("(p o) -> p o", o=1)).then_inc(conv_w_in, 16)
            act.dma_start(ab_bias[H:2 * H], dn_bb.rearrange("(p o) -> p o", o=1)).then_inc(conv_w_in, 16)
            for b in range(G):
                act.dma_start(rms_w[H * b:H * (b + 1)], dn_rms_w).then_inc(conv_w_in, 16)
            for dst, w in ((w_xq, xa_Wq), (w_xk, xa_Wk), (w_xv, xa_Wv), (w_xo, xa_Wo)):
                act.dma_start(dst[:], chunks(w)).then_inc(xa_w_in, 16)
            act.dma_start(attn_w[:].rearrange("p (m o) -> p m o", o=1), column(ff_attn_norm_w), allow_slow_non_contiguous=True).then_inc(ff_w_in, 16)
            act.dma_start(ffn_w[:].rearrange("p (m o) -> p m o", o=1), column(ff_ffn_norm_w), allow_slow_non_contiguous=True).then_inc(ff_w_in, 16)
            act.dma_start(w_fv[:], chunks(ff_wvT)).then_inc(ff_w_in, 16)
            act.dma_start(w_fo[:], chunks(ff_woT)).then_inc(ff_w_in, 16)
            act.dma_start(w_gate[:], chunks(ff_gateT)).then_inc(ff_w_in, 16)
            act.dma_start(w_exp[:], chunks(ff_expertT)).then_inc(ff_w_in, 16)
            act.wait_ge(pads_zero, 2)
            for j in range(KV):
                for k in range(KC):
                    act.dma_start(w_fq[:, k, :, 32 * j:32 * j + FD],
                                  ff_wqT[P * k:P * (k + 1), REP * FD * j:REP * FD * (j + 1)].rearrange("p (m d) -> p m d", d=FD)
                                  ).then_inc(ff_w_in, 16)
                    act.dma_start(w_fk[:, k, 32 * j:32 * j + FD], ff_wkT[P * k:P * (k + 1), FD * j:FD * (j + 1)]).then_inc(ff_w_in, 16)
            act.wait_ge(dve_const, 1)

            src3 = score4[:, 3]

            def tanh_of(g, m):
                act.wait_ge(conv_ready, g * CT + m + 1)
                if m >= 2:
                    act.wait_ge(act_ready, g * CT + m - 1)
                elif m == 0 and (not isinstance(g, int) or g > 0):
                    act.wait_ge(o_raw, g)
                nc.scalar.activation(tanh_half[:, m % 2], conv[:, m % 2], ACT.Tanh, scale=0.5).then_inc(tanh_ready, 1)

            def projection(g, u):
                act.wait_ge(proj_ready, g * PU + u + 1)
                if u < 2 * CT:
                    m, h = divmod(u, 2)
                    if m >= 2 and h == 0:
                        act.wait_ge(conv_ready, g * CT + m - 1)
                    nc.scalar.activation(raw[:, m % 2, G // 2 * h:G // 2 * (h + 1), PAD:],
                                         src3[:, 0:HG].rearrange("p (b t) -> p b t", t=T), ACT.Copy).then_inc(proj_taken, 1)
                    if m >= 1 and h == 1:
                        tanh_of(g, m - 1)
                elif u < GD:
                    h = u - 2 * CT
                    if not isinstance(g, int) or g > 0:
                        act.wait_ge(o_stored, g * 16)
                    nc.scalar.activation(ab[:, HG * h:HG * (h + 1)], src3[0:2 * H, 0:HG], ACT.Tanh, scale=0.5,
                                         bias=ab_bias[:]).then_inc(proj_taken, 1)
                    if h == 1:
                        tanh_of(g, CT - 1)
                elif u < GU:
                    h = u - GD
                    if h == 0:
                        act.wait_ge(act_ready, g * CT + CT)
                    nc.scalar.activation(conv[:, 0, HG * h:HG * (h + 1)], src3[:, 0:HG], ACT.Copy).then_inc(proj_taken, 1)
                    if h == 1:
                        act.wait_ge(proj_taken, g * PU + GU)
                        nc.scalar.activation(tanh_half[:, 0], conv[:, 0], ACT.Tanh, scale=0.5).then_inc(gate_raw, 1)
                else:
                    m, h = divmod(u - GU, 2)
                    act.wait_ge(act_stored[m], (g + 1) * 16 * (CT // 2))
                    nc.scalar.activation(gate_t[:, m, HG * h:HG * (h + 1)], src3[:, 0:HG], ACT.Tanh,
                                         scale=0.25).then_inc(proj_taken, 1)

            def pair_squares(g, n):
                act.wait_ge((k_in, q_in)[n], g * 16 + 16)
                if n == 1:
                    act.wait_ge(norm_ready, g * 2 + 1)
                nc.scalar.activation(sq[:], (kn[:], kq[:, 1])[n], ACT.Square).then_inc(squares, 1)

            def output_squares(g):
                act.wait_ge(o_raw, g + 1)
                nc.scalar.activation(kq[:, 0], val[:], ACT.Square, scale=DK ** -0.5).then_inc(o_squares, 1)

            def take(i, u):
                src = score4[:, u % 3]
                act.wait_ge(fill_ready, i * FU + u + 1)
                if u < FV:
                    nc.scalar.activation(kT[:, u], src[:, 0:S], ACT.Copy).then_inc(fill_taken, 1)
                elif u < FX:
                    c, h = divmod(u - FV, VH)
                    nc.scalar.activation(v_sb[:, c, 512 * h:512 * (h + 1)], src[0:SK, :], ACT.Copy).then_inc(fill_taken, 1)
                elif u < FQ:
                    nc.scalar.activation(xaT[:].rearrange("p c t -> p (c t)"), src[:, 0:KC * T], ACT.Copy).then_inc(fill_taken, 1)
                else:
                    n = NP // 2 * (u - FQ)
                    nc.scalar.activation(qT[:, n:n + NP // 2].rearrange("p m t -> p (m t)"), src[:, 0:NP // 2 * T], ACT.Copy,
                                         scale=XD ** -0.5).then_inc(fill_taken, 1)

            def attention(i, post=None):
                def copy_second(p):
                    act.wait_ge(pT_ready, i * NP + p + 1)
                    if p >= 2:
                        act.wait_ge(pv_ready, i * NP + p - 1)
                    nc.scalar.activation(probsT[:, p % 2, 1].rearrange("p c t -> p (c t)"), PT1[0:SK, 0:SC * T], ACT.Copy
                                         ).then_inc(pT_copied_s, 1)
                for p in range(NP):
                    act.wait_ge(max_ready, i * NP + p + 1)
                    for a in range(2):
                        h = 2 * p + a
                        nc.scalar.activation(probs[:, 2 * (p % 2) + a], score4[0:T, 2 * (p % 2) + a, 0:S], ACT.Exp,
                                             bias=negmax[:, h:h + 1], accum_out=rowsum[:, h:h + 1]).then_inc(exp_ready, 1)
                    if p >= 1:
                        copy_second(p - 1)
                    if p == 2 and post is not None:
                        output_squares(post)
                copy_second(NP - 1)

            def chain(i, fill, pre=None):
                def take_next(*us):
                    if fill:
                        for u in us:
                            take(i + 1, u)
                            if pre is not None and u < GU:
                                projection(pre, u)
                take_next(0)
                act.wait_ge(cxT_ready, i * 2 + 1)
                nc.scalar.activation(cxT[:, 0:4].rearrange("p m t -> p (m t)"), PT0[:, 0:4 * T], ACT.Copy).then_inc(cxT_copied_s, 1)
                take_next(1, 2, 3, 4, 5)
                act.wait_ge(x2_ready, i + 1)
                nc.scalar.activation(junk[:], x2[:], ACT.Square, scale=D ** -0.5, accum_out=ms2[:]).then_inc(ms2_ready, 1)
                take_next(6)
                act.wait_ge(xnT_ready, i + 1)
                nc.scalar.activation(xnT[:].rearrange("p c t -> p (c t)"), MX[:, 0:KC * T], ACT.Copy).then_inc(xnT_copied, 1)
                take_next(7)
                act.wait_ge(fq_ready, i + 1)
                nc.scalar.activation(fq[:].rearrange("p m t -> p (m t)"), PT0[:, 0:REP * T], ACT.Copy, scale=FD ** -0.5
                                     ).then_inc(fq_copied, 1)
                take_next(8)
                for j in range(KV):
                    act.wait_ge(fmax_ready, i * KV + j + 1)
                    if j >= 2:
                        act.wait_ge(fpT_ready, i * KV + j - 1)
                    for m in range(REP):
                        last = nc.scalar.activation(fp[:, j % 2, m], fs[:, j % 2, m], ACT.Exp, bias=fmax[:, j, m:m + 1],
                                                    accum_out=fsum[:, j, m:m + 1])
                    last.then_inc(fexp_ready, 1)
                    take_next(9 + j)
                take_next(13)
                act.wait_ge(foT_ready, i + 1)
                nc.scalar.activation(foT[:].rearrange("p c t -> p (c t)"), OV[:, 0:KC * T], ACT.Copy).then_inc(foT_copied, 1)
                take_next(14)
                act.wait_ge(h_ready, i + 1)
                nc.scalar.activation(junk[:], h_sb[:], ACT.Square, scale=D ** -0.5, accum_out=ms3[:]).then_inc(ms3_ready, 1)
                take_next(15, 16)
                act.wait_ge(hnT_ready, i + 1)
                nc.scalar.activation(hnT[:].rearrange("p c t -> p (c t)"), MX[:, 0:KC * T], ACT.Copy).then_inc(hnT_copied, 1)
                if pre is not None:
                    pair_squares(pre, 0)
                    for u in range(GU, PU):
                        projection(pre, u)
                act.wait_ge(logit_max, i + 1)
                nc.scalar.activation(elog[:], logit[:], ACT.Exp, bias=neglmax[:]).then_inc(elog_ready, 1)
                if pre is not None:
                    pair_squares(pre, 1)

            def sequence(i, fill=True, post=None, pre=None):
                attention(i, post)
                chain(i, fill, pre)

            for u in range(PU):
                projection(0, u)
            for n in range(2):
                pair_squares(0, n)
            for u in range(FX):
                take(0, u)
            output_squares(0)
            for u in range(FX, FU):
                take(0, u)
            for u in range(PU):
                projection(1, u)
            for n in range(2):
                pair_squares(1, n)
            if NG > 2:
                with act.Fori(0, NG - 2) as g:
                    with act.Fori(0, G - 1) as s:
                        sequence(g * G + s)
                    sequence(g * G + (G - 1), post=g + 1, pre=g + 2)
            with act.Fori(0, G - 1) as s:
                sequence((NG - 2) * G + s)
            sequence((NG - 1) * G - 1, post=NG - 1)
            with act.Fori((NG - 1) * G, B - 1) as i:
                sequence(i)
            sequence(B - 1, fill=False)

        @block.tensor
        def _(pe):
            def projection(g, u):
                if u == 0:
                    pe.wait_ge(xT_loaded, g * 16 + 16)
                if u > 0 or not isinstance(g, int) or g > 0:
                    pe.wait_ge(proj_taken, g * PU + u)
                if u == GU:
                    pe.wait_ge(gate_mid_ready, g + 1)
                first, w, width, src = ((0, w_qkv, P, xT_in) if u < AB else (AB, w_ab, 2 * H, xT_in) if u < GD else
                                        (GD, w_gd, P, xT_in) if u < GU else (GU, w_gu, P, gate_mid))
                m, h = divmod(u - first, 2)
                nk = w.shape[1]
                for k in range(nk):
                    last = nc.tensor.matmul(score4[0:width, 3, 0:HG], w[:, k, width * m:width * (m + 1)], src[:, k, HG * h:HG * (h + 1)],
                                            start=k == 0, stop=k == nk - 1)
                last.then_inc(proj_ready, 1)

            def output_rows(i):
                pe.wait_ge(gated_ready, i + 1)
                for k in range(KC):
                    last = nc.tensor.matmul(score4[0:T, 3, 0:D], gated[:, k], w_dno[:, k], start=k == 0, stop=k == KC - 1)
                last.then_inc(dn_out, 1)

            def fill(i, u):
                dst = score4[:, u % 3]
                if u >= 3:
                    pe.wait_ge(fill_taken, i * FU + u - 2)
                if u < FV:
                    if u == 0:
                        pe.wait_ge(cT_loaded, i * 16 + 16)
                    for k in range(KC):
                        last = nc.tensor.matmul(dst[:, 0:S], w_xk[:, k, P * u:P * (u + 1)], cT[:, k], start=k == 0, stop=k == KC - 1)
                elif u < FX:
                    c, h = divmod(u - FV, VH)
                    for k in range(KC):
                        last = nc.tensor.matmul(dst[0:SK, :], cT[:, k, SK * c:SK * (c + 1)], w_xv[:, k, 512 * h:512 * (h + 1)], start=k == 0, stop=k == KC - 1)
                elif u < FQ:
                    pe.wait_ge(x1_ready, i + 1)
                    for k in range(KC):
                        last = nc.tensor.transpose(dst[:, T * k:T * (k + 1)], x1[:, P * k:P * (k + 1)], ident[0:T, 0:T])
                else:
                    pe.wait_ge(fill_taken, i * FU + FQ)
                    for n in range(NP // 2):
                        m = NP // 2 * (u - FQ) + n
                        for k in range(KC):
                            last = nc.tensor.matmul(dst[:, T * n:T * (n + 1)], w_xq[:, k, P * m:P * (m + 1)], xaT[:, k], start=k == 0, stop=k == KC - 1)
                last.then_inc(fill_ready, 1)

            def attention(i):
                def scores(p):
                    if p >= 2:
                        pe.wait_ge(exp_ready, i * XH + 2 * p - 2)
                    for a in range(2):
                        r = slice(XD * a, XD * (a + 1))
                        last = nc.tensor.matmul(score4[0:T, 2 * (p % 2) + a, 0:S], qT[r, p], kT[r, p], start=True, stop=True)
                    last.then_inc(scores_ready, 1)

                def transposes(p):
                    pe.wait_ge(exp_ready, i * XH + 2 * p + 2)
                    if p >= 1:
                        pe.wait_ge(pT_copied_v, i * NP + p)
                        pe.wait_ge(pT_copied_s, i * NP + p)
                    for a in range(2):
                        for c in range(SC):
                            last = nc.tensor.transpose((PT0, PT1)[a][0:SK, T * c:T * (c + 1)], probs[:, 2 * (p % 2) + a, SK * c:SK * (c + 1)],
                                                       ident[0:T, 0:T])
                    last.then_inc(pT_ready, 1)

                def values(p):
                    pe.wait_ge(pT_copied_v, i * NP + p + 1)
                    pe.wait_ge(pT_copied_s, i * NP + p + 1)
                    dst = OV if p < NP // 2 else MX
                    for a in range(2):
                        h = 2 * p + a
                        col = XD * (h % (XH // 2))
                        for c in range(SC):
                            last = nc.tensor.matmul(dst[0:T, col:col + XD], probsT[:, p % 2, a, c], v_sb[:, c, XD * h:XD * (h + 1)],
                                                    start=c == 0, stop=c == SC - 1)
                    last.then_inc(pv_ready, 1)

                pe.wait_ge(fill_taken, i * FU + FU)
                scores(0)
                scores(1)
                if not isinstance(i, int) or i > 0:
                    pe.wait_ge(expert_step, i * E)
                for p in range(NP):
                    transposes(p)
                    if p >= 1:
                        values(p - 1)
                    if p + 2 < NP:
                        scores(p + 2)
                values(NP - 1)

            def chain(i, with_fill, pre):
                def fill_next(*us):
                    if with_fill:
                        for u in us:
                            fill(i + 1, u)
                            if pre is not None and u < GU:
                                if u == FV + 4:
                                    pe.wait_ge(sum1_ready, i + 2)
                                projection(pre, u)

                def gqa_scores(j):
                    if j >= 2:
                        pe.wait_ge(fs_masked, i * KV + j - 1)
                    r = slice(32 * j, 32 * j + FD)
                    for m in range(REP):
                        last = nc.tensor.matmul((MX, OV)[j % 2][0:T, T * m:T * (m + 1)], fq[r, m], fk[r], start=True, stop=True)
                    last.then_inc(fs_ready, 1)

                def gqa_transposes(j):
                    pe.wait_ge(fexp_ready, i * KV + j + 1)
                    if j >= 2:
                        pe.wait_ge(fpT_copied, i * KV + j - 1)
                    for m in range(REP):
                        last = nc.tensor.transpose((PT0, PT1)[j % 2][0:T, T * m:T * (m + 1)], fp[:, j % 2, m], ident[0:T, 0:T])
                    last.then_inc(fpT_ready, 1)

                def gqa_values(j):
                    pe.wait_ge(fpT_copied, i * KV + j + 1)
                    for m in range(REP):
                        h = REP * j + m
                        last = nc.tensor.matmul(MX[0:T, FD * h:FD * (h + 1)], fpT[:, j % 2, m], fv[:, FD * j:FD * (j + 1)], start=True, stop=True)
                    last.then_inc(fpv_ready, 1)

                fill_next(0)
                for half in range(2):
                    pe.wait_ge(cx_ready, i * 2 + half + 1)
                    for m in range(4):
                        c = 4 * half + m
                        last = nc.tensor.transpose((PT0, PT1)[half][:, T * m:T * (m + 1)], cx[:, P * c:P * (c + 1)], ident[0:T, 0:T])
                    last.then_inc(cxT_ready, 1)
                    fill_next(1 + half)
                pe.wait_ge(cxT_copied_s, i + 1)
                pe.wait_ge(cxT_copied_v, i + 1)
                for m in range(XC // P):
                    last = nc.tensor.matmul(OV[0:T, 0:D], cxT[:, m], w_xo[:, m], start=m == 0, stop=m == XC // P - 1)
                last.then_inc(xo_ready, 1)
                fill_next(3, 4, 5, 6)
                pe.wait_ge(xn_ready, i + 1)
                for k in range(KC):
                    last = nc.tensor.transpose(MX[:, T * k:T * (k + 1)], xn[:, P * k:P * (k + 1)], ident[0:T, 0:T])
                last.then_inc(xnT_ready, 1)
                fill_next(7)
                pe.wait_ge(xnT_copied, i + 1)
                for m in range(REP):
                    for k in range(KC):
                        last = nc.tensor.matmul(PT0[:, T * m:T * (m + 1)], w_fq[:, k, m], xnT[:, k], start=k == 0, stop=k == KC - 1)
                last.then_inc(fq_ready, 1)
                for k in range(KC):
                    nc.tensor.matmul(PT1[:, 0:T], w_fk[:, k], xnT[:, k], start=k == 0, stop=k == KC - 1)
                for k in range(KC):
                    last = nc.tensor.matmul(PT1[0:T, T:T + KV * FD], xnT[:, k], w_fv[:, k], start=k == 0, stop=k == KC - 1)
                last.then_inc(fkv_ready, 1)
                fill_next(8)
                pe.wait_ge(fq_copied, i + 1)
                pe.wait_ge(fkv_copied, i + 1)
                gqa_scores(0)
                gqa_scores(1)
                fill_next(9)
                gqa_scores(2)
                gqa_transposes(0)
                gqa_scores(3)
                fill_next(10)
                gqa_transposes(1)
                fill_next(11)
                if with_fill:
                    if pre is not None:
                        pe.wait_ge(proj_taken, pre * PU + 12)
                    output_rows(i + 1)
                pe.wait_ge(fs_masked, i * KV + KV)
                gqa_values(0)
                gqa_transposes(2)
                gqa_values(1)
                fill_next(12)
                gqa_transposes(3)
                gqa_values(2)
                fill_next(13)
                gqa_values(3)
                pe.wait_ge(fo_ready, i + 1)
                for k in range(KC):
                    last = nc.tensor.transpose(OV[:, T * k:T * (k + 1)], fo[:, P * k:P * (k + 1)], ident[0:T, 0:T])
                last.then_inc(foT_ready, 1)
                fill_next(14)
                pe.wait_ge(foT_copied, i + 1)
                for k in range(KC):
                    last = nc.tensor.matmul(PT0[0:T, 0:D], foT[:, k], w_fo[:, k], start=k == 0, stop=k == KC - 1)
                last.then_inc(fwo_ready, 1)
                fill_next(15, 16)
                pe.wait_ge(hn_ready, i + 1)
                for k in range(KC):
                    last = nc.tensor.transpose(MX[:, T * k:T * (k + 1)], hn[:, P * k:P * (k + 1)], ident[0:T, 0:T])
                last.then_inc(hnT_ready, 1)
                pe.wait_ge(hnT_copied, i + 1)
                for k in range(KC):
                    last = nc.tensor.matmul(PT1[0:T, 0:E], hnT[:, k], w_gate[:, k], start=k == 0, stop=k == KC - 1)
                last.then_inc(gate_ready, 1)
                for u in range(EU):
                    if pre is not None:
                        projection(pre, GU + u)
                        if u == EU - 1:
                            pe.wait_ge(proj_taken, pre * PU + PU)
                    if u == EU - 1:
                        pe.wait_ge(logit_ready, i + 1)
                    for k in range(KC):
                        last = nc.tensor.matmul((OV, PT0, MX, PT1)[u][0:T, :], hnT[:, k], w_exp[:, k, 512 * u:512 * (u + 1)], start=k == 0, stop=k == KC - 1)
                    last.then_inc(expert_ready, 1)

            pe.wait_ge(dn_w_in, DN_W)
            pe.wait_ge(pool_const, 9)
            def sequence(i, fill=True, post=None, pre=None):
                attention(i)
                chain(i, fill, pre)

            for u in range(PU):
                projection(0, u)
            pe.wait_ge(proj_taken, PU)
            pe.wait_ge(xa_w_in, XA_W)
            pe.wait_ge(ff_w_in, FF_W)
            pe.wait_ge(scaled_w, 5)
            for u in range(FX):
                fill(0, u)
            output_rows(0)
            for u in range(FX, FU):
                fill(0, u)
            for u in range(PU):
                projection(1, u)
            pe.wait_ge(proj_taken, 2 * PU)
            if NG > 2:
                with pe.Fori(0, NG - 2) as g:
                    with pe.Fori(0, G - 1) as s:
                        sequence(g * G + s)
                    sequence(g * G + (G - 1), post=g + 1, pre=g + 2)
            with pe.Fori(0, G - 1) as s:
                sequence((NG - 2) * G + s)
            sequence((NG - 1) * G - 1, post=NG - 1)
            with pe.Fori((NG - 1) * G, B - 1) as i:
                sequence(i)
            sequence(B - 1, fill=False)

        @block.vector
        def _(dve):
            nc.vector.memset(w_fq[:], 0.0).then_inc(pads_zero, 1)
            nc.vector.memset(w_fk[:], 0.0).then_inc(pads_zero, 1)
            nc.vector.memset(raw[:], 0.0)
            nc.vector.memset(ab_low[:], 0.0).then_inc(pads_zero, 1)
            dve.wait_ge(conv_w_in, CONV_W)
            dve.wait_ge(pads_zero, 3)
            nc.vector.memset(ab_low[0:H], 0.1)
            nc.vector.tensor_scalar(rms_w[:], rms_w[:], 0.5, None, ALU.mult)
            nc.vector.tensor_scalar(ab_bias[:], ab_bias[:], 0.5, None, ALU.mult).then_inc(dve_const, 1)

            def scale_weights():
                dve.wait_ge(ff_w_in, FF_W)
                for w, norm_w in ((w_fq, attn_w), (w_fk, attn_w), (w_fv, attn_w), (w_gate, ffn_w), (w_exp, ffn_w)):
                    for k in range(KC):
                        last = nc.vector.tensor_scalar(w[:, k], w[:, k], norm_w[:, k:k + 1], None, ALU.mult)
                    last.then_inc(scaled_w, 1)

            def convolution(g, m):
                dve.wait_ge(proj_taken, g * PU + 2 * m + 2)
                if m >= 2:
                    dve.wait_ge(act_ready, g * CT + m - 1)
                r = raw[:, m % 2]
                q = conv[:, m % 2].rearrange("p (b t) -> p b t", t=T)
                at = (g * CT + m) * PAD
                nc.vector.tensor_scalar(q, r[:, :, PAD:], taps[:, m, PAD:KS], conv_bias[:, m:m + 1], ALU.mult, ALU.add).then_inc(tap_done, 1)
                for k in range(PAD - 1, 0, -1):
                    dve.wait_ge(tap_done, at + PAD - k)
                    nc.vector.scalar_tensor_tensor(q, r[:, :, k:k + T], taps[:, m, k:k + 1], q, ALU.mult, ALU.add).then_inc(tap_done, 1)
                dve.wait_ge(tap_done, at + PAD)
                nc.vector.scalar_tensor_tensor(q, r[:, :, 0:T], taps[:, m, 0:1], q, ALU.mult, ALU.add).then_inc(conv_ready, 1)

            def twice_silu(g, m):
                dve.wait_ge(tanh_ready, g * CT + m + 1)
                if m >= 2:
                    dve.wait_ge(act_stored[m % 2], g * 16 * (CT // 2) + 16 * (m // 2))
                nc.vector.scalar_tensor_tensor(act2[:, m % 2], tanh_half[:, m % 2], 1.0, conv[:, m % 2], ALU.add, ALU.mult
                                               ).then_inc(act_ready, 1)

            def alpha_beta(g):
                dve.wait_ge(proj_taken, g * PU + AB + 2)
                nc.vector.tensor_scalar(ab, ab, 0.5, 0.5, ALU.mult, ALU.add).then_inc(ab_half, 1)
                dve.wait_ge(ab_half, g + 1)
                nc.vector.tensor_scalar(ab, ab, ab_low[:], 1.0, ALU.max, ALU.min).then_inc(ab_ready, 1)

            def gate_middle(g):
                dve.wait_ge(gate_raw, g + 1)
                nc.vector.scalar_tensor_tensor(gate_mid[:, 0], tanh_half[:, 0], 1.0, conv[:, 0], ALU.add, ALU.mult).then_inc(gate_mid_ready, 1)

            def pair_norm(g, n):
                dve.wait_ge(squares, g * 2 + n + 1)
                nc.vector.tensor_reduce(norm[:, n], sq[:].rearrange("p d t -> p t d"), X, ALU.add).then_inc(norm_ready, 1)
                dve.wait_ge(norm_ready, g * 2 + n + 1)
                nc.vector.tensor_scalar(norm[:, n], norm[:, n], (2 * NORM_FLOOR) ** 2, None, ALU.max).then_inc(norm_floor, 1)

            def pairs(g):
                at = g * 3
                dve.wait_ge(rnorm_ready, g * 2 + 1)
                nc.vector.tensor_tensor(kn[:], kn[:], over_channels(rnorm[:, 0]), ALU.mult)
                dve.wait_ge(vab_in, g * 48 + 48)
                nc.vector.scalar_tensor_tensor(val[:], val[:], 0.5, over_channels(beta[:]), ALU.mult, ALU.mult)
                dve.wait_ge(rnorm_ready, g * 2 + 2)
                nc.vector.tensor_tensor(kq[:, 1], kq[:, 1], over_channels(rnorm[:, 1]), ALU.mult).then_inc(pair_step, 1)
                dve.wait_ge(pair_step, at + 1)
                nc.vector.scalar_tensor_tensor(kq[:, 0], kn[:], -1.0, over_channels(beta[:]), ALU.mult, ALU.mult)
                nc.vector.tensor_tensor(sq[:], kn[:], kq[:, 1], ALU.mult).then_inc(pair_step, 1)
                dve.wait_ge(pair_step, at + 2)
                nc.vector.tensor_reduce(kdotq[:], sq[:].rearrange("p d t -> p t d"), X, ALU.add).then_inc(pair_step, 1)
                dve.wait_ge(pair_step, at + 3)
                dve.wait_ge(proj_ready, g * PU + PU)
                dve.wait_ge(gate_stored, g * 32 + 32)
                nc.vector.memset(state[:], 0.0).then_inc(state_ready, 1)

            def read_state(g, t):
                at = (g * T + t) * 4
                dve.wait_ge(state_ready, g * (T + 1) + t + 1)
                nc.vector.tensor_tensor(prod[:], state[:].rearrange("p (o j) i -> p o j i", o=1).broadcast_to([P, 2, DK, DK]),
                                        kq[:, :, :, ds(t, 1)].rearrange("p s i o -> p s o i").broadcast_to([P, 2, DK, DK]), ALU.mult
                                        ).then_inc(rec_step, 1)
                dve.wait_ge(rec_step, at + 1)
                nc.vector.tensor_reduce(read[:, ds(t, 1)].rearrange("p o s j -> p (o s) j"), prod[:], X, ALU.add).then_inc(rec_step, 1)

            def update_state(g, t):
                at = (g * T + t) * 4
                dve.wait_ge(rec_step, at + 2)
                nc.vector.tensor_tensor(upd[:, ds(t, 1)].rearrange("p o j -> p (o j)"), val[:, :, ds(t, 1)].rearrange("p j o -> p (j o)"),
                                        read[:, ds(t, 1), 0].rearrange("p o j -> p (o j)"), ALU.add).then_inc(rec_step, 1)
                dve.wait_ge(rec_step, at + 3)
                nc.vector.tensor_tensor(outer[:], upd[:, ds(t, 1)].rearrange("p o j -> p j o").broadcast_to([P, DK, DK]),
                                        kn[:, :, ds(t, 1)].rearrange("p i o -> p o i").broadcast_to([P, DK, DK]), ALU.mult).then_inc(rec_step, 1)
                dve.wait_ge(rec_step, at + 4)
                flat = state[:].rearrange("p j i -> p (j i)")
                nc.vector.scalar_tensor_tensor(flat, flat, alpha[:, ds(t, 1)], outer[:].rearrange("p j i -> p (j i)"), ALU.mult, ALU.add
                                               ).then_inc(state_ready, 1)

            def output_parts(g):
                dve.wait_ge(state_ready, g * (T + 1) + T + 1)
                nc.vector.tensor_tensor(kq[:, 0], read[:, :, 1].rearrange("p t j -> p j t"), over_channels(alpha[:]), ALU.mult)
                nc.vector.tensor_tensor(kq[:, 1], upd[:].rearrange("p t j -> p j t"), over_channels(kdotq[:]), ALU.mult).then_inc(o_part, 1)

            def output_sum(g):
                dve.wait_ge(o_part, g + 1)
                nc.vector.tensor_tensor(val[:], kq[:, 0], kq[:, 1], ALU.add).then_inc(o_raw, 1)

            def output_norm(g):
                dve.wait_ge(o_squares, g + 1)
                nc.vector.tensor_reduce(norm[:, 0], kq[:, 0].rearrange("p d t -> p t d"), X, ALU.add).then_inc(o_norm, 1)
                nc.vector.tensor_tensor(val[:], val[:], rms_w[:].rearrange("p (j o) -> p j o", o=1).broadcast_to([P, DK, T]), ALU.mult
                                        ).then_inc(o_weighted, 1)

            def output_scale(g):
                dve.wait_ge(o_rnorm, g + 1)
                dve.wait_ge(o_weighted, g + 1)
                nc.vector.tensor_tensor(val[:], val[:], over_channels(rnorm[:, 0]), ALU.mult).then_inc(o_ready, 1)

            def gate_output(i):
                dve.wait_ge(seq_loaded, i * 48 + 48)
                nc.vector.scalar_tensor_tensor(gated[:], gate_seq[:], 1.0, o_seq[:], ALU.add, ALU.mult).then_inc(gated_ready, 1)

            def first_statistics(i):
                dve.wait_ge(dn_out, i + 1)
                nc.vector.tensor_tensor(sum1[:], score4[0:T, 3, 0:D], x_seq[:], ALU.add).then_inc(sum1_ready, 1)
                dve.wait_ge(sum1_ready, i + 1)
                nc.vector.bn_stats(stats1[:], sum1[:]).then_inc(stats1_ready, 1)
                dve.wait_ge(dve_const, 1)
                dve.wait_ge(stats1_ready, i + 1)
                nc.vector.bn_aggr(mv1[:], stats1[:]).then_inc(mv1_ready, 1)

            def first_norm(i):
                dve.wait_ge(rstd1_ready, i + 1)
                nc.vector.tensor_scalar(x1[:], sum1[:], mv1[:, 0:1], rstd1[:], ALU.subtract, ALU.mult).then_inc(x1_ready, 1)

            def attention(i, g, t, post):
                def copy_first(p):
                    dve.wait_ge(pT_ready, i * NP + p + 1)
                    if p >= 2:
                        dve.wait_ge(pv_ready, i * NP + p - 1)
                    nc.vector.tensor_copy(probsT[:, p % 2, 0].rearrange("p c t -> p (c t)"), PT0[0:SK, 0:SC * T]).then_inc(pT_copied_v, 1)

                def normalise(half):
                    n = XH // 2
                    dve.wait_ge(exp_ready, i * XH + n * (half + 1))
                    nc.vector.reciprocal(rrow[:, n * half:n * (half + 1)], rowsum[:, n * half:n * (half + 1)]).then_inc(rrow_ready, 1)
                    dve.wait_ge(rrow_ready, i * 2 + half + 1)
                    dve.wait_ge(pv_ready, i * NP + NP // 2 * (half + 1))
                    nc.vector.tensor_tensor(cx[:, 512 * half:512 * (half + 1)].rearrange("p (h d) -> p h d", d=XD),
                                            (OV, MX)[half][0:T, :].rearrange("p (h d) -> p h d", d=XD),
                                            rrow[:, n * half:n * (half + 1)].rearrange("p (h o) -> p h o", o=1).broadcast_to([T, n, XD]),
                                            ALU.mult).then_inc(cx_ready, 1)
                for p in range(NP):
                    dve.wait_ge(scores_ready, i * NP + p + 1)
                    nc.vector.tensor_reduce(negmax[:, 2 * p:2 * p + 2], score4[0:T, 2 * (p % 2):2 * (p % 2) + 2, 0:S], X, ALU.max,
                                            negate=True).then_inc(max_ready, 1)
                    if g is not None and p in STEPS_IN_PAIRS:
                        read_state(g, t + STEPS_IN_PAIRS.index(p))
                    if p >= 1:
                        copy_first(p - 1)
                    if g is not None and p in STEPS_IN_PAIRS:
                        update_state(g, t + STEPS_IN_PAIRS.index(p))
                    if post is not None and p == 0:
                        output_parts(post)
                    if post is not None and p == 1:
                        output_sum(post)
                    if post is not None and p == 4:
                        output_norm(post)
                    if p == NP // 2 + 2:
                        normalise(0)
                copy_first(NP - 1)
                normalise(1)
                if post is not None:
                    output_scale(post)

            def chain(i, fill, g, t, pre):
                def step(*ns):
                    if g is not None:
                        for n in ns:
                            read_state(g, t + len(STEPS_IN_PAIRS) + n)
                            update_state(g, t + len(STEPS_IN_PAIRS) + n)

                def pre_convolution(m):
                    if pre is not None:
                        convolution(pre, m)
                        if m >= 1:
                            twice_silu(pre, m - 1)
                dve.wait_ge(cxT_ready, i * 2 + 2)
                nc.vector.tensor_copy(cxT[:, 4:8].rearrange("p m t -> p (m t)"), PT1[:, 0:4 * T]).then_inc(cxT_copied_v, 1)
                step(0)
                pre_convolution(0)
                dve.wait_ge(xo_ready, i + 1)
                dve.wait_ge(x1_ready, i + 1)
                nc.vector.tensor_tensor(sum2[:], OV[0:T, 0:D], x1[:], ALU.add).then_inc(sum2_ready, 1)
                dve.wait_ge(sum2_ready, i + 1)
                nc.vector.bn_stats(stats2[:], sum2[:]).then_inc(stats2_ready, 1)
                dve.wait_ge(dve_const, 1)
                dve.wait_ge(stats2_ready, i + 1)
                nc.vector.bn_aggr(mv2[:], stats2[:]).then_inc(mv2_ready, 1)
                step(1)
                pre_convolution(1)
                dve.wait_ge(rstd2_ready, i + 1)
                nc.vector.tensor_scalar(x2[:], sum2[:], mv2[:, 0:1], rstd2[:], ALU.subtract, ALU.mult).then_inc(x2_ready, 1)
                step(2)
                dve.wait_ge(rms2_ready, i + 1)
                nc.vector.tensor_scalar(xn[:], x2[:], rms2[:], None, ALU.mult).then_inc(xn_ready, 1)
                step(3)
                pre_convolution(2)
                if fill:
                    gate_output(i + 1)
                dve.wait_ge(fkv_ready, i + 1)
                nc.vector.tensor_copy(fk[:], PT1[:, 0:T])
                nc.vector.tensor_copy(fv[:], PT1[0:T, T:T + KV * FD]).then_inc(fkv_copied, 1)
                step(4)

                def masked_max(j):
                    dve.wait_ge(fs_ready, i * KV + j + 1)
                    if j >= 2:
                        dve.wait_ge(fexp_ready, i * KV + j - 1)
                    nc.vector.tensor_tensor(fs[:, j % 2], (MX, OV)[j % 2][0:T, 0:REP * T].rearrange("p (m t) -> p m t", t=T),
                                            causal[:].rearrange("p (o t) -> p o t", o=1).broadcast_to([T, REP, T]), ALU.add).then_inc(fs_masked, 1)
                    dve.wait_ge(fs_masked, i * KV + j + 1)
                    nc.vector.tensor_reduce(fmax[:, j], fs[:, j % 2], X, ALU.max, negate=True).then_inc(fmax_ready, 1)

                def copy_transposes(j):
                    dve.wait_ge(fpT_ready, i * KV + j + 1)
                    if j >= 2:
                        dve.wait_ge(fpv_ready, i * KV + j - 1)
                    nc.vector.tensor_copy(fpT[:, j % 2].rearrange("p m t -> p (m t)"), (PT0, PT1)[j % 2][0:T, 0:REP * T]).then_inc(fpT_copied, 1)
                masked_max(0)
                masked_max(1)
                pre_convolution(3)
                masked_max(2)
                copy_transposes(0)
                pre_convolution(4)
                masked_max(3)
                copy_transposes(1)
                pre_convolution(5)
                if fill:
                    first_statistics(i + 1)
                copy_transposes(2)
                if fill:
                    first_norm(i + 1)
                copy_transposes(3)
                if pre is not None:
                    twice_silu(pre, CT - 1)
                    alpha_beta(pre)
                dve.wait_ge(fexp_ready, i * KV + KV)
                nc.vector.reciprocal(frow[:], fsum[:].rearrange("p j m -> p (j m)")).then_inc(frow_ready, 1)
                dve.wait_ge(frow_ready, i + 1)
                dve.wait_ge(fpv_ready, i * KV + KV)
                nc.vector.tensor_tensor(fo[:].rearrange("p (h d) -> p h d", d=FD), MX[0:T, 0:D].rearrange("p (h d) -> p h d", d=FD),
                                        frow[:].rearrange("p (h o) -> p h o", o=1).broadcast_to([T, FH, FD]), ALU.mult).then_inc(fo_ready, 1)
                step(5)
                dve.wait_ge(fwo_ready, i + 1)
                nc.vector.tensor_tensor(h_sb[:], PT0[0:T, 0:D], x2[:], ALU.add).then_inc(h_ready, 1)
                step(6)
                if pre is not None:
                    gate_middle(pre)
                dve.wait_ge(rms3_ready, i + 1)
                nc.vector.tensor_scalar(hn[:], h_sb[:], rms3[:], None, ALU.mult).then_inc(hn_ready, 1)
                step(7)
                if pre is not None:
                    pair_norm(pre, 0)
                dve.wait_ge(gate_ready, i + 1)
                nc.vector.tensor_copy(logit[:], PT1[0:T, 0:E]).then_inc(logit_ready, 1)
                dve.wait_ge(logit_ready, i + 1)
                nc.vector.tensor_reduce(neglmax[:], logit[:], X, ALU.max, negate=True).then_inc(logit_max, 1)
                other = logit[:].rearrange("p (o f) -> p o f", o=1).broadcast_to([T, E, E])
                own = logit[:].rearrange("p (e o) -> p e o", o=1).broadcast_to([T, E, E])
                at = i * 5
                nc.vector.tensor_tensor(tied[:], other, own, ALU.is_equal).then_inc(ranks, 1)
                nc.vector.tensor_tensor(above[:], other, own, ALU.is_gt)
                dve.wait_ge(ranks, at + 1)
                nc.vector.tensor_tensor(tied[:], tied[:], before[:], ALU.mult).then_inc(ranks, 1)
                dve.wait_ge(ranks, at + 2)
                nc.vector.tensor_tensor(above[:], above[:], tied[:], ALU.add).then_inc(ranks, 1)
                dve.wait_ge(ranks, at + 3)
                nc.vector.tensor_reduce(rank[:], above[:], X, ALU.add).then_inc(ranks, 1)
                dve.wait_ge(ranks, at + 4)
                dve.wait_ge(elog_ready, i + 1)
                nc.vector.scalar_tensor_tensor(comb[:], rank[:], 2.0, elog[:], ALU.is_lt, ALU.mult).then_inc(ranks, 1)
                dve.wait_ge(ranks, at + 5)
                nc.vector.tensor_reduce(csum[:], comb[:], X, ALU.add).then_inc(comb_step, 1)
                dve.wait_ge(comb_step, i * 2 + 1)
                nc.vector.reciprocal(rcsum[:], csum[:]).then_inc(comb_step, 1)
                dve.wait_ge(comb_step, i * 2 + 2)
                nc.vector.tensor_scalar(comb[:], comb[:], rcsum[:], None, ALU.mult).then_inc(comb_ready, 1)
                dve.wait_ge(comb_ready, i + 1)
                dve.wait_ge(acc_start, i + 1)
                for e in range(E):
                    u = e // 2
                    if e % 2 == 0:
                        dve.wait_ge(expert_ready, i * EU + u + 1)
                    if e > 0:
                        dve.wait_ge(expert_step, i * E + e)
                    nc.vector.scalar_tensor_tensor(acc[:], (OV, PT0, MX, PT1)[u][0:T, D * (e % 2):D * (e % 2 + 1)], comb[:, e:e + 1], acc[:],
                                                   ALU.mult, ALU.add).then_inc(expert_step, 1)
                dve.wait_ge(expert_step, i * E + E)
                nc.vector.bn_stats(stats3[:], acc[:]).then_inc(stats3_ready, 1)
                dve.wait_ge(dve_const, 1)
                dve.wait_ge(stats3_ready, i + 1)
                nc.vector.bn_aggr(mv3[:], stats3[:]).then_inc(mv3_ready, 1)
                dve.wait_ge(rstd3_ready, i + 1)
                if not isinstance(i, int) or i > 0:
                    dve.wait_ge(y_stored, i * 16)
                nc.vector.tensor_scalar(y_out[:], acc[:], mv3[:, 0:1], rstd3[:], ALU.subtract, ALU.mult).then_inc(y_ready, 1)
                if pre is not None:
                    pair_norm(pre, 1)
                    pairs(pre)

            def sequence(i, fill=True, post=None, pre=None, g=None, t=None):
                attention(i, g, t, post)
                chain(i, fill, g, t, pre)

            def up_to_recurrence(g):
                for m in range(CT):
                    convolution(g, m)
                    if m >= 1:
                        twice_silu(g, m - 1)
                twice_silu(g, CT - 1)
                alpha_beta(g)
                gate_middle(g)
                if g == 0:
                    scale_weights()
                for n in range(2):
                    pair_norm(g, n)
                pairs(g)

            up_to_recurrence(0)
            with dve.Fori(0, T // 4) as quarter:
                for n in range(4):
                    read_state(0, quarter * 4 + n)
                    update_state(0, quarter * 4 + n)
            output_parts(0)
            output_sum(0)
            output_norm(0)
            output_scale(0)
            gate_output(0)
            first_statistics(0)
            first_norm(0)
            up_to_recurrence(1)
            if NG > 2:
                with dve.Fori(0, NG - 2) as g:
                    with dve.Fori(0, G - 1) as s:
                        sequence(g * G + s, g=g + 1, t=s * STEPS)
                    sequence(g * G + (G - 1), post=g + 1, pre=g + 2)
            with dve.Fori(0, G - 1) as s:
                sequence((NG - 2) * G + s, g=NG - 1, t=s * STEPS)
            sequence((NG - 1) * G - 1, post=NG - 1)
            with dve.Fori((NG - 1) * G, B - 1) as i:
                sequence(i)
            sequence(B - 1, fill=False)


_OUT = "out_0_dram"


def kernel(**inputs):
    import numpy as _np
    import concourse.bacc as _bacc
    from concourse import mybir as _mybir
    from concourse.bass_utils import run_bass_kernel_spmd as _run

    a = {k: _np.asarray(v) for k, v in inputs.items()}
    B, T, D = a["x"].shape
    E = a["L0_ffn_expert_w"].shape[0]
    layout = dict(
        x=a["x"], xT=a["x"].reshape(B * T, D).T, ctxT=a["ctx_1024"].transpose(0, 2, 1),
        dn_Wq=a["L0_attn_Wq"], dn_Wk=a["L0_attn_Wk"], dn_Wv=a["L0_attn_Wv"], dn_Wo=a["L0_attn_Wo"],
        dn_Wa=a["L0_attn_Wa"], dn_ba=a["L0_attn_ba"], dn_Wb=a["L0_attn_Wb"], dn_bb=a["L0_attn_bb"],
        dn_Wgd=a["L0_attn_Wgd"], dn_Wgu=a["L0_attn_Wgu"], dn_rms_w=a["L0_attn_rms_w"],
        dn_qcw=a["L0_attn_qcw"], dn_qcb=a["L0_attn_qcb"], dn_kcw=a["L0_attn_kcw"], dn_kcb=a["L0_attn_kcb"],
        dn_vcw=a["L0_attn_vcw"], dn_vcb=a["L0_attn_vcb"],
        xa_Wq=a["L0_xattn_Wq"], xa_Wk=a["L0_xattn_Wk"], xa_Wv=a["L0_xattn_Wv"], xa_Wo=a["L0_xattn_Wo"],
        ff_attn_norm_w=a["L0_ffn_attn_norm_w"], ff_ffn_norm_w=a["L0_ffn_ffn_norm_w"],
        ff_wqT=a["L0_ffn_wq"].T, ff_wkT=a["L0_ffn_wk"].T, ff_wvT=a["L0_ffn_wv"].T, ff_woT=a["L0_ffn_wo"].T,
        ff_gateT=a["L0_ffn_gate_w"].T, ff_expertT=a["L0_ffn_expert_w"].transpose(2, 0, 1).reshape(D, E * D))
    nc = _bacc.Bacc("TRN2", target_bir_lowering=False, num_devices=1)
    arrays, args = {}, {}
    for name, value in layout.items():
        value = _np.ascontiguousarray(value)
        arrays[f"in_{name}_dram"] = value
        args[name] = nc.dram_tensor(f"in_{name}_dram", value.shape, _mybir.dt.from_np(value.dtype), kind="ExternalInput").ap()
    args["out"] = nc.dram_tensor(_OUT, (B, T, D), _mybir.dt.float32, kind="ExternalOutput").ap()
    decoder_layer(nc, **args)
    r = _run(nc, [arrays], core_ids=[0])
    return r.results[0][_OUT]
```

```python
import concourse.bass as bass
from concourse import mybir
from contextlib import ExitStack


def decoder_layer(nc, x, xT, ctxT, dn_Wq, dn_Wk, dn_Wv, dn_Wo, dn_Wa, dn_ba, dn_Wb, dn_bb, dn_Wgd, dn_Wgu, dn_rms_w,
                  dn_qcw, dn_qcb, dn_kcw, dn_kcb, dn_vcw, dn_vcb, xa_Wq, xa_Wk, xa_Wv, xa_Wo,
                  ff_attn_norm_w, ff_ffn_norm_w, ff_wqT, ff_wkT, ff_wvT, ff_woT, ff_gateT, ff_expertT, out):
    ds = bass.ds
    fp32 = mybir.dt.float32
    int32 = mybir.dt.int32
    ALU = mybir.AluOpType
    ACT = mybir.ActivationFunctionType
    X = mybir.AxisListType.X

    B, T, D = x.shape
    P = 128
    KC = D // P
    LN_EPS, RMS_EPS, NORM_FLOOR = 1e-5, 1e-6, 1e-6

    H, DK = 16, 16
    G = P // H
    NG = B // G
    GT = G * T
    HG = GT // 2
    CH = H * DK
    KS = 4
    PAD = KS - 1
    CT = 3 * CH // P
    AB, GD = 2 * CT, 2 * CT + 2
    GU = GD + 2
    PU = GU + 2 * KC
    STEPS = T // (G - 1)
    PAIR_STEPS = (0, 0, 1, 1, 1, 1, 0, 2)
    CHAIN_STEPS = (2, 0, 2, 2, 0, 1, 1, 1, 1, 0)
    assert sum(PAIR_STEPS) + sum(CHAIN_STEPS) == STEPS and STEPS * (G - 1) == T

    S = ctxT.shape[2]
    XH, XD = 16, 64
    XC = XH * XD
    NP = XH // 2
    SC = 3
    SK = S // SC
    VH = XC // 512
    KV_UNITS = [("k", m) for m in range(3)] + [("v", n) for n in range(4)] + [("k", m) for m in range(3, 6)] + [
        ("v", 4), ("k", 6), ("v", 5), ("k", 7)]
    FX = len(KV_UNITS)
    FQ = FX + 1
    FU = FQ + 2

    FH, FD, KV = 16, 16, 4
    REP = FH // KV
    E = ff_gateT.shape[1]
    EU = E * D // 512
    MASKED = -1e30
    ROOT_STEPS = 2 + 3 * 3

    ctx = ExitStack()
    with ctx:
        def sb(name, shape, dt=fp32):
            return ctx.enter_context(nc.sbuf_tensor(name, shape, dt))

        def sem(name):
            return ctx.enter_context(nc.semaphore(name))

        def dram(name, shape):
            return nc.dram_tensor(name, shape, fp32, kind="Internal").ap()

        qkv_dram = dram("qkv_dram", (3, B, CH, T))
        ab_dram = dram("ab_dram", (2, B, H, T))
        gate_dram = dram("gate_dram", (B, CH, T))
        o_dram = dram("o_dram", (B, CH, T))

        ident = sb("ident", [P, P])
        causal = sb("causal", [T, T])
        before = sb("before", [T, E, E])
        minus_half, ln_eps, rms_eps = sb("minus_half", [P, 1]), sb("ln_eps", [P, 1]), sb("rms_eps", [P, 1])
        w_qkv = sb("w_qkv", [P, KC, 3 * CH])
        w_ab = sb("w_ab", [P, KC, 2 * H])
        w_gd = sb("w_gd", [P, KC, CH // 2])
        w_gu = sb("w_gu", [P, 1, CH])
        w_dno = sb("w_dno", [P, KC, D])
        taps = sb("taps", [P, CT, KS])
        conv_bias = sb("conv_bias", [P, CT])
        ab_bias = sb("ab_bias", [2 * H, 1])
        ab_low = sb("ab_low", [2 * H, 1])
        rms_w = sb("rms_w", [P, DK])
        w_xq = sb("w_xq", [P, KC, XC])
        w_xk = sb("w_xk", [P, KC, XC])
        w_xv = sb("w_xv", [P, KC, XC])
        w_xo = sb("w_xo", [P, XC // P, D])
        attn_w = sb("attn_w", [P, KC])
        ffn_w = sb("ffn_w", [P, KC])
        w_fq = sb("w_fq", [P, KC, REP, P])
        w_fk = sb("w_fk", [P, KC, P])
        w_fv = sb("w_fv", [P, KC, KV * FD])
        w_fo = sb("w_fo", [P, KC, D])
        w_gate = sb("w_gate", [P, KC, E])
        w_exp = sb("w_exp", [P, KC, E * D])

        xT_in = sb("xT_in", [P, KC, GT])
        raw = sb("raw", [P, 2, G, T + PAD])
        work = sb("work", [P, 4, GT])
        conv = work[:, 0:2]
        tanh_half = work[:, 2:4]
        gate_mid = work[:, 3:4]
        act2 = sb("act2", [P, 2, GT])
        gate_t = act2
        kq = sb("kq", [P, 2, DK, T])
        kn = sb("kn", [P, DK, T])
        val = sb("val", [P, DK, T])
        ab = val[:].rearrange("p d t -> p (d t)")[0:2 * H, 0:GT]
        alpha = sb("alpha", [P, T])
        beta = sb("beta", [P, T])
        sq = sb("sq", [P, DK, T])
        norm = sb("norm", [P, 2, T])
        kdotq = beta
        state = sb("state", [P, DK, DK])
        prod = sb("prod", [P, 2, DK, DK])
        outer = sb("outer", [P, DK, DK])
        scratch = prod[:].rearrange("p s j i -> p (s j i)")
        rnorm = scratch[:, 0:2 * T].rearrange("p (s t) -> p s t", s=2)
        newton = scratch[:, 2 * T:4 * T].rearrange("p (s t) -> p s t", s=2)
        read = work[:].rearrange("p a n -> p (a n)").rearrange("p (t s j) -> p t s j", s=2, j=DK)
        upd = act2[:].rearrange("p a n -> p (a n)").rearrange("p (t j) -> p t j", j=DK)
        o_seq = sb("o_seq", [P, KC, T])
        gate_seq = sb("gate_seq", [P, KC, T])
        gated = o_seq
        x_seq = sb("x_seq", [T, D])
        sum1 = x_seq
        stats1 = sb("stats1", [T, 6])
        mv1 = sb("mv1", [T, 2])
        rstd1 = sb("rstd1", [T, 1])
        x1 = sb("x1", [T, D])

        xaT = sb("xaT", [P, KC, T])
        cT = sb("cT", [P, KC, S])
        qT = sb("qT", [P, NP, 2, T])
        kT = sb("kT", [P, NP, S])
        v_sb = sb("v_sb", [SK, SC, XC])
        cx = sb("cx", [T, XC])
        negmax = sb("negmax", [T, XH])
        rowsum = sb("rowsum", [T, XH])
        rrow = sb("rrow", [T, XH])
        probs_flat = sb("probs_flat", [P, 4 * S])
        probs = probs_flat[0:T].rearrange("p (a s) -> p a s", a=4)
        probsT = sb("probsT", [SK, 2, 2, SC, T])
        cxT = probs_flat[:, 0:XC // P * T].rearrange("p (m t) -> p m t", t=T)
        sum2 = sb("sum2", [T, D])
        stats2 = sb("stats2", [T, 6])
        mv2 = sb("mv2", [T, 2])
        rstd2 = sb("rstd2", [T, 1])
        x2 = sb("x2", [T, D])
        junk = sum2
        ms2 = sb("ms2", [T, 1])
        rms2 = sb("rms2", [T, 1])
        xn = sb("xn", [T, D])
        xnT = sb("xnT", [P, KC, T])
        fq = sb("fq", [P, REP, T])
        fk = sb("fk", [P, T])
        fv = sb("fv", [T, KV * FD])
        fs = probs_flat[0:T, 0:2 * REP * T].rearrange("p (a m t) -> p a m t", a=2, m=REP)
        fmax = sb("fmax", [T, KV, REP])
        fsum = sb("fsum", [T, KV, REP])
        frow = sb("frow", [T, KV * REP])
        fp = cx[:, 0:2 * REP * T].rearrange("p (a m t) -> p a m t", a=2, m=REP)
        fpT = probsT[0:T].rearrange("p a b c t -> p (a b c t)")[:, 0:2 * REP * T].rearrange("p (a m t) -> p a m t", a=2, m=REP)
        fo = sum2
        foT = xnT
        h_sb = sb("h_sb", [T, D])
        ms3 = sb("ms3", [T, 1])
        rms3 = sb("rms3", [T, 1])
        hn = xn
        hnT = xnT
        logit = sb("logit", [T, E])
        neglmax = sb("neglmax", [T, 1])
        above = sb("above", [T, E, E])
        tied = sb("tied", [T, E, E])
        rank = sb("rank", [T, E])
        elog = sb("elog", [T, E])
        comb = sb("comb", [T, E])
        csum = sb("csum", [T, 1])
        rcsum = sb("rcsum", [T, 1])
        acc = x2
        stats3 = sb("stats3", [T, 6])
        mv3 = sb("mv3", [T, 2])
        rstd3 = sb("rstd3", [T, 1])
        y_out = h_sb

        bank = [ctx.enter_context(nc.psum_tensor(f"bank{n}", [P, 512], fp32)) for n in range(4, 8)]
        score4 = ctx.enter_context(nc.psum_tensor("score4", [P, 4, 512], fp32))
        PT0, PT1, OV, MX = bank

        k_w_in = sem("k_w_in")
        dn_w_in, conv_w_in, xa_w_in, ff_w_in = sem("dn_w_in"), sem("conv_w_in"), sem("xa_w_in"), sem("ff_w_in")
        dve_const, pool_const, scaled_w = sem("dve_const"), sem("pool_const"), sem("scaled_w")
        pads_zero = sem("pads_zero")
        xT_loaded = sem("xT_loaded")
        proj_ready, proj_taken = sem("proj_ready"), sem("proj_taken")
        last_tap = sem("last_tap")
        tap_done, conv_ready, tanh_ready, act_ready = sem("tap_done"), sem("conv_ready"), sem("tanh_ready"), sem("act_ready")
        act_stored = [sem("act_stored0"), sem("act_stored1")]
        ab_half, ab_ready, ab_stored = sem("ab_half"), sem("ab_ready"), sem("ab_stored")
        gate_raw, gate_mid_ready, gate_stored = sem("gate_raw"), sem("gate_mid_ready"), sem("gate_stored")
        k_in, q_in, vab_in = sem("k_in"), sem("q_in"), sem("vab_in")
        squares, norm_ready, norm_floor, root_step, pair_step = (
            sem("squares"), sem("norm_ready"), sem("norm_floor"), sem("root_step"), sem("pair_step"))
        rec_step, state_ready = [sem("rec_step0"), sem("rec_step1")], [sem("state_ready0"), sem("state_ready1")]
        o_part, o_raw, o_squares, o_weighted, o_norm, o_floor, o_ready, o_stored = (
            sem("o_part"), sem("o_raw"), sem("o_squares"), sem("o_weighted"), sem("o_norm"), sem("o_floor"),
            sem("o_ready"), sem("o_stored"))
        seq_loaded, gated_ready, dn_out, sum1_ready, stats1_ready, mv1_ready, var1_ready, rstd1_ready, x1_ready = (
            sem("seq_loaded"), sem("gated_ready"), sem("dn_out"), sem("sum1_ready"), sem("stats1_ready"), sem("mv1_ready"),
            sem("var1_ready"), sem("rstd1_ready"), sem("x1_ready"))

        cT_loaded, fill_ready, fill_taken = sem("cT_loaded"), sem("fill_ready"), sem("fill_taken")
        scores_ready, max_ready, exp_ready = sem("scores_ready"), sem("max_ready"), sem("exp_ready")
        pT_ready, pT_copied, pv_ready = sem("pT_ready"), sem("pT_copied"), sem("pv_ready")
        rrow_ready, cx_ready, cxT_ready, cxT_copied = (
            sem("rrow_ready"), sem("cx_ready"), sem("cxT_ready"), sem("cxT_copied"))
        xo_ready, sum2_ready, stats2_ready, mv2_ready, var2_ready, rstd2_ready, x2_ready = (
            sem("xo_ready"), sem("sum2_ready"), sem("stats2_ready"), sem("mv2_ready"), sem("var2_ready"), sem("rstd2_ready"),
            sem("x2_ready"))
        ms2_ready, msv2_ready, rms2_ready, xn_ready, xnT_ready, xnT_copied = (
            sem("ms2_ready"), sem("msv2_ready"), sem("rms2_ready"), sem("xn_ready"), sem("xnT_ready"), sem("xnT_copied"))
        fq_ready, fkv_ready, fq_copied, fkv_copied = sem("fq_ready"), sem("fkv_ready"), sem("fq_copied"), sem("fkv_copied")
        fs_ready, fs_masked, fmax_ready, fexp_ready, fpT_ready, fpT_copied = (
            sem("fs_ready"), sem("fs_masked"), sem("fmax_ready"), sem("fexp_ready"), sem("fpT_ready"), sem("fpT_copied"))
        fpv_ready, frow_ready, fo_ready, foT_ready, foT_copied, fwo_ready, h_ready = (
            sem("fpv_ready"), sem("frow_ready"), sem("fo_ready"), sem("foT_ready"), sem("foT_copied"), sem("fwo_ready"),
            sem("h_ready"))
        ms3_ready, msv3_ready, rms3_ready, hn_ready, hnT_ready, hnT_copied = (
            sem("ms3_ready"), sem("msv3_ready"), sem("rms3_ready"), sem("hn_ready"), sem("hnT_ready"), sem("hnT_copied"))
        gate_ready, logit_ready, logit_max, ranks, elog_ready, comb_step, comb_ready, acc_start = (
            sem("gate_ready"), sem("logit_ready"), sem("logit_max"), sem("ranks"), sem("elog_ready"), sem("comb_step"),
            sem("comb_ready"), sem("acc_start"))
        expert_ready, expert_step, stats3_ready, mv3_ready, var3_ready, rstd3_ready, y_ready, y_stored = (
            sem("expert_ready"), [sem("expert_step0"), sem("expert_step1")], sem("stats3_ready"), sem("mv3_ready"), sem("var3_ready"),
            sem("rstd3_ready"), sem("y_ready"), sem("y_stored"))

        DN_W = 16 * 7
        CONV_W = 16 * (6 + 2 + G)
        XA_W = 16 * 4
        FF_W = 16 * (2 + 2 * KC * KV + 3 + 1)

        def chunks(w):
            return w.rearrange("(c p) n -> p c n", p=P)

        def column(w):
            return w.rearrange("(m p o) -> p m o", p=P, o=1)

        def over_channels(row):
            return row.rearrange("p (o t) -> p o t", o=1).broadcast_to([P, DK, T])

        block = ctx.enter_context(nc.Block())

        @block.sync
        def _(sp):
            def input_load(g):
                if not isinstance(g, int) or g > 0:
                    sp.wait_ge(proj_ready, g * PU)
                sp.dma_start(xT_in[:], chunks(xT)[:, :, ds(g * GT, GT)]).then_inc(xT_loaded, 16)

            def to_pairs(g):
                def load(n, dst, loaded):
                    for parity in range(2):
                        sp.wait_ge(act_stored[parity], g * 16 * (CT // 2) + 16 * (n + 1))
                    if n == 2:
                        sp.wait_ge(ab_stored, g * 32 + 32)
                    sp.dma_start(dst.rearrange("p d t -> p (d t)"),
                                 qkv_dram[n, ds(g * G, G)].rearrange("b (h d) t -> (b h) (d t)", d=DK)).then_inc(loaded, 16)
                for m in range(CT):
                    sp.wait_ge(act_ready, g * CT + m + 1)
                    sp.dma_start(qkv_dram[m // KC, ds(g * G, G), P * (m % KC):P * (m % KC + 1)].rearrange("b p t -> p b t"),
                                 act2[:, m % 2].rearrange("p (b t) -> p b t", b=G)).then_inc(act_stored[m % 2], 16)
                    if m == 2:
                        load(0, kn[:], k_in)
                    if m == 4:
                        load(1, kq[:, 1], q_in)
                sp.wait_ge(ab_ready, g + 1)
                for n in range(2):
                    sp.dma_start(ab_dram[n, ds(g * G, G)].rearrange("b h t -> h b t"),
                                 ab[H * n:H * (n + 1)].rearrange("p (b t) -> p b t", b=G)).then_inc(ab_stored, 16)
                load(2, val[:], vab_in)
                for n, dst in enumerate((alpha, beta)):
                    sp.dma_start(dst[:], ab_dram[n, ds(g * G, G)].rearrange("b h t -> (b h) t")).then_inc(vab_in, 16)

            def gate_store(g):
                for m in range(KC):
                    sp.wait_ge(proj_taken, g * PU + GU + 2 * (m + 1))
                    sp.dma_start(gate_dram[ds(g * G, G), P * m:P * (m + 1)].rearrange("b p t -> p b t"),
                                 gate_t[:, m].rearrange("p (b t) -> p b t", b=G)).then_inc(gate_stored, 16)

            def output_store(g):
                sp.wait_ge(o_ready, g + 1)
                sp.dma_start(o_dram[ds(g * G, G)].rearrange("b (h d) t -> (b h) (d t)", d=DK),
                             val[:].rearrange("p d t -> p (d t)")).then_inc(o_stored, 16)
                sp.wait_ge(o_stored, g * 16 + 16)
                sp.wait_ge(gate_stored, g * 32 + 32)

            def context_load(i):
                if not isinstance(i, int):
                    sp.wait_ge(fill_ready, i * FU + (FX - FU))
                sp.dma_start(cT[:], ctxT[ds(i, 1)].rearrange("o (c p) s -> p (o c) s", p=P)).then_inc(cT_loaded, 16)

            def sequence_load(i):
                if not isinstance(i, int) or i > 0:
                    sp.wait_ge(x1_ready, i)
                sp.dma_start(o_seq[:], o_dram[ds(i, 1)].rearrange("o (c p) t -> p (o c) t", p=P)).then_inc(seq_loaded, 16)
                sp.dma_start(gate_seq[:], gate_dram[ds(i, 1)].rearrange("o (c p) t -> p (o c) t", p=P)).then_inc(seq_loaded, 16)
                sp.dma_start(x_seq[:], x[ds(i, 1)].rearrange("o t d -> t (o d)")).then_inc(seq_loaded, 16)

            def store(i):
                sp.wait_ge(y_ready, i + 1)
                sp.dma_start(out[ds(i, 1)].rearrange("o t d -> t (o d)"), y_out[:]).then_inc(y_stored, 16)

            def sequence(i, fill=True, post=None, pre=None):
                if fill:
                    context_load(i + 1)
                if pre is not None:
                    input_load(pre)
                if post is not None:
                    output_store(post)
                if fill:
                    sequence_load(i + 1)
                if pre is not None:
                    to_pairs(pre)
                store(i)
                if pre is not None:
                    gate_store(pre)

            sp.dma_start(w_qkv[:, :, 0:CH], chunks(dn_Wk)).then_inc(k_w_in, 16)
            input_load(0)
            for n, w in enumerate((dn_Wq, dn_Wv)):
                sp.dma_start(w_qkv[:, :, CH * (n + 1):CH * (n + 2)], chunks(w)).then_inc(dn_w_in, 16)
            sp.dma_start(w_ab[:, :, 0:H], chunks(dn_Wa)).then_inc(dn_w_in, 16)
            sp.dma_start(w_ab[:, :, H:2 * H], chunks(dn_Wb)).then_inc(dn_w_in, 16)
            sp.dma_start(w_gd[:], chunks(dn_Wgd)).then_inc(dn_w_in, 16)
            sp.dma_start(w_gu[:], dn_Wgu.rearrange("(o p) n -> p o n", o=1)).then_inc(dn_w_in, 16)
            sp.dma_start(w_dno[:], chunks(dn_Wo)).then_inc(dn_w_in, 16)
            for dst, w in ((w_xq, xa_Wq), (w_xk, xa_Wk), (w_xv, xa_Wv), (w_xo, xa_Wo)):
                sp.dma_start(dst[:], chunks(w)).then_inc(xa_w_in, 16)
            sp.dma_start(attn_w[:].rearrange("p (m o) -> p m o", o=1), column(ff_attn_norm_w), allow_slow_non_contiguous=True).then_inc(ff_w_in, 16)
            sp.dma_start(ffn_w[:].rearrange("p (m o) -> p m o", o=1), column(ff_ffn_norm_w), allow_slow_non_contiguous=True).then_inc(ff_w_in, 16)
            sp.dma_start(w_fv[:], chunks(ff_wvT)).then_inc(ff_w_in, 16)
            sp.dma_start(w_fo[:], chunks(ff_woT)).then_inc(ff_w_in, 16)
            sp.dma_start(w_gate[:], chunks(ff_gateT)).then_inc(ff_w_in, 16)
            sp.dma_start(w_exp[:], chunks(ff_expertT)).then_inc(ff_w_in, 16)
            sp.wait_ge(pads_zero, 2)
            for j in range(KV):
                for k in range(KC):
                    sp.dma_start(w_fq[:, k, :, 32 * j:32 * j + FD],
                                  ff_wqT[P * k:P * (k + 1), REP * FD * j:REP * FD * (j + 1)].rearrange("p (m d) -> p m d", d=FD)
                                  ).then_inc(ff_w_in, 16)
                    sp.dma_start(w_fk[:, k, 32 * j:32 * j + FD], ff_wkT[P * k:P * (k + 1), FD * j:FD * (j + 1)]).then_inc(ff_w_in, 16)
            to_pairs(0)
            gate_store(0)
            context_load(0)
            input_load(1)
            output_store(0)
            sequence_load(0)
            to_pairs(1)
            gate_store(1)
            if NG > 2:
                with sp.Fori(0, NG - 2) as g:
                    with sp.Fori(0, G - 1) as s:
                        sequence(g * G + s)
                    sequence(g * G + (G - 1), post=g + 1, pre=g + 2)
            with sp.Fori(0, G - 1) as s:
                sequence((NG - 2) * G + s)
            sequence((NG - 1) * G - 1, post=NG - 1)
            with sp.Fori((NG - 1) * G, B - 1) as i:
                sequence(i)
            sequence(B - 1, fill=False)
            sp.wait_ge(y_stored, 16 * B + 16)

        @block.gpsimd
        def _(pool):
            nc.gpsimd.memset(ident[:], 0.0).then_inc(pool_const, 1)
            nc.gpsimd.memset(causal[:], 0.0).then_inc(pool_const, 1)
            nc.gpsimd.memset(before[:], 1.0).then_inc(pool_const, 1)
            nc.gpsimd.memset(minus_half[:], -0.5).then_inc(pool_const, 1)
            nc.gpsimd.memset(ln_eps[:], LN_EPS).then_inc(pool_const, 1)
            nc.gpsimd.memset(rms_eps[:], RMS_EPS).then_inc(pool_const, 1)
            pool.wait_ge(pool_const, 6)
            nc.gpsimd.affine_select(out=ident[:], in_=ident[:], compare_op=ALU.not_equal, fill=1.0, base=0,
                                    pattern=[[-1, P]], channel_multiplier=1).then_inc(pool_const, 1)
            nc.gpsimd.affine_select(out=causal[:], in_=causal[:], compare_op=ALU.is_ge, fill=MASKED, base=0,
                                    pattern=[[-1, T]], channel_multiplier=1).then_inc(pool_const, 1)
            nc.gpsimd.affine_select(out=before[:], in_=before[:], compare_op=ALU.is_gt, fill=0.0, base=0,
                                    pattern=[[1, E], [-1, E]], channel_multiplier=0).then_inc(pool_const, 1)
            pool.wait_ge(pool_const, 9)

            def first_norm(i):
                pool.wait_ge(mv1_ready, i + 1)
                nc.gpsimd.tensor_tensor(mv1[:, 1:2], mv1[:, 1:2], ln_eps[0:T], ALU.add).then_inc(var1_ready, 1)
                pool.wait_ge(var1_ready, i + 1)
                nc.gpsimd.tensor_tensor(rstd1[:], mv1[:, 1:2], minus_half[0:T], ALU.pow).then_inc(rstd1_ready, 1)

            def second_norms(i):
                pool.wait_ge(mv2_ready, i + 1)
                nc.gpsimd.tensor_tensor(mv2[:, 1:2], mv2[:, 1:2], ln_eps[0:T], ALU.add).then_inc(var2_ready, 1)
                pool.wait_ge(var2_ready, i + 1)
                nc.gpsimd.tensor_tensor(rstd2[:], mv2[:, 1:2], minus_half[0:T], ALU.pow).then_inc(rstd2_ready, 1)
                pool.wait_ge(ms2_ready, i + 1)
                nc.gpsimd.tensor_tensor(ms2[:], ms2[:], rms_eps[0:T], ALU.add).then_inc(msv2_ready, 1)
                pool.wait_ge(msv2_ready, i + 1)
                nc.gpsimd.tensor_tensor(rms2[:], ms2[:], minus_half[0:T], ALU.pow).then_inc(rms2_ready, 1)

            def third_norms(i):
                pool.wait_ge(ms3_ready, i + 1)
                nc.gpsimd.tensor_tensor(ms3[:], ms3[:], rms_eps[0:T], ALU.add).then_inc(msv3_ready, 1)
                pool.wait_ge(msv3_ready, i + 1)
                nc.gpsimd.tensor_tensor(rms3[:], ms3[:], minus_half[0:T], ALU.pow).then_inc(rms3_ready, 1)
                pool.wait_ge(h_ready, i + 1)
                nc.gpsimd.tensor_tensor(acc[:], h_sb[:], x2[:], ALU.add).then_inc(acc_start, 1)
                pool.wait_ge(mv3_ready, i + 1)
                nc.gpsimd.tensor_tensor(mv3[:, 1:2], mv3[:, 1:2], ln_eps[0:T], ALU.add).then_inc(var3_ready, 1)
                pool.wait_ge(var3_ready, i + 1)
                nc.gpsimd.tensor_tensor(rstd3[:], mv3[:, 1:2], minus_half[0:T], ALU.pow).then_inc(rstd3_ready, 1)

            def sequence(i, fill=True, post=None, pre=None):
                second_norms(i)
                if fill:
                    first_norm(i + 1)
                third_norms(i)

            first_norm(0)
            if NG > 2:
                with pool.Fori(0, NG - 2) as g:
                    with pool.Fori(0, G - 1) as s:
                        sequence(g * G + s)
                    sequence(g * G + (G - 1), post=g + 1, pre=g + 2)
            with pool.Fori(0, G - 1) as s:
                sequence((NG - 2) * G + s)
            sequence((NG - 1) * G - 1, post=NG - 1)
            with pool.Fori((NG - 1) * G, B - 1) as i:
                sequence(i)
            sequence(B - 1, fill=False)

        @block.scalar
        def _(act):
            for n, (cw, cb) in enumerate(((dn_kcw, dn_kcb), (dn_qcw, dn_qcb), (dn_vcw, dn_vcb))):
                act.dma_start(taps[:, KC * n:KC * (n + 1)], cw.rearrange("(m p) k -> p m k", p=P)).then_inc(conv_w_in, 16)
                act.dma_start(conv_bias[:, KC * n:KC * (n + 1)].rearrange("p (m o) -> p m o", o=1), column(cb), allow_slow_non_contiguous=True).then_inc(conv_w_in, 16)
            act.dma_start(ab_bias[0:H], dn_ba.rearrange("(p o) -> p o", o=1)).then_inc(conv_w_in, 16)
            act.dma_start(ab_bias[H:2 * H], dn_bb.rearrange("(p o) -> p o", o=1)).then_inc(conv_w_in, 16)
            for b in range(G):
                act.dma_start(rms_w[H * b:H * (b + 1)], dn_rms_w).then_inc(conv_w_in, 16)
            act.wait_ge(dve_const, 1)

            def tanh_of(g, m):
                act.wait_ge(conv_ready, g * CT + m + 1)
                if m >= 2:
                    act.wait_ge(act_ready, g * CT + m - 1)
                nc.scalar.activation(tanh_half[:, m % 2], conv[:, m % 2], ACT.Tanh, scale=0.5).then_inc(tanh_ready, 1)

            def projection(g, u, two_banks=False):
                src = OV if two_banks and u % 2 else score4[:, 3]
                act.wait_ge(proj_ready, g * PU + u + 1)
                if u < 2 * CT:
                    m, h = divmod(u, 2)
                    if m >= 2 and h == 0:
                        act.wait_ge(conv_ready, g * CT + m - 1)
                    nc.scalar.activation(raw[:, m % 2, G // 2 * h:G // 2 * (h + 1), PAD:],
                                         src[:, 0:HG].rearrange("p (b t) -> p b t", t=T), ACT.Copy).then_inc(proj_taken, 1)
                    if h == 1:
                        if m >= 2:
                            act.wait_ge(act_ready, g * CT + m - 1)
                        elif m == 0 and (not isinstance(g, int) or g > 0):
                            act.wait_ge(o_part, g)
                        act.wait_ge(proj_taken, g * PU + u + 1)
                        nc.scalar.activation(conv[:, m % 2].rearrange("p (b t) -> p b t", t=T), raw[:, m % 2, :, PAD:], ACT.Identity,
                                             scale=taps[:, m, PAD:KS], bias=conv_bias[:, m:m + 1]).then_inc(last_tap, 1)
                        if m >= 1:
                            tanh_of(g, m - 1)
                elif u < GD:
                    h = u - 2 * CT
                    if not isinstance(g, int) or g > 0:
                        act.wait_ge(o_stored, g * 16)
                    nc.scalar.activation(ab[:, HG * h:HG * (h + 1)], src[0:2 * H, 0:HG], ACT.Tanh, scale=0.5,
                                         bias=ab_bias[:]).then_inc(proj_taken, 1)
                    if h == 0:
                        tanh_of(g, CT - 1)
                elif u < GU:
                    h = u - GD
                    if h == 0:
                        act.wait_ge(act_ready, g * CT + CT)
                    nc.scalar.activation(conv[:, 0, HG * h:HG * (h + 1)], src[:, 0:HG], ACT.Copy).then_inc(proj_taken, 1)
                    if h == 1:
                        act.wait_ge(proj_taken, g * PU + GU)
                        nc.scalar.activation(tanh_half[:, 0], conv[:, 0], ACT.Tanh, scale=0.5).then_inc(gate_raw, 1)
                else:
                    m, h = divmod(u - GU, 2)
                    act.wait_ge(act_stored[m], (g + 1) * 16 * (CT // 2))
                    nc.scalar.activation(gate_t[:, m, HG * h:HG * (h + 1)], src[:, 0:HG], ACT.Tanh,
                                         scale=0.25).then_inc(proj_taken, 1)

            def pair_squares(g, n):
                act.wait_ge((k_in, q_in)[n], g * 16 + 16)
                if n == 1:
                    act.wait_ge(norm_ready, g * 2 + 1)
                nc.scalar.activation(sq[:], (kn[:], kq[:, 1])[n], ACT.Square).then_inc(squares, 1)

            def output_squares(g):
                act.wait_ge(o_raw, g + 1)
                nc.scalar.activation(kq[:, 0], val[:], ACT.Square, scale=DK ** -0.5).then_inc(o_squares, 1)

            def take(i, u):
                src = score4[:, u % 3]
                act.wait_ge(fill_ready, i * FU + u + 1)
                kind, n = KV_UNITS[u] if u < FX else ("x", 0)
                if kind == "k":
                    nc.scalar.activation(kT[:, n], src[:, 0:S], ACT.Copy).then_inc(fill_taken, 1)
                elif kind == "v":
                    c, h = divmod(n, VH)
                    nc.scalar.activation(v_sb[:, c, 512 * h:512 * (h + 1)], src[0:SK, :], ACT.Copy).then_inc(fill_taken, 1)
                elif u < FQ:
                    nc.scalar.activation(xaT[:].rearrange("p c t -> p (c t)"), src[:, 0:KC * T], ACT.Copy).then_inc(fill_taken, 1)
                else:
                    n = NP // 2 * (u - FQ)
                    for a in range(2):
                        r = slice(XD * a, XD * (a + 1))
                        last = nc.scalar.activation(qT[r, n:n + NP // 2, a], src[r, 0:NP // 2 * T].rearrange("p (m t) -> p m t", t=T),
                                                    ACT.Copy, scale=XD ** -0.5)
                    last.then_inc(fill_taken, 1)

            def attention(i, post=None):
                def copies(p):
                    act.wait_ge(pT_ready, i * NP + p + 1)
                    if p >= 2:
                        act.wait_ge(pv_ready, i * NP + p - 1)
                    for a in range(2):
                        nc.scalar.activation(probsT[:, p % 2, a].rearrange("p c t -> p (c t)"), (PT0, PT1)[a][0:SK, 0:SC * T], ACT.Copy
                                             ).then_inc(pT_copied, 1)
                for p in range(NP):
                    act.wait_ge(max_ready, i * NP + p + 1)
                    for a in range(2):
                        h = 2 * p + a
                        nc.scalar.activation(probs[:, 2 * (p % 2) + a], score4[0:T, 2 * (p % 2) + a, 0:S], ACT.Exp,
                                             bias=negmax[:, h:h + 1], accum_out=rowsum[:, h:h + 1]).then_inc(exp_ready, 1)
                    if p >= 1:
                        copies(p - 1)
                    if p == 5 and post is not None:
                        output_squares(post)
                copies(NP - 1)

            def chain(i, fill, pre=None):
                def take_next(*us):
                    if fill:
                        for u in us:
                            take(i + 1, u)
                            if pre is not None and u < GU:
                                projection(pre, u)
                take_next(0, 1)
                act.wait_ge(cxT_ready, i * 2 + 1)
                nc.scalar.activation(cxT[:, 0:4].rearrange("p m t -> p (m t)"), PT0[:, 0:4 * T], ACT.Copy).then_inc(cxT_copied, 1)
                act.wait_ge(cxT_ready, i * 2 + 2)
                nc.scalar.activation(cxT[:, 4:8].rearrange("p m t -> p (m t)"), PT1[:, 0:4 * T], ACT.Copy).then_inc(cxT_copied, 1)
                take_next(2, 3, 4, 5)
                act.wait_ge(x2_ready, i + 1)
                nc.scalar.activation(junk[:], x2[:], ACT.Square, scale=D ** -0.5, accum_out=ms2[:]).then_inc(ms2_ready, 1)
                take_next(6)
                act.wait_ge(xnT_ready, i + 1)
                nc.scalar.activation(xnT[:].rearrange("p c t -> p (c t)"), MX[:, 0:KC * T], ACT.Copy).then_inc(xnT_copied, 1)
                take_next(7)
                act.wait_ge(fq_ready, i + 1)
                nc.scalar.activation(fq[:].rearrange("p m t -> p (m t)"), PT0[:, 0:REP * T], ACT.Copy, scale=FD ** -0.5
                                     ).then_inc(fq_copied, 1)
                take_next(8)

                def copy_transposes(j):
                    act.wait_ge(fpT_ready, i * KV + j + 1)
                    if j >= 2:
                        act.wait_ge(fpv_ready, i * KV + j - 1)
                    nc.scalar.activation(fpT[:, j % 2].rearrange("p m t -> p (m t)"), (PT0, PT1)[j % 2][0:T, 0:REP * T], ACT.Copy
                                         ).then_inc(fpT_copied, 1)
                for j in range(KV):
                    act.wait_ge(fmax_ready, i * KV + j + 1)
                    if j >= 2:
                        act.wait_ge(fpT_ready, i * KV + j - 1)
                    for m in range(REP):
                        last = nc.scalar.activation(fp[:, j % 2, m], fs[:, j % 2, m], ACT.Exp, bias=fmax[:, j, m:m + 1],
                                                    accum_out=fsum[:, j, m:m + 1])
                    last.then_inc(fexp_ready, 1)
                    if j == 0:
                        take_next(9)
                    if j == 1:
                        take_next(10)
                        copy_transposes(0)
                    if j == 2:
                        take_next(11)
                        copy_transposes(1)
                copy_transposes(2)
                take_next(12)
                copy_transposes(3)
                take_next(13)
                if pre is not None:
                    pair_squares(pre, 0)
                act.wait_ge(foT_ready, i + 1)
                nc.scalar.activation(foT[:].rearrange("p c t -> p (c t)"), OV[:, 0:KC * T], ACT.Copy).then_inc(foT_copied, 1)
                take_next(14)
                if pre is not None:
                    pair_squares(pre, 1)
                act.wait_ge(h_ready, i + 1)
                nc.scalar.activation(junk[:], h_sb[:], ACT.Square, scale=D ** -0.5, accum_out=ms3[:]).then_inc(ms3_ready, 1)
                take_next(15, 16)
                act.wait_ge(hnT_ready, i + 1)
                nc.scalar.activation(hnT[:].rearrange("p c t -> p (c t)"), MX[:, 0:KC * T], ACT.Copy).then_inc(hnT_copied, 1)
                act.wait_ge(logit_max, i + 1)
                nc.scalar.activation(elog[:], logit[:], ACT.Exp, bias=neglmax[:]).then_inc(elog_ready, 1)
                if pre is not None:
                    for u in range(GU, PU):
                        projection(pre, u)

            def sequence(i, fill=True, post=None, pre=None):
                attention(i, post)
                chain(i, fill, pre)

            for u in range(PU):
                if u == AB:
                    pair_squares(0, 0)
                projection(0, u, two_banks=True)
            pair_squares(0, 1)
            for u in range(FX):
                take(0, u)
            output_squares(0)
            for u in range(AB):
                projection(1, u)
            pair_squares(1, 0)
            for u in range(FX, FU):
                take(0, u)
            for u in range(AB, GD):
                projection(1, u)
            pair_squares(1, 1)
            for u in range(GD, PU):
                projection(1, u)
            if NG > 2:
                with act.Fori(0, NG - 2) as g:
                    with act.Fori(0, G - 1) as s:
                        sequence(g * G + s)
                    sequence(g * G + (G - 1), post=g + 1, pre=g + 2)
            with act.Fori(0, G - 1) as s:
                sequence((NG - 2) * G + s)
            sequence((NG - 1) * G - 1, post=NG - 1)
            with act.Fori((NG - 1) * G, B - 1) as i:
                sequence(i)
            sequence(B - 1, fill=False)

        @block.tensor
        def _(pe):
            def projection(g, u, two_banks=False):
                if u == 0:
                    pe.wait_ge(xT_loaded, g * 16 + 16)
                if two_banks:
                    if u > 1:
                        pe.wait_ge(proj_taken, g * PU + u - 1)
                elif u > 0 or not isinstance(g, int) or g > 0:
                    pe.wait_ge(proj_taken, g * PU + u)
                dst = OV if two_banks and u % 2 else score4[:, 3]
                if u == GU:
                    pe.wait_ge(gate_mid_ready, g + 1)
                first, w, width, src = ((0, w_qkv, P, xT_in) if u < AB else (AB, w_ab, 2 * H, xT_in) if u < GD else
                                        (GD, w_gd, P, xT_in) if u < GU else (GU, w_gu, P, gate_mid))
                m, h = divmod(u - first, 2)
                nk = w.shape[1]
                for k in range(nk):
                    last = nc.tensor.matmul(dst[0:width, 0:HG], w[:, k, width * m:width * (m + 1)], src[:, k, HG * h:HG * (h + 1)],
                                            start=k == 0, stop=k == nk - 1)
                last.then_inc(proj_ready, 1)

            def output_rows(i):
                pe.wait_ge(gated_ready, i + 1)
                for k in range(KC):
                    last = nc.tensor.matmul(score4[0:T, 3, 0:D], gated[:, k], w_dno[:, k], start=k == 0, stop=k == KC - 1)
                last.then_inc(dn_out, 1)

            def fill(i, u):
                dst = score4[:, u % 3]
                if u >= 3:
                    pe.wait_ge(fill_taken, i * FU + u - 2)
                kind, n = KV_UNITS[u] if u < FX else ("x", 0)
                if kind == "k":
                    if u == 0:
                        pe.wait_ge(cT_loaded, i * 16 + 16)
                    for k in range(KC):
                        last = nc.tensor.matmul(dst[:, 0:S], w_xk[:, k, P * n:P * (n + 1)], cT[:, k], start=k == 0, stop=k == KC - 1)
                elif kind == "v":
                    c, h = divmod(n, VH)
                    for k in range(KC):
                        last = nc.tensor.matmul(dst[0:SK, :], cT[:, k, SK * c:SK * (c + 1)], w_xv[:, k, 512 * h:512 * (h + 1)], start=k == 0, stop=k == KC - 1)
                elif u < FQ:
                    pe.wait_ge(x1_ready, i + 1)
                    for k in range(KC):
                        last = nc.tensor.transpose(dst[:, T * k:T * (k + 1)], x1[:, P * k:P * (k + 1)], ident[0:T, 0:T])
                else:
                    pe.wait_ge(fill_taken, i * FU + FQ)
                    for n in range(NP // 2):
                        m = NP // 2 * (u - FQ) + n
                        for k in range(KC):
                            last = nc.tensor.matmul(dst[:, T * n:T * (n + 1)], w_xq[:, k, P * m:P * (m + 1)], xaT[:, k], start=k == 0, stop=k == KC - 1)
                last.then_inc(fill_ready, 1)

            def scores(i, p):
                if p == 0:
                    pe.wait_ge(fill_taken, i * FU + FU)
                if p >= 2:
                    pe.wait_ge(exp_ready, i * XH + 2 * p - 2)
                for a in range(2):
                    last = nc.tensor.matmul(score4[0:T, 2 * (p % 2) + a, 0:S], qT[:, p, a], kT[:, p], start=True, stop=True)
                last.then_inc(scores_ready, 1)

            def attention(i, with_fill):
                def transposes(p):
                    pe.wait_ge(exp_ready, i * XH + 2 * p + 2)
                    if p >= 1:
                        pe.wait_ge(pT_copied, i * XH + 2 * p)
                    for a in range(2):
                        for c in range(SC):
                            last = nc.tensor.transpose((PT0, PT1)[a][0:SK, T * c:T * (c + 1)], probs[:, 2 * (p % 2) + a, SK * c:SK * (c + 1)],
                                                       ident[0:T, 0:T])
                    last.then_inc(pT_ready, 1)

                def values(p):
                    pe.wait_ge(pT_copied, i * XH + 2 * p + 2)
                    dst = OV if p < NP // 2 else MX
                    for a in range(2):
                        h = 2 * p + a
                        col = XD * (h % (XH // 2))
                        for c in range(SC):
                            last = nc.tensor.matmul(dst[0:T, col:col + XD], probsT[:, p % 2, a, c], v_sb[:, c, XD * h:XD * (h + 1)],
                                                    start=c == 0, stop=c == SC - 1)
                    last.then_inc(pv_ready, 1)

                scores(i, 1)
                for p in range(NP):
                    if p < 2:
                        pe.wait_ge(expert_step[p], i * (E // 2) + 1)
                    if p == NP - 1 and with_fill:
                        fill(i + 1, 0)
                    transposes(p)
                    if p >= 1:
                        values(p - 1)
                    if p + 2 < NP:
                        scores(i, p + 2)
                if with_fill:
                    fill(i + 1, 1)
                values(NP - 1)

            def chain(i, with_fill, pre):
                def fill_next(*us):
                    if with_fill:
                        for u in us:
                            fill(i + 1, u)
                            if pre is not None and u < GU:
                                if u == 12:
                                    pe.wait_ge(sum1_ready, i + 2)
                                projection(pre, u)

                def gqa_scores(j):
                    if j >= 2:
                        pe.wait_ge(fs_masked, i * KV + j - 1)
                    r = slice(32 * j, 32 * j + FD)
                    for m in range(REP):
                        last = nc.tensor.matmul((MX, OV)[j % 2][0:T, T * m:T * (m + 1)], fq[r, m], fk[r], start=True, stop=True)
                    last.then_inc(fs_ready, 1)

                def gqa_transposes(j):
                    pe.wait_ge(fexp_ready, i * KV + j + 1)
                    if j >= 2:
                        pe.wait_ge(fpT_copied, i * KV + j - 1)
                    for m in range(REP):
                        last = nc.tensor.transpose((PT0, PT1)[j % 2][0:T, T * m:T * (m + 1)], fp[:, j % 2, m], ident[0:T, 0:T])
                    last.then_inc(fpT_ready, 1)

                def gqa_values(j):
                    pe.wait_ge(fpT_copied, i * KV + j + 1)
                    for m in range(REP):
                        h = REP * j + m
                        last = nc.tensor.matmul(MX[0:T, FD * h:FD * (h + 1)], fpT[:, j % 2, m], fv[:, FD * j:FD * (j + 1)], start=True, stop=True)
                    last.then_inc(fpv_ready, 1)

                if pre is not None:
                    projection(pre, 0)
                    projection(pre, 1)
                for half in range(2):
                    pe.wait_ge(cx_ready, i * 2 + half + 1)
                    for m in range(4):
                        c = 4 * half + m
                        last = nc.tensor.transpose((PT0, PT1)[half][:, T * m:T * (m + 1)], cx[:, P * c:P * (c + 1)], ident[0:T, 0:T])
                    last.then_inc(cxT_ready, 1)
                    if half == 1:
                        fill_next(2)
                for m in range(XC // P):
                    if m % 4 == 0:
                        pe.wait_ge(cxT_copied, i * 2 + m // 4 + 1)
                    last = nc.tensor.matmul(OV[0:T, 0:D], cxT[:, m], w_xo[:, m], start=m == 0, stop=m == XC // P - 1)
                last.then_inc(xo_ready, 1)
                fill_next(3, 4, 5, 6)
                pe.wait_ge(xn_ready, i + 1)
                for k in range(KC):
                    last = nc.tensor.transpose(MX[:, T * k:T * (k + 1)], xn[:, P * k:P * (k + 1)], ident[0:T, 0:T])
                last.then_inc(xnT_ready, 1)
                fill_next(7)
                pe.wait_ge(xnT_copied, i + 1)
                for m in range(REP):
                    for k in range(KC):
                        last = nc.tensor.matmul(PT0[:, T * m:T * (m + 1)], w_fq[:, k, m], xnT[:, k], start=k == 0, stop=k == KC - 1)
                last.then_inc(fq_ready, 1)
                for k in range(KC):
                    nc.tensor.matmul(PT1[:, 0:T], w_fk[:, k], xnT[:, k], start=k == 0, stop=k == KC - 1)
                for k in range(KC):
                    last = nc.tensor.matmul(PT1[0:T, T:T + KV * FD], xnT[:, k], w_fv[:, k], start=k == 0, stop=k == KC - 1)
                last.then_inc(fkv_ready, 1)
                fill_next(8)
                pe.wait_ge(fq_copied, i + 1)
                pe.wait_ge(fkv_copied, i + 1)
                gqa_scores(0)
                gqa_scores(1)
                fill_next(9)
                gqa_scores(2)
                gqa_transposes(0)
                gqa_scores(3)
                fill_next(10)
                gqa_transposes(1)
                fill_next(11)
                if with_fill:
                    if pre is not None:
                        pe.wait_ge(proj_taken, pre * PU + 12)
                    output_rows(i + 1)
                pe.wait_ge(fs_masked, i * KV + KV)
                gqa_values(0)
                gqa_transposes(2)
                fill_next(12)
                gqa_values(1)
                gqa_transposes(3)
                gqa_values(2)
                gqa_values(3)
                fill_next(13)
                pe.wait_ge(fo_ready, i + 1)
                for k in range(KC):
                    last = nc.tensor.transpose(OV[:, T * k:T * (k + 1)], fo[:, P * k:P * (k + 1)], ident[0:T, 0:T])
                last.then_inc(foT_ready, 1)
                fill_next(14)
                pe.wait_ge(foT_copied, i + 1)
                for k in range(KC):
                    last = nc.tensor.matmul(PT0[0:T, 0:D], foT[:, k], w_fo[:, k], start=k == 0, stop=k == KC - 1)
                last.then_inc(fwo_ready, 1)
                fill_next(15, 16)
                pe.wait_ge(hn_ready, i + 1)
                for k in range(KC):
                    last = nc.tensor.transpose(MX[:, T * k:T * (k + 1)], hn[:, P * k:P * (k + 1)], ident[0:T, 0:T])
                last.then_inc(hnT_ready, 1)
                pe.wait_ge(hnT_copied, i + 1)
                for k in range(KC):
                    last = nc.tensor.matmul(PT1[0:T, 0:E], hnT[:, k], w_gate[:, k], start=k == 0, stop=k == KC - 1)
                last.then_inc(gate_ready, 1)
                for u in range(EU):
                    if pre is not None:
                        projection(pre, GU + u)
                        if u == EU - 1:
                            pe.wait_ge(proj_taken, pre * PU + PU)
                    if u == 1:
                        pe.wait_ge(logit_ready, i + 1)
                    if u == EU - 1 and with_fill:
                        scores(i + 1, 0)
                    for k in range(KC):
                        last = nc.tensor.matmul((PT0, PT1, OV, MX)[u][0:T, :], hnT[:, k], w_exp[:, k, 512 * u:512 * (u + 1)], start=k == 0, stop=k == KC - 1)
                    last.then_inc(expert_ready, 1)

            pe.wait_ge(k_w_in, 16)
            pe.wait_ge(pool_const, 9)
            def sequence(i, fill=True, post=None, pre=None):
                attention(i, fill)
                chain(i, fill, pre)

            for u in range(PU):
                if u == 2 * KC:
                    pe.wait_ge(dn_w_in, DN_W)
                projection(0, u, two_banks=True)
            pe.wait_ge(proj_taken, PU)
            pe.wait_ge(xa_w_in, XA_W)
            pe.wait_ge(ff_w_in, FF_W)
            pe.wait_ge(scaled_w, 5)
            for u in range(FX):
                fill(0, u)
            for u in range(8):
                projection(1, u)
            pe.wait_ge(proj_taken, PU + 8)
            output_rows(0)
            pe.wait_ge(sum1_ready, 1)
            for u in range(8, AB):
                projection(1, u)
            for u in range(FX, FU):
                fill(0, u)
            for u in range(AB, PU):
                projection(1, u)
            pe.wait_ge(proj_taken, 2 * PU)
            scores(0, 0)
            if NG > 2:
                with pe.Fori(0, NG - 2) as g:
                    with pe.Fori(0, G - 1) as s:
                        sequence(g * G + s)
                    sequence(g * G + (G - 1), post=g + 1, pre=g + 2)
            with pe.Fori(0, G - 1) as s:
                sequence((NG - 2) * G + s)
            sequence((NG - 1) * G - 1, post=NG - 1)
            with pe.Fori((NG - 1) * G, B - 1) as i:
                sequence(i)
            sequence(B - 1, fill=False)

        @block.vector
        def _(dve):
            nc.vector.memset(w_fq[:], 0.0).then_inc(pads_zero, 1)
            nc.vector.memset(w_fk[:], 0.0).then_inc(pads_zero, 1)
            nc.vector.memset(norm[:], 0.0).then_inc(y_stored, 16)
            nc.vector.memset(upd[:], 0.0).then_inc(expert_step[0], 1)
            nc.vector.memset(qT[:], 0.0).then_inc(expert_step[1], 1)
            nc.vector.memset(raw[:], 0.0)
            nc.vector.memset(ab_low[:], 0.0).then_inc(pads_zero, 1)
            dve.wait_ge(conv_w_in, CONV_W)
            dve.wait_ge(pads_zero, 3)
            nc.vector.memset(ab_low[0:H], 0.1)
            nc.vector.tensor_scalar(rms_w[:], rms_w[:], 0.5, None, ALU.mult)
            nc.vector.tensor_scalar(ab_bias[:], ab_bias[:], 0.5, None, ALU.mult).then_inc(dve_const, 1)

            def scale_weights():
                dve.wait_ge(ff_w_in, FF_W)
                for w, norm_w in ((w_fq, attn_w), (w_fk, attn_w), (w_fv, attn_w), (w_gate, ffn_w), (w_exp, ffn_w)):
                    for k in range(KC):
                        last = nc.vector.tensor_scalar(w[:, k], w[:, k], norm_w[:, k:k + 1], None, ALU.mult)
                    last.then_inc(scaled_w, 1)

            def convolution(g, m):
                dve.wait_ge(last_tap, g * CT + m + 1)
                r = raw[:, m % 2]
                q = conv[:, m % 2].rearrange("p (b t) -> p b t", t=T)
                at = (g * CT + m) * (PAD - 1)
                for k in range(PAD - 1, 0, -1):
                    if k < PAD - 1:
                        dve.wait_ge(tap_done, at + PAD - 1 - k)
                    nc.vector.scalar_tensor_tensor(q, r[:, :, k:k + T], taps[:, m, k:k + 1], q, ALU.mult, ALU.add).then_inc(tap_done, 1)
                dve.wait_ge(tap_done, at + PAD - 1)
                nc.vector.scalar_tensor_tensor(q, r[:, :, 0:T], taps[:, m, 0:1], q, ALU.mult, ALU.add).then_inc(conv_ready, 1)

            def twice_silu(g, m):
                dve.wait_ge(tanh_ready, g * CT + m + 1)
                if m >= 2:
                    dve.wait_ge(act_stored[m % 2], g * 16 * (CT // 2) + 16 * (m // 2))
                nc.vector.scalar_tensor_tensor(act2[:, m % 2], tanh_half[:, m % 2], 1.0, conv[:, m % 2], ALU.add, ALU.mult
                                               ).then_inc(act_ready, 1)

            def alpha_beta(g):
                dve.wait_ge(proj_taken, g * PU + AB + 2)
                nc.vector.tensor_scalar(ab, ab, 0.5, 0.5, ALU.mult, ALU.add).then_inc(ab_half, 1)
                dve.wait_ge(ab_half, g + 1)
                nc.vector.tensor_scalar(ab, ab, ab_low[:], 1.0, ALU.max, ALU.min).then_inc(ab_ready, 1)

            def gate_middle(g):
                dve.wait_ge(gate_raw, g + 1)
                nc.vector.scalar_tensor_tensor(gate_mid[:, 0], tanh_half[:, 0], 1.0, conv[:, 0], ALU.add, ALU.mult).then_inc(gate_mid_ready, 1)

            def pair_norm(g, n):
                dve.wait_ge(squares, g * 2 + n + 1)
                nc.vector.tensor_reduce(norm[:, n], sq[:].rearrange("p d t -> p t d"), X, ALU.add).then_inc(norm_ready, 1)
                dve.wait_ge(norm_ready, g * 2 + n + 1)
                nc.vector.tensor_scalar(norm[:, n], norm[:, n], (2 * NORM_FLOOR) ** 2, None, ALU.max).then_inc(norm_floor, 1)

            def inverse_roots(which, done_before):
                x_, y_, t_ = norm[:, which], rnorm[:, which], newton[:, which]
                at = done_before * ROOT_STEPS
                nc.vector.tensor_scalar(t_.bitcast(int32), x_.bitcast(int32), 1, None, ALU.logical_shift_right).then_inc(root_step, 1)
                dve.wait_ge(root_step, at + 1)
                nc.vector.tensor_scalar(y_.bitcast(int32), t_.bitcast(int32), -1, 0x5F3759DF, ALU.mult, ALU.add).then_inc(root_step, 1)
                for n in range(3):
                    dve.wait_ge(root_step, at + 3 * n + 2)
                    nc.vector.tensor_tensor(t_, y_, y_, ALU.mult).then_inc(root_step, 1)
                    dve.wait_ge(root_step, at + 3 * n + 3)
                    nc.vector.scalar_tensor_tensor(t_, t_, -0.5, x_, ALU.mult, ALU.mult).then_inc(root_step, 1)
                    dve.wait_ge(root_step, at + 3 * n + 4)
                    nc.vector.scalar_tensor_tensor(y_, t_, 1.5, y_, ALU.add, ALU.mult).then_inc(root_step, 1)
                dve.wait_ge(root_step, at + ROOT_STEPS)

            def pairs(g):
                at = g * 4
                dve.wait_ge(norm_floor, g * 2 + 2)
                inverse_roots(slice(0, 2), 2 * g)
                nc.vector.tensor_tensor(kn[:], kn[:], over_channels(rnorm[:, 0]), ALU.mult)
                dve.wait_ge(vab_in, g * 48 + 48)
                nc.vector.scalar_tensor_tensor(val[:], val[:], 0.5, over_channels(beta[:]), ALU.mult, ALU.mult)
                nc.vector.tensor_tensor(kq[:, 1], kq[:, 1], over_channels(rnorm[:, 1]), ALU.mult).then_inc(pair_step, 1)
                dve.wait_ge(pair_step, at + 1)
                nc.vector.scalar_tensor_tensor(kq[:, 0], kn[:], -1.0, over_channels(beta[:]), ALU.mult, ALU.mult).then_inc(pair_step, 1)

            def state_start(g):
                dve.wait_ge(pair_step, g * 4 + 2)
                dve.wait_ge(proj_ready, g * PU + PU)
                dve.wait_ge(gate_stored, g * 32 + 32)
                for h in range(2):
                    nc.vector.memset(state[:, DK // 2 * h:DK // 2 * (h + 1)], 0.0).then_inc(state_ready[h], 1)

            HALVES = [slice(DK // 2 * h, DK // 2 * (h + 1)) for h in range(2)]
            NJ = DK // 2

            def state_products(g, t):
                for h, js in enumerate(HALVES):
                    dve.wait_ge(state_ready[h], g * (T + 1) + t + 1)
                    nc.vector.tensor_tensor(prod[:, :, js], state[:, js].rearrange("p (o j) i -> p o j i", o=1).broadcast_to([P, 2, NJ, DK]),
                                            kq[:, :, :, ds(t, 1)].rearrange("p s i o -> p s o i").broadcast_to([P, 2, NJ, DK]), ALU.mult
                                            ).then_inc(rec_step[h], 1)

            def state_reads(g, t):
                for h, js in enumerate(HALVES):
                    dve.wait_ge(rec_step[h], (g * T + t) * 4 + 1)
                    nc.vector.tensor_reduce(read[:, ds(t, 1), :, js].rearrange("p o s j -> p (o s) j"), prod[:, :, js], X, ALU.add
                                            ).then_inc(rec_step[h], 1)

            def update_row(g, t):
                for h, js in enumerate(HALVES):
                    dve.wait_ge(rec_step[h], (g * T + t) * 4 + 2)
                    nc.vector.tensor_tensor(upd[:, ds(t, 1), js].rearrange("p o j -> p (o j)"), val[:, js, ds(t, 1)].rearrange("p j o -> p (j o)"),
                                            read[:, ds(t, 1), 0, js].rearrange("p o j -> p (o j)"), ALU.add).then_inc(rec_step[h], 1)

            def outer_product(g, t):
                for h, js in enumerate(HALVES):
                    dve.wait_ge(rec_step[h], (g * T + t) * 4 + 3)
                    nc.vector.tensor_tensor(outer[:, js], upd[:, ds(t, 1), js].rearrange("p o j -> p j o").broadcast_to([P, NJ, DK]),
                                            kn[:, :, ds(t, 1)].rearrange("p i o -> p o i").broadcast_to([P, NJ, DK]), ALU.mult
                                            ).then_inc(rec_step[h], 1)

            def new_state(g, t):
                for h, js in enumerate(HALVES):
                    dve.wait_ge(rec_step[h], (g * T + t) * 4 + 4)
                    flat = state[:, js].rearrange("p j i -> p (j i)")
                    nc.vector.scalar_tensor_tensor(flat, flat, alpha[:, ds(t, 1)], outer[:, js].rearrange("p j i -> p (j i)"), ALU.mult, ALU.add
                                                   ).then_inc(state_ready[h], 1)

            def steps(g, first, count):
                for n in range(count):
                    for part in (state_products, state_reads, update_row, outer_product, new_state):
                        part(g, first + n)

            def key_query(g):
                nc.vector.tensor_tensor(sq[:], kn[:], kq[:, 1], ALU.mult).then_inc(pair_step, 1)

            def key_query_sum(g):
                dve.wait_ge(pair_step, g * 4 + 3)
                nc.vector.tensor_reduce(kdotq[:], sq[:].rearrange("p d t -> p t d"), X, ALU.add).then_inc(pair_step, 1)

            def output_read(g):
                for h in range(2):
                    dve.wait_ge(state_ready[h], g * (T + 1) + T + 1)
                nc.vector.tensor_tensor(kq[:, 0], read[:, :, 1].rearrange("p t j -> p j t"), over_channels(alpha[:]), ALU.mult)

            def output_update(g):
                dve.wait_ge(pair_step, g * 4 + 4)
                nc.vector.tensor_tensor(kq[:, 1], upd[:].rearrange("p t j -> p j t"), over_channels(kdotq[:]), ALU.mult).then_inc(o_part, 1)

            def output_sum(g):
                dve.wait_ge(o_part, g + 1)
                nc.vector.tensor_tensor(val[:], kq[:, 0], kq[:, 1], ALU.add).then_inc(o_raw, 1)

            def output_norm(g):
                dve.wait_ge(o_squares, g + 1)
                nc.vector.tensor_reduce(norm[:, 0], kq[:, 0].rearrange("p d t -> p t d"), X, ALU.add).then_inc(o_norm, 1)

            def output_weight(g):
                nc.vector.tensor_tensor(val[:], val[:], rms_w[:].rearrange("p (j o) -> p j o", o=1).broadcast_to([P, DK, T]), ALU.mult
                                        ).then_inc(o_weighted, 1)

            def output_roots(g):
                dve.wait_ge(o_norm, g + 1)
                nc.vector.tensor_scalar(norm[:, 0], norm[:, 0], RMS_EPS, None, ALU.add).then_inc(o_floor, 1)
                dve.wait_ge(o_floor, g + 1)
                inverse_roots(slice(0, 1), 2 * g + 1)

            def output_scale(g):
                nc.vector.tensor_tensor(val[:], val[:], over_channels(rnorm[:, 0]), ALU.mult).then_inc(o_ready, 1)

            def gate_output(i):
                dve.wait_ge(seq_loaded, i * 48 + 48)
                nc.vector.scalar_tensor_tensor(gated[:], gate_seq[:], 1.0, o_seq[:], ALU.add, ALU.mult).then_inc(gated_ready, 1)

            def first_statistics(i):
                dve.wait_ge(dn_out, i + 1)
                nc.vector.tensor_tensor(sum1[:], score4[0:T, 3, 0:D], x_seq[:], ALU.add).then_inc(sum1_ready, 1)
                dve.wait_ge(sum1_ready, i + 1)
                nc.vector.bn_stats(stats1[:], sum1[:]).then_inc(stats1_ready, 1)
                dve.wait_ge(dve_const, 1)
                dve.wait_ge(stats1_ready, i + 1)
                nc.vector.bn_aggr(mv1[:], stats1[:]).then_inc(mv1_ready, 1)

            def first_norm(i):
                dve.wait_ge(rstd1_ready, i + 1)
                nc.vector.tensor_scalar(x1[:], sum1[:], mv1[:, 0:1], rstd1[:], ALU.subtract, ALU.mult).then_inc(x1_ready, 1)

            def pair_maxima(i, p):
                dve.wait_ge(scores_ready, i * NP + p + 1)
                nc.vector.tensor_reduce(negmax[:, 2 * p:2 * p + 2], score4[0:T, 2 * (p % 2):2 * (p % 2) + 2, 0:S], X, ALU.max,
                                        negate=True).then_inc(max_ready, 1)

            def attention(i, g, t, post):
                def normalise(half):
                    n = XH // 2
                    dve.wait_ge(exp_ready, i * XH + n * (half + 1))
                    nc.vector.reciprocal(rrow[:, n * half:n * (half + 1)], rowsum[:, n * half:n * (half + 1)]).then_inc(rrow_ready, 1)
                    dve.wait_ge(rrow_ready, i * 2 + half + 1)
                    dve.wait_ge(pv_ready, i * NP + NP // 2 * (half + 1))
                    nc.vector.tensor_tensor(cx[:, 512 * half:512 * (half + 1)].rearrange("p (h d) -> p h d", d=XD),
                                            (OV, MX)[half][0:T, :].rearrange("p (h d) -> p h d", d=XD),
                                            rrow[:, n * half:n * (half + 1)].rearrange("p (h o) -> p h o", o=1).broadcast_to([T, n, XD]),
                                            ALU.mult).then_inc(cx_ready, 1)
                for p in range(NP):
                    if p >= 2:
                        pair_maxima(i, p)
                    if g is not None:
                        steps(g, t + sum(PAIR_STEPS[:p]), PAIR_STEPS[p])
                    if post is not None:
                        for part in ((key_query,), (), (key_query_sum,), (output_read,), (output_update,), (output_sum,), (),
                                     (output_norm, output_weight, output_roots))[p]:
                            part(post)
                    if p == NP // 2 + 2:
                        normalise(0)
                normalise(1)
                if post is not None:
                    output_scale(post)

            def chain(i, fill, g, t, pre):
                def point(n):
                    if g is not None:
                        steps(g, t + sum(PAIR_STEPS) + sum(CHAIN_STEPS[:n]), CHAIN_STEPS[n])

                def pre_convolution(m):
                    if pre is not None:
                        convolution(pre, m)
                        if m >= 1:
                            twice_silu(pre, m - 1)
                point(0)
                pre_convolution(0)
                dve.wait_ge(xo_ready, i + 1)
                dve.wait_ge(x1_ready, i + 1)
                nc.vector.tensor_tensor(sum2[:], OV[0:T, 0:D], x1[:], ALU.add).then_inc(sum2_ready, 1)
                dve.wait_ge(sum2_ready, i + 1)
                nc.vector.bn_stats(stats2[:], sum2[:]).then_inc(stats2_ready, 1)
                dve.wait_ge(dve_const, 1)
                dve.wait_ge(stats2_ready, i + 1)
                nc.vector.bn_aggr(mv2[:], stats2[:]).then_inc(mv2_ready, 1)
                point(1)
                pre_convolution(1)
                dve.wait_ge(rstd2_ready, i + 1)
                nc.vector.tensor_scalar(x2[:], sum2[:], mv2[:, 0:1], rstd2[:], ALU.subtract, ALU.mult).then_inc(x2_ready, 1)
                point(2)
                dve.wait_ge(rms2_ready, i + 1)
                nc.vector.tensor_scalar(xn[:], x2[:], rms2[:], None, ALU.mult).then_inc(xn_ready, 1)
                point(3)
                pre_convolution(2)
                if fill:
                    gate_output(i + 1)
                pre_convolution(3)
                dve.wait_ge(fkv_ready, i + 1)
                nc.vector.tensor_copy(fk[:], PT1[:, 0:T])
                nc.vector.tensor_copy(fv[:], PT1[0:T, T:T + KV * FD]).then_inc(fkv_copied, 1)
                point(4)

                def masked_max(j):
                    dve.wait_ge(fs_ready, i * KV + j + 1)
                    if j >= 2:
                        dve.wait_ge(fexp_ready, i * KV + j - 1)
                    nc.vector.tensor_tensor(fs[:, j % 2], (MX, OV)[j % 2][0:T, 0:REP * T].rearrange("p (m t) -> p m t", t=T),
                                            causal[:].rearrange("p (o t) -> p o t", o=1).broadcast_to([T, REP, T]), ALU.add).then_inc(fs_masked, 1)
                    dve.wait_ge(fs_masked, i * KV + j + 1)
                    nc.vector.tensor_reduce(fmax[:, j], fs[:, j % 2], X, ALU.max, negate=True).then_inc(fmax_ready, 1)

                masked_max(0)
                masked_max(1)
                point(5)
                pre_convolution(4)
                masked_max(2)
                masked_max(3)
                point(6)
                pre_convolution(5)
                if fill:
                    first_statistics(i + 1)
                if fill:
                    first_norm(i + 1)
                if pre is not None:
                    twice_silu(pre, CT - 1)
                dve.wait_ge(fexp_ready, i * KV + KV)
                nc.vector.reciprocal(frow[:], fsum[:].rearrange("p j m -> p (j m)")).then_inc(frow_ready, 1)
                dve.wait_ge(frow_ready, i + 1)
                dve.wait_ge(fpv_ready, i * KV + KV)
                nc.vector.tensor_tensor(fo[:].rearrange("p (h d) -> p h d", d=FD), MX[0:T, 0:D].rearrange("p (h d) -> p h d", d=FD),
                                        frow[:].rearrange("p (h o) -> p h o", o=1).broadcast_to([T, FH, FD]), ALU.mult).then_inc(fo_ready, 1)
                if pre is not None:
                    alpha_beta(pre)
                    pair_norm(pre, 0)
                point(7)
                dve.wait_ge(fwo_ready, i + 1)
                dve.wait_ge(y_stored, i * 16 + 16)
                nc.vector.tensor_tensor(h_sb[:], PT0[0:T, 0:D], x2[:], ALU.add).then_inc(h_ready, 1)
                point(8)
                if pre is not None:
                    gate_middle(pre)
                dve.wait_ge(rms3_ready, i + 1)
                nc.vector.tensor_scalar(hn[:], h_sb[:], rms3[:], None, ALU.mult).then_inc(hn_ready, 1)
                if pre is not None:
                    pair_norm(pre, 1)
                dve.wait_ge(gate_ready, i + 1)
                nc.vector.tensor_copy(logit[:], PT1[0:T, 0:E]).then_inc(logit_ready, 1)
                dve.wait_ge(logit_ready, i + 1)
                nc.vector.tensor_reduce(neglmax[:], logit[:], X, ALU.max, negate=True).then_inc(logit_max, 1)
                other = logit[:].rearrange("p (o f) -> p o f", o=1).broadcast_to([T, E, E])
                own = logit[:].rearrange("p (e o) -> p e o", o=1).broadcast_to([T, E, E])
                at = i * 5
                nc.vector.tensor_tensor(tied[:], other, own, ALU.is_equal).then_inc(ranks, 1)
                nc.vector.tensor_tensor(above[:], other, own, ALU.is_gt)
                dve.wait_ge(ranks, at + 1)
                nc.vector.tensor_tensor(tied[:], tied[:], before[:], ALU.mult).then_inc(ranks, 1)
                dve.wait_ge(ranks, at + 2)
                nc.vector.tensor_tensor(above[:], above[:], tied[:], ALU.add).then_inc(ranks, 1)
                dve.wait_ge(ranks, at + 3)
                nc.vector.tensor_reduce(rank[:], above[:], X, ALU.add).then_inc(ranks, 1)
                dve.wait_ge(ranks, at + 4)
                dve.wait_ge(elog_ready, i + 1)
                nc.vector.scalar_tensor_tensor(comb[:], rank[:], 2.0, elog[:], ALU.is_lt, ALU.mult).then_inc(ranks, 1)
                dve.wait_ge(ranks, at + 5)
                nc.vector.tensor_reduce(csum[:], comb[:], X, ALU.add).then_inc(comb_step, 1)
                dve.wait_ge(comb_step, i * 2 + 1)
                nc.vector.reciprocal(rcsum[:], csum[:]).then_inc(comb_step, 1)
                dve.wait_ge(comb_step, i * 2 + 2)
                nc.vector.tensor_scalar(comb[:], comb[:], rcsum[:], None, ALU.mult).then_inc(comb_ready, 1)
                dve.wait_ge(comb_ready, i + 1)
                dve.wait_ge(acc_start, i + 1)
                for e in range(E):
                    u = e // 2
                    if e % 2 == 0:
                        dve.wait_ge(expert_ready, i * EU + u + 1)
                    half, n = divmod(e, E // 2)
                    if e > 0:
                        dve.wait_ge(expert_step[(e - 1) // (E // 2)], i * (E // 2) + (e - 1) % (E // 2) + 2)
                    nc.vector.scalar_tensor_tensor(acc[:], (PT0, PT1, OV, MX)[u][0:T, D * (e % 2):D * (e % 2 + 1)], comb[:, e:e + 1], acc[:],
                                                   ALU.mult, ALU.add).then_inc(expert_step[half], 1)
                    if e == E - 3 and fill:
                        pair_maxima(i + 1, 0)
                dve.wait_ge(expert_step[1], (i + 1) * (E // 2) + 1)
                nc.vector.bn_stats(stats3[:], acc[:]).then_inc(stats3_ready, 1)
                if fill:
                    pair_maxima(i + 1, 1)
                dve.wait_ge(dve_const, 1)
                dve.wait_ge(stats3_ready, i + 1)
                nc.vector.bn_aggr(mv3[:], stats3[:]).then_inc(mv3_ready, 1)
                point(9)
                dve.wait_ge(rstd3_ready, i + 1)
                nc.vector.tensor_scalar(y_out[:], acc[:], mv3[:, 0:1], rstd3[:], ALU.subtract, ALU.mult).then_inc(y_ready, 1)
                if pre is not None:
                    pairs(pre)
                    state_start(pre)

            def sequence(i, fill=True, post=None, pre=None, g=None, t=None):
                attention(i, g, t, post)
                chain(i, fill, g, t, pre)

            for m in range(CT):
                convolution(0, m)
                if m >= 1:
                    twice_silu(0, m - 1)
            twice_silu(0, CT - 1)
            alpha_beta(0)
            gate_middle(0)
            pair_norm(0, 0)
            scale_weights()
            pair_norm(0, 1)
            pairs(0)
            state_start(0)
            with dve.Fori(0, T // 8) as eight:
                steps(0, eight * 8, 8)
            for part in (key_query, key_query_sum, output_read, output_update, output_sum, output_norm, output_weight, output_roots,
                         output_scale):
                part(0)
            for m in range(3):
                convolution(1, m)
                if m >= 1:
                    twice_silu(1, m - 1)
            gate_output(0)
            convolution(1, 3)
            twice_silu(1, 2)
            first_statistics(0)
            convolution(1, 4)
            twice_silu(1, 3)
            first_norm(0)
            pair_norm(1, 0)
            convolution(1, 5)
            twice_silu(1, 4)
            twice_silu(1, 5)
            alpha_beta(1)
            pair_norm(1, 1)
            gate_middle(1)
            pairs(1)
            pair_maxima(0, 0)
            pair_maxima(0, 1)
            state_start(1)
            if NG > 2:
                with dve.Fori(0, NG - 2) as g:
                    with dve.Fori(0, G - 1) as s:
                        sequence(g * G + s, g=g + 1, t=s * STEPS)
                    sequence(g * G + (G - 1), post=g + 1, pre=g + 2)
            with dve.Fori(0, G - 1) as s:
                sequence((NG - 2) * G + s, g=NG - 1, t=s * STEPS)
            sequence((NG - 1) * G - 1, post=NG - 1)
            with dve.Fori((NG - 1) * G, B - 1) as i:
                sequence(i)
            sequence(B - 1, fill=False)


_OUT = "out_0_dram"


def kernel(**inputs):
    import numpy as _np
    import concourse.bacc as _bacc
    from concourse import mybir as _mybir
    from concourse.bass_utils import run_bass_kernel_spmd as _run

    a = {k: _np.asarray(v) for k, v in inputs.items()}
    B, T, D = a["x"].shape
    E = a["L0_ffn_expert_w"].shape[0]
    layout = dict(
        x=a["x"], xT=a["x"].reshape(B * T, D).T, ctxT=a["ctx_1024"].transpose(0, 2, 1),
        dn_Wq=a["L0_attn_Wq"], dn_Wk=a["L0_attn_Wk"], dn_Wv=a["L0_attn_Wv"], dn_Wo=a["L0_attn_Wo"],
        dn_Wa=a["L0_attn_Wa"], dn_ba=a["L0_attn_ba"], dn_Wb=a["L0_attn_Wb"], dn_bb=a["L0_attn_bb"],
        dn_Wgd=a["L0_attn_Wgd"], dn_Wgu=a["L0_attn_Wgu"], dn_rms_w=a["L0_attn_rms_w"],
        dn_qcw=a["L0_attn_qcw"], dn_qcb=a["L0_attn_qcb"], dn_kcw=a["L0_attn_kcw"], dn_kcb=a["L0_attn_kcb"],
        dn_vcw=a["L0_attn_vcw"], dn_vcb=a["L0_attn_vcb"],
        xa_Wq=a["L0_xattn_Wq"], xa_Wk=a["L0_xattn_Wk"], xa_Wv=a["L0_xattn_Wv"], xa_Wo=a["L0_xattn_Wo"],
        ff_attn_norm_w=a["L0_ffn_attn_norm_w"], ff_ffn_norm_w=a["L0_ffn_ffn_norm_w"],
        ff_wqT=a["L0_ffn_wq"].T, ff_wkT=a["L0_ffn_wk"].T, ff_wvT=a["L0_ffn_wv"].T, ff_woT=a["L0_ffn_wo"].T,
        ff_gateT=a["L0_ffn_gate_w"].T, ff_expertT=a["L0_ffn_expert_w"].transpose(2, 0, 1).reshape(D, E * D))
    nc = _bacc.Bacc("TRN2", target_bir_lowering=False, num_devices=1)
    arrays, args = {}, {}
    for name, value in layout.items():
        value = _np.ascontiguousarray(value)
        arrays[f"in_{name}_dram"] = value
        args[name] = nc.dram_tensor(f"in_{name}_dram", value.shape, _mybir.dt.from_np(value.dtype), kind="ExternalInput").ap()
    args["out"] = nc.dram_tensor(_OUT, (B, T, D), _mybir.dt.float32, kind="ExternalOutput").ap()
    decoder_layer(nc, **args)
    r = _run(nc, [arrays], core_ids=[0])
    return r.results[0][_OUT]
```
